# Optimizing a Trainium2 kernel written in Bass

```python
import numpy as np
import jax
import jax.numpy as jnp

def _softmax(x, axis=-1):
    return jax.nn.softmax(x, axis=axis)

def _gelu(x):
    return jax.nn.gelu(x, approximate=True)

def _silu(x):
    return jax.nn.silu(x)

def _sigmoid(x):
    return jax.nn.sigmoid(x)

def _layernorm(x, axis=-1, eps=1e-05):
    m = jnp.mean(x, axis=axis, keepdims=True)
    v = jnp.var(x, axis=axis, keepdims=True)
    return (x - m) / jnp.sqrt(v + eps)

def _scatter_add(tgt, idx, src, axis=0):
    return tgt.at[idx].add(src)

def _segment_sum(src, seg, n):
    return jax.ops.segment_sum(src, seg, n)
kernel_name = 'mk_perceiver_d1_seqx_r4_590e2e'

def setup_inputs(seed: int=0):
    np.random.seed(seed)
    _w = jnp.asarray

    def _rec_inputs():
        import jax
        import jax.numpy as jnp
        _rk = jax.random.key(seed)
        x = 7.22e-05 + 1 * jax.random.normal(jax.random.fold_in(_rk, 1), (1, 256, 512), jnp.float32)
        _lenS = 256 - jax.random.randint(jax.random.fold_in(_rk, 7), (1,), 0, max(1, 256 // 4) + 1, jnp.int32)
        _lenS2 = 4096 - jax.random.randint(jax.random.fold_in(_rk, 8), (1,), 0, max(1, 4096 // 4) + 1, jnp.int32)
        _ctx_1024P = jax.random.normal(jax.random.fold_in(_rk, 11), (1, 16, 256), jnp.float32)
        _ctx_1024c = jax.random.dirichlet(jax.random.fold_in(_rk, 511), 0.3 * jnp.ones((16,), jnp.float32), (1, 4096))
        _ctx_1024t = jnp.einsum('bsk,bkd->bsd', _ctx_1024c, _ctx_1024P)
        _ctx_1024t = _ctx_1024t * jax.lax.rsqrt(jnp.mean(jnp.square(_ctx_1024t)) + 1e-12) * 0.953939
        ctx_1024 = -0.000673644 + 1.00013 * (_ctx_1024t + 0.3 * jax.random.normal(jax.random.fold_in(_rk, 611), (1, 4096, 256), jnp.float32))
        return (x, ctx_1024)
    x, ctx_1024 = _rec_inputs()

    def _L0_xattn_setup():
        import jax, jax.numpy as jnp
        import numpy as np
        B, S1, S2, DCA = (2, 512, 256, 16)
        QDIM, KDIM, H = (512, 256, 16)
        HD = QDIM // H
        SCALE = HD ** (-0.5)
        EPS = 1e-06
        DCA_WEIGHT = 1.0

        def _ln(t, w, b):
            m = jnp.mean(t, axis=-1, keepdims=True)
            v = jnp.var(t, axis=-1, keepdims=True)
            return (t - m) * jax.lax.rsqrt(v + EPS) * w + b

        def _attn(q, k, v):
            s = jnp.einsum('bhqd,bhkd->bhqk', q, k) * SCALE
            p = jax.nn.softmax(s, axis=-1)
            return jnp.einsum('bhqk,bhkd->bhqd', p, v)
        key = jax.random.key(seed)
        ks = jax.random.split(key, 8)
        w = lambda k, shape: jax.random.normal(k, shape, jnp.float32) * 0.02
        return {'x': jax.random.normal(ks[0], (B, S1, QDIM), jnp.float32), 'y': jax.random.normal(ks[1], (B, S2 + DCA, KDIM), jnp.float32), 'Wq': w(ks[2], (QDIM, QDIM)), 'bq': jnp.zeros((QDIM,), jnp.float32), 'Wk': w(ks[3], (KDIM, QDIM)), 'bk': jnp.zeros((QDIM,), jnp.float32), 'Wv': w(ks[4], (KDIM, QDIM)), 'bv': jnp.zeros((QDIM,), jnp.float32), 'Wkv_dca': w(ks[5], (KDIM, 2 * QDIM)), 'bkv_dca': jnp.zeros((2 * QDIM,), jnp.float32), 'qn_w': jnp.ones((HD,), jnp.float32), 'qn_b': jnp.zeros((HD,), jnp.float32), 'kn_w': jnp.ones((HD,), jnp.float32), 'kn_b': jnp.zeros((HD,), jnp.float32), 'kn_dca_w': jnp.ones((HD,), jnp.float32), 'kn_dca_b': jnp.zeros((HD,), jnp.float32), 'Wo': w(ks[6], (QDIM, QDIM)), 'bo': jnp.zeros((QDIM,), jnp.float32)}
    _L0_xattn_all = _L0_xattn_setup()
    _L0_xattn_in = {k: v for k, v in _L0_xattn_all.items() if k in ('Wq', 'bq', 'Wk', 'bk', 'Wv', 'bv', 'Wkv_dca', 'bkv_dca', 'qn_w', 'qn_b', 'kn_w', 'kn_b', 'kn_dca_w', 'kn_dca_b', 'Wo', 'bo')}
    del _L0_xattn_all

    def _L0_attn_setup():
        import jax, jax.numpy as jnp
        import numpy as np
        D_MODEL = 512
        EXPAND = 2
        D_INNER = EXPAND * D_MODEL
        D_STATE = 128
        NGROUPS = 1
        HEADDIM = 64
        NHEADS = D_INNER // HEADDIM
        D_CONV = 4
        CHUNK = 128
        D_XBC = D_INNER + 2 * NGROUPS * D_STATE
        D_IN_PROJ = 2 * D_INNER + 2 * NGROUPS * D_STATE + NHEADS
        EPS = 1e-05

        def _causal_conv1d(xBC, conv_w, conv_b):
            x = jnp.transpose(xBC, (0, 2, 1))
            x = jnp.pad(x, ((0, 0), (0, 0), (D_CONV - 1, 0)))
            y = jax.lax.conv_general_dilated(x, conv_w[:, None, :], window_strides=(1,), padding='VALID', feature_group_count=D_XBC, dimension_numbers=('NCH', 'OIH', 'NCH'))
            y = y + conv_b[None, :, None]
            return jnp.transpose(jax.nn.silu(y), (0, 2, 1))

        def _ssd(x, dt, A, B, C, D):
            b, L, h, p = x.shape
            n = B.shape[-1]
            c = L // CHUNK
            hpg = h // NGROUPS
            Bh = jnp.repeat(B, hpg, axis=2)
            Ch = jnp.repeat(C, hpg, axis=2)
            xr = x.reshape(b, c, CHUNK, h, p)
            dtr = dt.reshape(b, c, CHUNK, h)
            Br = Bh.reshape(b, c, CHUNK, h, n)
            Cr = Ch.reshape(b, c, CHUNK, h, n)
            xdt = xr * dtr[..., None]
            dA = jnp.transpose((dt * A[None, None, :]).reshape(b, c, CHUNK, h), (0, 3, 1, 2))
            A_cs = jnp.cumsum(dA, axis=-1)
            diff = A_cs[..., :, None] - A_cs[..., None, :]
            mask = jnp.tril(jnp.ones((CHUNK, CHUNK), dtype=bool))
            Lmat = jnp.where(mask, jnp.exp(jnp.where(mask, diff, 0.0)), 0.0)
            Y_diag = jnp.einsum('bclhn,bcshn,bhcls,bcshp->bclhp', Cr, Br, Lmat, xdt)
            decay_states = jnp.exp(A_cs[..., -1:] - A_cs)
            states = jnp.einsum('bclhn,bhcl,bclhp->bchpn', Br, decay_states, xdt)
            chunk_decay = jnp.exp(A_cs[..., -1])

            def step(carry, inp):
                s, d = inp
                return (carry * d[..., None, None] + s, carry)
            init = jnp.zeros((b, h, p, n), dtype=x.dtype)
            _, prev = jax.lax.scan(step, init, (jnp.transpose(states, (1, 0, 2, 3, 4)), jnp.transpose(chunk_decay, (2, 0, 1))))
            prev_states = jnp.transpose(prev, (1, 0, 2, 3, 4))
            Y_off = jnp.einsum('bclhn,bchpn,bhcl->bclhp', Cr, prev_states, jnp.exp(A_cs))
            Y = (Y_diag + Y_off).reshape(b, L, h, p) + x * D[None, None, :, None]
            return Y
        key = jax.random.key(seed)
        ks = jax.random.split(key, 9)
        u = jax.random.normal(ks[0], (2, 512, D_MODEL), dtype=jnp.float32)
        W_in = jax.random.normal(ks[1], (D_IN_PROJ, D_MODEL), dtype=jnp.float32) / np.sqrt(D_MODEL)
        conv_w = jax.random.normal(ks[2], (D_XBC, D_CONV), dtype=jnp.float32) / np.sqrt(D_CONV)
        conv_b = jax.random.normal(ks[3], (D_XBC,), dtype=jnp.float32) * 0.1
        dt_bias = jnp.log(jnp.expm1(jax.random.uniform(ks[4], (NHEADS,), minval=0.001, maxval=0.1)))
        A_log = jnp.log(jax.random.uniform(ks[5], (NHEADS,), minval=1.0, maxval=16.0))
        D = jnp.ones((NHEADS,), dtype=jnp.float32)
        norm_weight = jnp.ones((D_INNER,), dtype=jnp.float32)
        W_out = jax.random.normal(ks[8], (D_MODEL, D_INNER), dtype=jnp.float32) / np.sqrt(D_INNER)
        return {'u': u, 'W_in': W_in, 'conv_w': conv_w, 'conv_b': conv_b, 'dt_bias': dt_bias, 'A_log': A_log, 'D': D, 'norm_weight': norm_weight, 'W_out': W_out}
    _L0_attn_all = _L0_attn_setup()
    _L0_attn_in = {k: v for k, v in _L0_attn_all.items() if k in ('W_in', 'conv_w', 'conv_b', 'dt_bias', 'A_log', 'D', 'norm_weight', 'W_out')}
    del _L0_attn_all

    def _L0_ffn_setup():
        import jax, jax.numpy as jnp
        import numpy as np
        TOP_K = 8
        NEG_INF = -1000000000.0
        key = jax.random.key(seed)
        ks = jax.random.split(key, 6)
        B, S, H, I, E, G, GS = (1, 512, 512, 352, 64, 8, 8)
        sc = 0.02
        return {'hidden_states': jax.random.normal(ks[0], (B, S, H), jnp.float32), 'gate_w': jax.random.normal(ks[1], (E, H), jnp.float32) * sc, 'mask_up_w': jax.random.normal(ks[2], (G, H, GS), jnp.float32) * sc, 'gate_proj_w': jax.random.normal(ks[3], (G, I, H), jnp.float32) * sc, 'up_proj_w': jax.random.normal(ks[4], (G, I, H), jnp.float32) * sc, 'down_proj_w': jax.random.normal(ks[5], (G, H, I), jnp.float32) * sc, 'inv_map': jnp.arange(G * GS, dtype=jnp.int64).reshape(G, GS)}
    _L0_ffn_all = _L0_ffn_setup()
    _L0_ffn_in = {k: v for k, v in _L0_ffn_all.items() if k in ('gate_w', 'mask_up_w', 'gate_proj_w', 'up_proj_w', 'down_proj_w', 'inv_map')}
    del _L0_ffn_all
    return {'x': x, 'ctx_1024': ctx_1024, 'L0_xattn_Wq': _L0_xattn_in['Wq'], 'L0_xattn_bq': _L0_xattn_in['bq'], 'L0_xattn_Wk': _L0_xattn_in['Wk'], 'L0_xattn_bk': _L0_xattn_in['bk'], 'L0_xattn_Wv': _L0_xattn_in['Wv'], 'L0_xattn_bv': _L0_xattn_in['bv'], 'L0_xattn_Wkv_dca': _L0_xattn_in['Wkv_dca'], 'L0_xattn_bkv_dca': _L0_xattn_in['bkv_dca'], 'L0_xattn_qn_w': _L0_xattn_in['qn_w'], 'L0_xattn_qn_b': _L0_xattn_in['qn_b'], 'L0_xattn_kn_w': _L0_xattn_in['kn_w'], 'L0_xattn_kn_b': _L0_xattn_in['kn_b'], 'L0_xattn_kn_dca_w': _L0_xattn_in['kn_dca_w'], 'L0_xattn_kn_dca_b': _L0_xattn_in['kn_dca_b'], 'L0_xattn_Wo': _L0_xattn_in['Wo'], 'L0_xattn_bo': _L0_xattn_in['bo'], 'L0_attn_W_in': _L0_attn_in['W_in'], 'L0_attn_conv_w': _L0_attn_in['conv_w'], 'L0_attn_conv_b': _L0_attn_in['conv_b'], 'L0_attn_dt_bias': _L0_attn_in['dt_bias'], 'L0_attn_A_log': _L0_attn_in['A_log'], 'L0_attn_D': _L0_attn_in['D'], 'L0_attn_norm_weight': _L0_attn_in['norm_weight'], 'L0_attn_W_out': _L0_attn_in['W_out'], 'L0_ffn_gate_w': _L0_ffn_in['gate_w'], 'L0_ffn_mask_up_w': _L0_ffn_in['mask_up_w'], 'L0_ffn_gate_proj_w': _L0_ffn_in['gate_proj_w'], 'L0_ffn_up_proj_w': _L0_ffn_in['up_proj_w'], 'L0_ffn_down_proj_w': _L0_ffn_in['down_proj_w'], 'L0_ffn_inv_map': _L0_ffn_in['inv_map']}

def reference(x, ctx_1024, L0_xattn_Wq, L0_xattn_bq, L0_xattn_Wk, L0_xattn_bk, L0_xattn_Wv, L0_xattn_bv, L0_xattn_Wkv_dca, L0_xattn_bkv_dca, L0_xattn_qn_w, L0_xattn_qn_b, L0_xattn_kn_w, L0_xattn_kn_b, L0_xattn_kn_dca_w, L0_xattn_kn_dca_b, L0_xattn_Wo, L0_xattn_bo, L0_attn_W_in, L0_attn_conv_w, L0_attn_conv_b, L0_attn_dt_bias, L0_attn_A_log, L0_attn_D, L0_attn_norm_weight, L0_attn_W_out, L0_ffn_gate_w, L0_ffn_mask_up_w, L0_ffn_gate_proj_w, L0_ffn_up_proj_w, L0_ffn_down_proj_w, L0_ffn_inv_map):
    import jax
    import jax.numpy as jnp

    def _L0_xattn_ref(x, y, Wq, bq, Wk, bk, Wv, bv, Wkv_dca, bkv_dca, qn_w, qn_b, kn_w, kn_b, kn_dca_w, kn_dca_b, Wo, bo):
        import jax, jax.numpy as jnp
        import numpy as np
        B, S1, S2, DCA = (2, 512, 256, 16)
        QDIM, KDIM, H = (512, 256, 16)
        HD = QDIM // H
        SCALE = HD ** (-0.5)
        EPS = 1e-06
        DCA_WEIGHT = 1.0

        def _ln(t, w, b):
            m = jnp.mean(t, axis=-1, keepdims=True)
            v = jnp.var(t, axis=-1, keepdims=True)
            return (t - m) * jax.lax.rsqrt(v + EPS) * w + b

        def _attn(q, k, v):
            s = jnp.einsum('bhqd,bhkd->bhqk', q, k) * SCALE
            p = jax.nn.softmax(s, axis=-1)
            return jnp.einsum('bhqk,bhkd->bhqd', p, v)
        b, s1, _ = x.shape
        y_dca = y[:, -DCA:, :]
        y_main = y[:, :-DCA, :]
        kv_dca = (y_dca @ Wkv_dca + bkv_dca).reshape(b, DCA, 2, H, HD)
        k_dca = _ln(kv_dca[:, :, 0], kn_dca_w, kn_dca_b)
        v_dca = kv_dca[:, :, 1]
        s2 = y_main.shape[1]
        q = _ln((x @ Wq + bq).reshape(b, s1, H, HD), qn_w, qn_b)
        kv = jnp.concatenate([y_main @ Wk + bk, y_main @ Wv + bv], axis=-1)
        kv = kv.reshape(b, s2, H, 2 * HD)
        k = _ln(kv[..., :HD], kn_w, kn_b)
        v = kv[..., HD:]
        qT = q.transpose(0, 2, 1, 3)
        ctx = _attn(qT, k.transpose(0, 2, 1, 3), v.transpose(0, 2, 1, 3))
        ctx = ctx.transpose(0, 2, 1, 3).reshape(b, s1, QDIM)
        ctx_dca = _attn(qT, k_dca.transpose(0, 2, 1, 3), v_dca.transpose(0, 2, 1, 3))
        ctx_dca = ctx_dca.transpose(0, 2, 1, 3).reshape(b, s1, QDIM)
        ctx = ctx + DCA_WEIGHT * ctx_dca
        return ctx @ Wo + bo

    def _L0_attn_ref(u, W_in, conv_w, conv_b, dt_bias, A_log, D, norm_weight, W_out):
        import jax, jax.numpy as jnp
        import numpy as np
        D_MODEL = 512
        EXPAND = 2
        D_INNER = EXPAND * D_MODEL
        D_STATE = 128
        NGROUPS = 1
        HEADDIM = 64
        NHEADS = D_INNER // HEADDIM
        D_CONV = 4
        CHUNK = 128
        D_XBC = D_INNER + 2 * NGROUPS * D_STATE
        D_IN_PROJ = 2 * D_INNER + 2 * NGROUPS * D_STATE + NHEADS
        EPS = 1e-05

        def _causal_conv1d(xBC, conv_w, conv_b):
            x = jnp.transpose(xBC, (0, 2, 1))
            x = jnp.pad(x, ((0, 0), (0, 0), (D_CONV - 1, 0)))
            y = jax.lax.conv_general_dilated(x, conv_w[:, None, :], window_strides=(1,), padding='VALID', feature_group_count=D_XBC, dimension_numbers=('NCH', 'OIH', 'NCH'))
            y = y + conv_b[None, :, None]
            return jnp.transpose(jax.nn.silu(y), (0, 2, 1))

        def _ssd(x, dt, A, B, C, D):
            b, L, h, p = x.shape
            n = B.shape[-1]
            c = L // CHUNK
            hpg = h // NGROUPS
            Bh = jnp.repeat(B, hpg, axis=2)
            Ch = jnp.repeat(C, hpg, axis=2)
            xr = x.reshape(b, c, CHUNK, h, p)
            dtr = dt.reshape(b, c, CHUNK, h)
            Br = Bh.reshape(b, c, CHUNK, h, n)
            Cr = Ch.reshape(b, c, CHUNK, h, n)
            xdt = xr * dtr[..., None]
            dA = jnp.transpose((dt * A[None, None, :]).reshape(b, c, CHUNK, h), (0, 3, 1, 2))
            A_cs = jnp.cumsum(dA, axis=-1)
            diff = A_cs[..., :, None] - A_cs[..., None, :]
            mask = jnp.tril(jnp.ones((CHUNK, CHUNK), dtype=bool))
            Lmat = jnp.where(mask, jnp.exp(jnp.where(mask, diff, 0.0)), 0.0)
            Y_diag = jnp.einsum('bclhn,bcshn,bhcls,bcshp->bclhp', Cr, Br, Lmat, xdt)
            decay_states = jnp.exp(A_cs[..., -1:] - A_cs)
            states = jnp.einsum('bclhn,bhcl,bclhp->bchpn', Br, decay_states, xdt)
            chunk_decay = jnp.exp(A_cs[..., -1])

            def step(carry, inp):
                s, d = inp
                return (carry * d[..., None, None] + s, carry)
            init = jnp.zeros((b, h, p, n), dtype=x.dtype)
            _, prev = jax.lax.scan(step, init, (jnp.transpose(states, (1, 0, 2, 3, 4)), jnp.transpose(chunk_decay, (2, 0, 1))))
            prev_states = jnp.transpose(prev, (1, 0, 2, 3, 4))
            Y_off = jnp.einsum('bclhn,bchpn,bhcl->bclhp', Cr, prev_states, jnp.exp(A_cs))
            Y = (Y_diag + Y_off).reshape(b, L, h, p) + x * D[None, None, :, None]
            return Y
        b, L, _ = u.shape
        zxbcdt = jnp.einsum('bld,ed->ble', u, W_in)
        z = zxbcdt[..., :D_INNER]
        xBC = zxbcdt[..., D_INNER:D_INNER + D_XBC]
        dt = zxbcdt[..., D_INNER + D_XBC:]
        xBC = _causal_conv1d(xBC, conv_w, conv_b)
        x = xBC[..., :D_INNER]
        B = xBC[..., D_INNER:D_INNER + NGROUPS * D_STATE].reshape(b, L, NGROUPS, D_STATE)
        C = xBC[..., D_INNER + NGROUPS * D_STATE:].reshape(b, L, NGROUPS, D_STATE)
        dt = jax.nn.softplus(dt + dt_bias[None, None, :])
        A = -jnp.exp(A_log)
        y = _ssd(x.reshape(b, L, NHEADS, HEADDIM), dt, A, B, C, D)
        y = y.reshape(b, L, D_INNER)
        yg = y * jax.nn.silu(z)
        y = yg * jax.lax.rsqrt(jnp.mean(yg * yg, axis=-1, keepdims=True) + EPS) * norm_weight
        return jnp.einsum('bld,ed->ble', y, W_out)

    def _L0_ffn_ref(hidden_states, gate_w, mask_up_w, gate_proj_w, up_proj_w, down_proj_w, inv_map):
        import jax, jax.numpy as jnp
        import numpy as np
        TOP_K = 8
        NEG_INF = -1000000000.0
        B, S, H = hidden_states.shape
        x = hidden_states.reshape(-1, H)
        N = x.shape[0]
        E = gate_w.shape[0]
        scores = jax.nn.softmax(x @ gate_w.T, axis=-1)
        topk_w, topk_idx = jax.lax.top_k(scores, TOP_K)
        w_e = jnp.zeros((N, E), x.dtype).at[jnp.arange(N)[:, None], topk_idx].add(topk_w)
        flat = w_e[:, inv_map]
        scalar = flat.sum(-1)
        soft = jax.nn.softmax(jnp.where(flat == 0, NEG_INF, flat), axis=-1)
        xg = x[:, None, :] + jnp.einsum('ngi,ghi->ngh', soft, mask_up_w)
        g = jnp.einsum('ngh,gih->ngi', xg, gate_proj_w)
        u = jnp.einsum('ngh,gih->ngi', xg, up_proj_w)
        a = jax.nn.silu(g) * u
        d = jnp.einsum('ngi,ghi->ngh', a, down_proj_w)
        y = jnp.einsum('ng,ngh->nh', scalar, d)
        return y.reshape(B, S, H)
    x = x + _L0_xattn_ref(_layernorm(x, axis=-1), ctx_1024, L0_xattn_Wq, L0_xattn_bq, L0_xattn_Wk, L0_xattn_bk, L0_xattn_Wv, L0_xattn_bv, L0_xattn_Wkv_dca, L0_xattn_bkv_dca, L0_xattn_qn_w, L0_xattn_qn_b, L0_xattn_kn_w, L0_xattn_kn_b, L0_xattn_kn_dca_w, L0_xattn_kn_dca_b, L0_xattn_Wo, L0_xattn_bo)
    x = x + _L0_attn_ref(_layernorm(x, axis=-1), L0_attn_W_in, L0_attn_conv_w, L0_attn_conv_b, L0_attn_dt_bias, L0_attn_A_log, L0_attn_D, L0_attn_norm_weight, L0_attn_W_out)
    x = x + _L0_ffn_ref(_layernorm(x, axis=-1), L0_ffn_gate_w, L0_ffn_mask_up_w, L0_ffn_gate_proj_w, L0_ffn_up_proj_w, L0_ffn_down_proj_w, L0_ffn_inv_map)
    return x

_drawn_inputs = setup_inputs


def setup_inputs(seed=0):
    import zlib

    import numpy as np

    out = dict(_drawn_inputs(seed))
    spreads = {'L0_xattn_bq': (0.0, 0.57),
     'L0_xattn_bk': (0.0, 0.1),
     'L0_xattn_bv': (0.0, 0.1),
     'L0_xattn_bkv_dca': (0.0, 0.1),
     'L0_xattn_qn_w': (1.0, 0.6),
     'L0_xattn_qn_b': (0.0, 0.8),
     'L0_xattn_kn_w': (1.0, 0.6),
     'L0_xattn_kn_b': (0.0, 0.8),
     'L0_xattn_kn_dca_w': (1.0, 0.6),
     'L0_xattn_kn_dca_b': (0.0, 0.8),
     'L0_xattn_bo': (0.0, 0.1),
     'L0_attn_D': (1.0, 0.2),
     'L0_attn_norm_weight': (1.0, 0.2)}
    factors = {'L0_ffn_gate_w': 6.029,
     'L0_ffn_mask_up_w': 8.0,
     'L0_ffn_gate_proj_w': 4.222,
     'L0_ffn_up_proj_w': 4.146,
     'L0_ffn_down_proj_w': 4.178}
    for name, (base, spread) in spreads.items():
        noise = np.random.default_rng([zlib.crc32(name.encode()), seed]).standard_normal(out[name].shape)
        drawn = base * np.exp(spread * noise) if base else spread * noise
        out[name] = jnp.asarray(drawn.astype(out[name].dtype))
    for name, factor in factors.items():
        out[name] = (out[name] * factor).astype(out[name].dtype)
    return out
```

```python
import concourse.bass as bass
from concourse import mybir
from contextlib import ExitStack

F32 = mybir.dt.float32
F32R = mybir.dt.float32r
I32 = mybir.dt.int32
ALU = mybir.AluOpType
ACT = mybir.ActivationFunctionType
AX = mybir.AxisListType

P = 128
LQ = 256
QT = LQ // P
DM = 512
MC = DM // P
LK = 4096
NDCA = 16
KDIM = 256
KC = KDIM // P
H = 16
HD = 32
G = 4
NG = H // G
NB = 8
TB = LK // P // NB
BK = TB * P
KEYS = LK - NDCA
LAST = KEYS - (LK - P)
SCALE = float(HD) ** -0.5


def two_part(t):
    return t.bitcast(F32)


class Pools:

    def __init__(self, nc, ctx):
        self.nc, self.ctx, self.sems = nc, ctx, []
        ctx.callback(self.clear)

    def clear(self):
        if self.sems:
            self.nc.clear_and_free_semaphores(self.sems)
            self.nc.all_engine_barrier()

    def sb(self, name, shape, dt=F32):
        return self.ctx.enter_context(self.nc.sbuf_tensor(name, shape, dt))

    def ps(self, name, shape):
        return self.ctx.enter_context(self.nc.psum_tensor(name, shape, F32))

    def sem(self, name):
        self.sems.append(self.nc.alloc_semaphore(name))
        return self.sems[-1]

    def chain(self, eng, name):
        sem, count = self.sem(name), [0]

        def link(ins):
            count[0] += 1
            ins.then_inc(sem, 1)
            eng.wait_ge(sem, count[0])
        return link


def bc(ap, axis, n):
    ap = ap.unsqueeze(axis)
    shape = list(ap.shape)
    shape[axis] = n
    return ap.to_broadcast(shape)


def prepare_attention(nc, io, keep, q_scr, w_scr):
    with ExitStack() as ctx:
        p = Pools(nc, ctx)
        x = p.sb("x_in", [P, QT, DM])
        xn = p.sb("x_norm", [P, QT, DM])
        xT = p.sb("x_norm_T", [P, MC, LQ])
        stat = p.sb("x_stat", [P, QT, 6])
        aggr = p.sb("x_aggr", [P, QT, 2])
        xr = p.sb("x_rstd", [P, QT])
        mhalf = p.sb("minus_half", [P, 32])
        cin = p.sb("ctx_in", [P, NB, TB, KDIM])
        wkv = p.sb("w_kv", [P, KC, 2 * DM])
        wsp = p.sb("w_kv_parts", [P, 2, KC, 2 * DM], F32R)
        wq = p.sb("w_q", [P, MC, DM])
        bq = p.sb("b_q", [P, DM])
        wd = p.sb("w_dca", [P, KC, 2 * DM])
        bd = p.sb("b_dca", [NDCA, 2 * DM])
        qw = p.sb("qn_w", [P, HD])
        qb = p.sb("qn_b", [P, HD])
        dw = p.sb("kn_dca_w", [NDCA, HD])
        db = p.sb("kn_dca_b", [NDCA, HD])
        mean = p.sb("w_mean", [P, MC * H])
        q = p.sb("q", [P, QT * H, HD])
        qsq = p.sb("q_sq", [P, QT * H, HD])
        qv = p.sb("q_var", [P, QT * H])
        qs = p.sb("q_stack", [P, QT, H, 3 * HD], F32R)
        spare = cin[:].rearrange("p b t c -> p (b t c)")
        qall = spare[0:3 * HD, 0:H * LQ].rearrange("p (h l) -> p h l", h=H).bitcast(F32R)
        pdT = spare[0:G * NDCA, H * LQ:(H + 4) * LQ].rearrange("p (g l) -> p g l", g=NG)
        qT = spare[:, (H + 4) * LQ:(H + 8) * LQ].rearrange("p (g l) -> p g l", g=NG)
        vdb = spare[0:G * NDCA, (H + 8) * LQ:(H + 10) * LQ].rearrange("p (g n) -> p g n", g=NG)
        ydT = p.sb("y_dca_T", [P, KC, NDCA])
        kd = p.sb("kv_dca", [NDCA, 2 * DM])
        kdsq = p.sb("k_dca_sq", [NDCA, H, HD])
        kdv = p.sb("k_dca_var", [NDCA, H])
        kdb = p.sb("k_dca_blocks", [P, NG, G * NDCA])
        sd = p.sb("s_dca", [P, QT * H, NDCA])
        sm = p.sb("s_dca_max", [P, QT * H])
        ssum = p.sb("s_dca_sum", [P, QT * H])
        mkd = p.sb("mask_k_dca", [P, G, NDCA])
        mvd = p.sb("mask_v_dca", [G * NDCA, G, HD])
        rep = p.sb("repeat_dca", [NDCA, G, NDCA])
        psc = [p.ps(f"ps_ctx{i}", [P, KC, BK]) for i in range(2)]
        psa = [p.ps(f"ps_a{i}", [P, DM]) for i in range(2)]
        psb = [p.ps(f"ps_b{i}", [P, DM]) for i in range(2)]

        x_in, mask_done, pool_aux = p.sem("x_in_"), p.sem("masks_done"), p.sem("pool_aux")
        ctx_in = [p.sem(f"ctx_in{b}") for b in range(NB)]
        wkv_in, wq_in, wd_in, par_in = p.sem("wkv_in"), p.sem("wq_in"), p.sem("wd_in"), p.sem("par_in")
        cT_ready, chi_ready, clo_ready = p.sem("cT_ready"), p.sem("chi_ready"), p.sem("clo_ready")
        var_ready, rstd_ready = p.sem("var_ready"), p.sem("rstd_ready")
        xn_ready, xT_ps, xT_ready = p.sem("xn_ready"), p.sem("xT_ps"), p.sem("xT_ready")
        wq_ready, q_ps, qc_ready, qsq_ready = p.sem("wq_ready"), p.sem("q_ps"), p.sem("qc_ready"), p.sem("qsq_ready")
        q_ready, qst_ps, qst_ready, qT_ps, qT_ready = (p.sem(n) for n in ("q_ready", "qst_ps", "qst_ready", "qT_ps", "qT_ready"))
        wsp_ready, scr_out = p.sem("wsp_ready"), p.sem("scr_out")
        yd_ready, kd_ps, kdc_ready, kdsq_ready, kd_ready = (p.sem(n) for n in ("yd_ready", "kd_ps", "kdc_ready", "kdsq_ready", "kd_ready"))
        kdT_ps, vrep_ps, blocks_ready, sd_ps, sdm_ready, sde_ready = (p.sem(n) for n in ("kdT_ps", "vrep_ps", "blocks_ready", "sd_ps", "sdm_ready", "sde_ready"))
        pd_ready, pdT_ps, pdT_ready, cd_ps = (p.sem(n) for n in ("pd_ready", "pdT_ps", "pdT_ready", "cd_ps"))
        block = ctx.enter_context(nc.Block())

        @block.sync
        def _(sp):
            sp.dma_start(x[:], io["x"].rearrange("o (t p) d -> p (o t) d", p=P)).then_inc(x_in, 16)
            for b in range(NB):
                src = io["ctx_1024"][0, b * BK:(b + 1) * BK, :].rearrange("(t p) c -> p t c", p=P)
                sp.dma_start(cin[:, b], src).then_inc(ctx_in[b], 16)
            sp.wait_ge(wsp_ready, 1)
            sp.dma_start(w_scr, two_part(wsp[:])).then_inc(scr_out, 16)
            sp.wait_ge(qst_ready, NB)
            sp.dma_start(q_scr, two_part(qall)).then_inc(scr_out, 16)
            sp.wait_ge(scr_out, 32)

        @block.scalar
        def _(act):
            w3 = lambda a: a.rearrange("(c p) n -> p c n", p=P)
            act.dma_start(wkv[:, :, 0:DM], w3(io["L0_xattn_Wk"])).then_inc(wkv_in, 16)
            act.dma_start(wkv[:, :, DM:], w3(io["L0_xattn_Wv"])).then_inc(wkv_in, 16)
            act.dma_start(keep.bkv[:, 0:DM], io["L0_xattn_bk"].partition_broadcast(P)).then_inc(wkv_in, 16)
            act.dma_start(keep.bkv[:, DM:], io["L0_xattn_bv"].partition_broadcast(P)).then_inc(wkv_in, 16)
            act.dma_start(wq[:], w3(io["L0_xattn_Wq"])).then_inc(wq_in, 16)
            act.dma_start(bq[:], io["L0_xattn_bq"].partition_broadcast(P)).then_inc(wq_in, 16)
            act.dma_start(wd[:], w3(io["L0_xattn_Wkv_dca"])).then_inc(wd_in, 16)
            act.dma_start(bd[:], io["L0_xattn_bkv_dca"].partition_broadcast(NDCA)).then_inc(wd_in, 16)
            act.dma_start(qw[:], io["L0_xattn_qn_w"].partition_broadcast(P)).then_inc(par_in, 16)
            act.dma_start(qb[:], io["L0_xattn_qn_b"].partition_broadcast(P)).then_inc(par_in, 16)
            act.dma_start(dw[:], io["L0_xattn_kn_dca_w"].partition_broadcast(NDCA)).then_inc(par_in, 16)
            act.dma_start(db[:], io["L0_xattn_kn_dca_b"].partition_broadcast(NDCA)).then_inc(par_in, 16)
            for h in range(G):
                rows = slice(h * HD, (h + 1) * HD)
                act.dma_start(keep.knw[rows, :], io["L0_xattn_kn_w"].unsqueeze(1)).then_inc(keep.kn_in, 16)
                act.dma_start(keep.knb[rows, :], io["L0_xattn_kn_b"].unsqueeze(1)).then_inc(keep.kn_in, 16)
            for b in range(NB):
                act.wait_ge(cT_ready, b + 1)
                act.activation(keep.cTh[:, :, b * BK:(b + 1) * BK], psc[b % 2][:], ACT.Copy).then_inc(chi_ready, 1)
            for i in range(2):
                act.wait_ge(xT_ps, i + 1)
                act.activation(xT[:, 2 * i:2 * i + 2, :], psa[i][:].rearrange("p (c l) -> p c l", c=2), ACT.Copy).then_inc(xT_ready, 1)
            act.wait_ge(qc_ready, 1)
            act.activation(qsq[:], q[:], ACT.Square).then_inc(qsq_ready, 1)
            act.wait_ge(kdc_ready, 1)
            act.activation(kdsq[:], kd[:, 0:DM].rearrange("p (h d) -> p h d", d=HD), ACT.Square).then_inc(kdsq_ready, 1)
            for b in range(NB):
                act.wait_ge(qst_ps, b + 1)
                act.activation(qall[:, 2 * b:2 * b + 2, :], psa[b % 2][0:3 * HD, :].rearrange("p (h l) -> p h l", h=2),
                               ACT.Copy).then_inc(qst_ready, 1)
            for i in range(2):
                act.wait_ge(qT_ps, i + 1)
                act.activation(qT[:, 2 * i:2 * i + 2, :], psb[i][:].rearrange("p (c l) -> p c l", c=2), ACT.Copy).then_inc(qT_ready, 1)
            act.wait_ge(sdm_ready, 1)
            act.activation(sd[:], sd[:], ACT.Exp).then_inc(sde_ready, 1)

        @block.gpsimd
        def _(pool):
            link = p.chain(pool, "pool_chain")
            link(pool.memset(keep.ident[:], 0.0))
            link(pool.affine_select(out=keep.ident[:], in_=keep.ident[:], compare_op=ALU.not_equal, fill=1.0, base=0,
                                    pattern=[[-1, P]], channel_multiplier=1))
            pool.memset(mhalf[:], -0.5).then_inc(mask_done, 1)
            pool.wait_ge(mask_done, 1)
            pool.wait_ge(var_ready, 1)
            pool.tensor_tensor(xr[:], xr[:], mhalf[:, 0:QT], ALU.pow).then_inc(rstd_ready, 1)
            link(pool.memset(mkd[:], 1.0))
            link(pool.affine_select(out=mkd[:], in_=mkd[:], compare_op=ALU.is_ge, fill=0.0, base=0,
                                    pattern=[[-HD, G], [0, NDCA]], channel_multiplier=1))
            link(pool.affine_select(out=mkd[:], in_=mkd[:], compare_op=ALU.is_ge, fill=0.0, base=HD - 1,
                                    pattern=[[HD, G], [0, NDCA]], channel_multiplier=-1))
            link(pool.memset(mvd[:], 1.0))
            link(pool.affine_select(out=mvd[:], in_=mvd[:], compare_op=ALU.is_ge, fill=0.0, base=0,
                                    pattern=[[-NDCA, G], [0, HD]], channel_multiplier=1))
            link(pool.affine_select(out=mvd[:], in_=mvd[:], compare_op=ALU.is_ge, fill=0.0, base=NDCA - 1,
                                    pattern=[[NDCA, G], [0, HD]], channel_multiplier=-1))
            link(pool.memset(rep[:], 0.0))
            link(pool.affine_select(out=rep[:], in_=rep[:], compare_op=ALU.not_equal, fill=1.0, base=0,
                                    pattern=[[0, G], [-1, NDCA]], channel_multiplier=1))
            for f, base in ((keep.fold_num, 0), (keep.fold_den, HD)):
                link(pool.memset(f[:], 0.0))
                for off in (base, base + 2 * HD):
                    link(pool.affine_select(out=f[:], in_=f[:], compare_op=ALU.not_equal, fill=1.0, base=-off,
                                            pattern=[[-1, HD]], channel_multiplier=1))
            pool.memset(keep.eps[:], 0.0).then_inc(mask_done, 1)
            pool.wait_ge(var_ready, 2)
            pool.tensor_tensor(qv[:], qv[:], mhalf[:, 0:QT * H], ALU.pow).then_inc(rstd_ready, 1)
            pool.wait_ge(var_ready, 3)
            pool.tensor_tensor(kdv[:], kdv[:], mhalf[0:NDCA, 0:H], ALU.pow).then_inc(rstd_ready, 1)

        @block.vector
        def _(dve):
            link = p.chain(dve, "dve_chain")

            def centre(w, groups):
                n = w.shape[0]
                link(dve.tensor_reduce(mean[0:n, 0:groups], w, AX.X, ALU.add))
                link(dve.tensor_scalar(mean[0:n, 0:groups], mean[0:n, 0:groups], 1.0 / HD, None, ALU.mult))
                link(dve.tensor_tensor(w, w, bc(mean[0:n, 0:groups], 2, HD), ALU.subtract))

            dve.wait_ge(x_in, 16)
            for t in range(QT):
                link(dve.bn_stats(stat[:, t, :], x[:, t, :]))
                link(dve.bn_aggr(aggr[:, t, :], stat[:, t, :]))
            dve.tensor_scalar(xr[:], aggr[:, :, 1], 1e-5, None, ALU.add).then_inc(var_ready, 1)

            def low(b):
                dve.wait_ge(chi_ready, b + 1)
                part = slice(b * BK, (b + 1) * BK)
                dve.tensor_tensor(keep.cTl[:, :, part], psc[b % 2][:], two_part(keep.cTh[:, :, part]), ALU.subtract).then_inc(clo_ready, 1)

            low(0)
            low(1)
            dve.wait_ge(rstd_ready, 1)
            for t in range(QT):
                dve.tensor_scalar(xn[:, t, :], x[:, t, :], aggr[:, t, 0:1], xr[:, t:t + 1], ALU.subtract, ALU.mult).then_inc(xn_ready, 1)
            low(2)
            low(3)
            dve.wait_ge(wq_in, 32)
            centre(wq[:].rearrange("p c (h d) -> p (c h) d", d=HD), MC * H)
            centre(bq[:].rearrange("p (h d) -> p h d", d=HD), H)
            low(4)
            low(5)
            dve.wait_ge(wkv_in, 64)
            centre(wkv[:].rearrange("p c (h e) -> p (c h) e", e=2 * HD)[:, :, 0:HD], KC * H)
            centre(keep.bkv[:].rearrange("p (h e) -> p h e", e=2 * HD)[:, :, 0:HD], H)
            low(6)
            low(7)
            link(dve.tensor_copy(wsp[:, 0], wkv[:]))
            dve.tensor_tensor(wsp[:, 1], wkv[:], two_part(wsp[:, 0]), ALU.subtract).then_inc(wsp_ready, 1)
            tail = slice(LK - NDCA, LK)
            dve.wait_ge(clo_ready, NB)
            link(dve.tensor_tensor(ydT[:], two_part(keep.cTh[:, :, tail]), two_part(keep.cTl[:, :, tail]), ALU.add))
            dve.wait_ge(wd_in, 32)
            kpart = wd[:, :, 0:DM]
            for c in range(KC):
                centre(kpart[:, c].rearrange("p (h d) -> p h d", d=HD), H)
            centre(bd[:, 0:DM].rearrange("p (h d) -> p h d", d=HD), H)
            dve.tensor_copy(sm[0:1, 0:1], mean[0:1, 0:1]).then_inc(yd_ready, 1)
            for t in range(QT):
                dve.wait_ge(q_ps, t + 1)
                ins = dve.tensor_tensor(q[:, t * H:(t + 1) * H, :].rearrange("p h d -> p (h d)"), psa[t][:], bq[:], ALU.add)
                link(ins) if t + 1 < QT else ins.then_inc(qc_ready, 1)
            dve.wait_ge(par_in, 64)
            dve.wait_ge(qsq_ready, 1)
            link(dve.tensor_reduce(qv[:], qsq[:], AX.X, ALU.add))
            dve.tensor_scalar(qv[:], qv[:], 1.0 / HD, 1e-6, ALU.mult, ALU.add).then_inc(var_ready, 1)
            dve.wait_ge(rstd_ready, 2)
            link(dve.tensor_tensor(q[:], q[:], bc(qv[:], 2, HD), ALU.mult))
            link(dve.tensor_tensor(q[:], q[:], bc(qw[:], 1, QT * H), ALU.mult))
            link(dve.tensor_tensor(q[:], q[:], bc(qb[:], 1, QT * H), ALU.add))
            link(dve.tensor_scalar(q[:], q[:], SCALE, None, ALU.mult))
            qs3 = qs[:].rearrange("p t h e -> p (t h) e")
            link(dve.tensor_copy(qs3[:, :, 0:HD], q[:]))
            link(dve.tensor_copy(qs3[:, :, HD:2 * HD], q[:]))
            dve.tensor_tensor(qs3[:, :, 2 * HD:], q[:], two_part(qs3[:, :, 0:HD]), ALU.subtract).then_inc(q_ready, 1)
            for i in range(2):
                dve.wait_ge(kd_ps, i + 1)
                ins = dve.tensor_tensor(kd[:, i * DM:(i + 1) * DM], psb[i][0:NDCA, :], bd[:, i * DM:(i + 1) * DM], ALU.add)
                link(ins) if i == 0 else ins.then_inc(kdc_ready, 1)
            dve.wait_ge(kdsq_ready, 1)
            link(dve.tensor_reduce(kdv[:], kdsq[:], AX.X, ALU.add))
            dve.tensor_scalar(kdv[:], kdv[:], 1.0 / HD, 1e-6, ALU.mult, ALU.add).then_inc(var_ready, 1)
            dve.wait_ge(rstd_ready, 3)
            k3 = kd[:, 0:DM].rearrange("p (h d) -> p h d", d=HD)
            link(dve.tensor_tensor(k3, k3, bc(kdv[:], 2, HD), ALU.mult))
            link(dve.tensor_tensor(k3, k3, bc(dw[:], 1, H), ALU.mult))
            dve.tensor_tensor(k3, k3, bc(db[:], 1, H), ALU.add).then_inc(kd_ready, 1)
            dve.wait_ge(mask_done, 2)
            dve.wait_ge(kdT_ps, 1)
            for g in range(NG):
                dve.tensor_tensor(kdb[:, g, :].rearrange("p (h k) -> p h k", h=G),
                                  bc(psa[0][:, g * NDCA:(g + 1) * NDCA], 1, G), mkd[:], ALU.mult).then_inc(blocks_ready, 1)
            dve.wait_ge(vrep_ps, 1)
            for g in range(NG):
                dve.tensor_tensor(vdb[:, g, :], psa[1][0:G * NDCA, g * P:(g + 1) * P],
                                  mvd[:].rearrange("p h d -> p (h d)"), ALU.mult).then_inc(blocks_ready, 1)
            dve.wait_ge(sd_ps, 1)
            s3 = psa[0][:].rearrange("p (h k) -> p h k", k=NDCA)
            link(dve.tensor_reduce(sm[:], s3, AX.X, ALU.max))
            dve.tensor_tensor(sd[:], s3, bc(sm[:], 2, NDCA), ALU.subtract).then_inc(sdm_ready, 1)
            dve.wait_ge(sde_ready, 1)
            link(dve.tensor_reduce(ssum[:], sd[:], AX.X, ALU.add))
            link(dve.reciprocal(ssum[:], ssum[:]))
            dve.tensor_tensor(sd[:], sd[:], bc(ssum[:], 2, NDCA), ALU.mult).then_inc(pd_ready, 1)
            for i in range(2):
                dve.wait_ge(pdT_ps, i + 1)
                dve.tensor_copy(pdT[:, 2 * i:2 * i + 2, :], psb[i][0:G * NDCA, :].rearrange("p (c l) -> p c l", c=2)).then_inc(pdT_ready, 1)
            for i in range(2):
                dve.wait_ge(cd_ps, i + 1)
                dve.tensor_copy(keep.dcaT[:, 2 * i:2 * i + 2, :], psa[i][:].rearrange("p (c l) -> p c l", c=2)).then_inc(keep.dca_done, 1)

        @block.tensor
        def _(pe):
            pe.wait_ge(mask_done, 1)
            for b in range(NB):
                pe.wait_ge(ctx_in[b], 16)
                if b >= 2:
                    pe.wait_ge(clo_ready, b - 1)
                for t in range(TB):
                    for c in range(KC):
                        last = pe.transpose(psc[b % 2][:, c, t * P:(t + 1) * P], cin[:, b, t, c * P:(c + 1) * P], keep.ident[:])
                last.then_inc(cT_ready, 1)
            pe.wait_ge(xn_ready, QT)
            for c in range(MC):
                for t in range(QT):
                    last = pe.transpose(psa[c // 2][:, (c % 2) * LQ + t * P:(c % 2) * LQ + (t + 1) * P],
                                        xn[:, t, c * P:(c + 1) * P], keep.ident[:])
                if c % 2:
                    last.then_inc(xT_ps, 1)
            pe.wait_ge(xT_ready, 2)
            pe.wait_ge(yd_ready, 1)
            for t in range(QT):
                for c in range(MC):
                    last = pe.matmul(psa[t][:], xT[:, c, t * P:(t + 1) * P], wq[:, c, :], start=c == 0, stop=c == MC - 1)
                last.then_inc(q_ps, 1)
            for i in range(2):
                for c in range(KC):
                    last = pe.matmul(psb[i][0:NDCA, :], ydT[:, c, :], wd[:, c, i * DM:(i + 1) * DM], start=c == 0, stop=c == KC - 1)
                last.then_inc(kd_ps, 1)
            pe.wait_ge(q_ready, 1)
            for b in range(NB):
                if b >= 2:
                    pe.wait_ge(qst_ready, b - 1)
                for hh in range(2):
                    for t in range(QT):
                        last = pe.transpose(psa[b % 2][0:3 * HD, hh * LQ + t * P:hh * LQ + (t + 1) * P],
                                            two_part(qs[:, t, 2 * b + hh, :]), keep.ident[:])
                last.then_inc(qst_ps, 1)
            pe.wait_ge(kdc_ready, 1)
            for g in range(NG):
                for t in range(QT):
                    src = q[:, t * H + g * G:t * H + (g + 1) * G, :].rearrange("p h d -> p (h d)")
                    last = pe.transpose(psb[g // 2][:, (g % 2) * LQ + t * P:(g % 2) * LQ + (t + 1) * P], src, keep.ident[:])
                if g % 2:
                    last.then_inc(qT_ps, 1)
            pe.wait_ge(kd_ready, 1)
            pe.wait_ge(mask_done, 2)
            pe.wait_ge(qst_ready, NB)
            for g in range(NG):
                last = pe.transpose(psa[0][:, g * NDCA:(g + 1) * NDCA], kd[:, g * P:(g + 1) * P], keep.ident[0:NDCA, 0:NDCA])
            last.then_inc(kdT_ps, 1)
            pe.matmul(psa[1][0:G * NDCA, :], rep[:].rearrange("p h k -> p (h k)"), kd[:, DM:], start=True, stop=True).then_inc(vrep_ps, 1)
            pe.wait_ge(blocks_ready, 2 * NG)
            pe.wait_ge(qT_ready, 2)
            for t in range(QT):
                for g in range(NG):
                    at = (t * NG + g) * G * NDCA
                    last = pe.matmul(psa[0][:, at:at + G * NDCA], qT[:, g, t * P:(t + 1) * P], kdb[:, g, :], start=True, stop=True)
            last.then_inc(sd_ps, 1)
            pe.wait_ge(pd_ready, 1)
            for g in range(NG):
                for t in range(QT):
                    src = sd[:, t * H + g * G:t * H + (g + 1) * G, :].rearrange("p h k -> p (h k)")
                    last = pe.transpose(psb[g // 2][0:G * NDCA, (g % 2) * LQ + t * P:(g % 2) * LQ + (t + 1) * P], src, keep.ident[:])
                if g % 2:
                    last.then_inc(pdT_ps, 1)
            pe.wait_ge(pdT_ready, 2)
            for g in range(NG):
                last = pe.matmul(psa[g // 2][:, (g % 2) * LQ:(g % 2 + 1) * LQ], vdb[:, g, :], pdT[:, g, :], start=True, stop=True)
                if g % 2:
                    last.then_inc(cd_ps, 1)


def attend(nc, io, keep, q_scr, w_scr):
    with ExitStack() as ctx:
        p = Pools(nc, ctx)
        wg = p.sb("w_group", [P, 2, KC, G * 2 * HD], F32R)
        kth = p.sb("k_T_hi", [P, LK], F32R)
        ktl = p.sb("k_T_lo", [P, LK], F32R)
        vx = p.sb("v_ones", [P, NB * TB, G, 2 * HD])
        kst = [p.sb(f"k_stack{i}", [3 * HD + 2, LK], F32R) for i in range(2)]
        qg = p.sb("q_group", [3 * HD + 2, G, LQ], F32R)
        KR = 4
        kc = p.sb("k_centred", [P, KR, TB * G, HD])
        ksq = p.sb("k_sq", [P, TB * G, HD])
        kv = p.sb("k_var", [P, NB, TB * G])
        kn = p.sb("k_normed", [P, 2, TB, P])
        ktf = p.sb("k_T_f32", [P, 2, BK])
        pr = kc[:].rearrange("p r h d -> p (r h d)").rearrange("p (r t l) -> p r t l", r=2, t=TB)
        mx = p.sb("row_max", [P, QT, NB])
        nm = p.sb("minus_max", [P, QT])
        mp = p.sb("minus_max_parts", [P, QT, 2], F32R)
        o = p.sb("out_parts", [P, LQ])
        rden = p.sb("rden", [P, LQ])
        mhalf = p.sb("minus_half2", [P, TB * G])
        epst = p.sb("k_eps", [P, TB * G])
        ps_e = [p.ps(f"ps_e{i}", [P, TB, LQ]) for i in range(2)]
        ps_m = [p.ps(f"ps_m{i}", [P, BK]) for i in range(2)]
        ps_o = p.ps("ps_o", [P, 2 * LQ])
        ps_f = p.ps("ps_f", [P, 2 * LQ])

        names = ("wg_in qg_in consts kv_ps kv_evac ksq_ready kss_ready kvar_ready krstd_ready kn_ready kt_ps kthi_ready "
                 "ktf_ready ktlo_ready ms_ready mx_ready nm_ready mp_hi mp_ready mt_ps qm_ready es_ready p_ready pv_ready o_ready f_ready rden_ready cx_ready")
        s = {n: p.sem(n) for n in names.split()}
        kst_in = [[p.sem(f"kst_in{i}_{c}") for c in range(NB // 2)] for i in range(2)]
        block = ctx.enter_context(nc.Block())
        PVB = G * NB
        MXU = QT * NB
        DEEP = 5

        def keys_in(b):
            return min(BK, KEYS - b * BK)

        @block.sync
        def _(sp):
            def load_w(g):
                sp.dma_start(two_part(wg[:]), w_scr[:, :, :, bass.ts(g, 2 * P)]).then_inc(s["wg_in"], 16)

            def load_q(g):
                sp.dma_start(two_part(qg[0:3 * HD, :, :]), q_scr[:, bass.ts(g, G), :]).then_inc(s["qg_in"], 16)

            def group(g, more):
                if more:
                    sp.wait_ge(s["kv_ps"], g * NB + NB)
                    load_w(g + 1)
                for h in range(G):
                    for c in range(NB // 2):
                        if h == 0:
                            sp.wait_ge(s["ktlo_ready"], g * NB + 2 * (c + 1))
                        if h >= 2:
                            sp.wait_ge(s["es_ready"], g * PVB + (h - 2) * NB + 2 * (c + 1))
                        ks = slice(c * 2 * BK, (c + 1) * 2 * BK)
                        hr = slice(h * HD, (h + 1) * HD)
                        done = kst_in[h % 2][c]
                        sp.dma_start(two_part(kst[h % 2][0:HD, ks]), two_part(kth[hr, ks])).then_inc(done, 16)
                        sp.dma_start(two_part(kst[h % 2][HD:2 * HD, ks]), two_part(ktl[hr, ks])).then_inc(done, 16)
                        sp.dma_start(two_part(kst[h % 2][2 * HD:3 * HD, ks]), two_part(kth[hr, ks])).then_inc(done, 16)
                if more:
                    sp.wait_ge(s["es_ready"], g * PVB + PVB)
                    load_q(g + 1)

            load_w(0)
            load_q(0)
            with sp.Fori(0, NG - 1) as g:
                group(g, True)
            group(NG - 1, False)

        @block.gpsimd
        def _(pool):
            pool.memset(vx[:], 1.0).then_inc(s["consts"], 1)
            pool.wait_ge(s["consts"], 1)
            for i in range(2):
                pool.memset(two_part(kst[i][3 * HD:, :]), 1.0).then_inc(s["consts"], 1)
                pool.wait_ge(s["consts"], i + 2)
            pool.memset(epst[:], 1e-6).then_inc(s["consts"], 1)
            pool.memset(mhalf[:], -0.5).then_inc(s["consts"], 1)
            pool.wait_ge(s["consts"], 5)
            with pool.Fori(0, NG) as g:
                for b in range(NB):
                    pool.wait_ge(s["kss_ready"], g * NB + b + 1)
                    pool.tensor_tensor(kv[:, b, :], kv[:, b, :], epst[:], ALU.add).then_inc(s["kvar_ready"], 1)
                    pool.wait_ge(s["kvar_ready"], g * NB + b + 1)
                    pool.tensor_tensor(kv[:, b, :], kv[:, b, :], mhalf[:], ALU.pow).then_inc(s["krstd_ready"], 1)

        @block.scalar
        def _(act):
            act.wait_ge(keep.kn_in, 16 * 2 * G)
            with act.Fori(0, NG) as g:
                for step in range(NB + 4):
                    b = step
                    if b < NB:
                        act.wait_ge(s["kv_evac"], g * NB + b + 1)
                        if b >= 1:
                            act.wait_ge(s["kss_ready"], g * NB + b)
                        act.activation(ksq[:], kc[:, b % KR], ACT.Square, scale=HD ** -0.5).then_inc(s["ksq_ready"], 1)
                    b = step - 4
                    if b >= 0:
                        act.wait_ge(s["kt_ps"], g * NB + b + 1)
                        if b >= 2:
                            act.wait_ge(s["ktlo_ready"], g * NB + b - 1)
                        act.activation(ktf[:, b % 2], ps_m[b % 2][:], ACT.Identity, bias=keep.knb[:], scale=keep.knw[:]).then_inc(s["ktf_ready"], 1)
                        act.activation(kth[:, b * BK:(b + 1) * BK], ps_m[b % 2][:], ACT.Identity, bias=keep.knb[:],
                                       scale=keep.knw[:]).then_inc(s["kthi_ready"], 1)
                for h in range(G):
                    for b in range(NB):
                        n = h * NB + b
                        act.wait_ge(s["es_ready"], g * PVB + n + 1)
                        if n >= 2:
                            act.wait_ge(s["pv_ready"], g * PVB + n - 1)
                        if b < NB - 1:
                            act.activation(pr[:, n % 2], ps_e[n % 2][:], ACT.Exp).then_inc(s["p_ready"], 1)
                        else:
                            act.activation(pr[:, n % 2, 0:TB - 1], ps_e[n % 2][:, 0:TB - 1], ACT.Exp)
                            act.activation(pr[0:LAST, n % 2, TB - 1], ps_e[n % 2][0:LAST, TB - 1], ACT.Exp).then_inc(s["p_ready"], 1)

        @block.vector
        def _(dve):
            dve.wait_ge(s["consts"], 5)
            with dve.Fori(0, NG) as g:
                bias = keep.bkv[:, bass.ts(g, 2 * P)]
                for step in range(NB + DEEP):
                    b = step
                    if b < NB:
                        dve.wait_ge(s["kv_ps"], g * NB + b + 1)
                        kv_t = ps_e[b % 2][:].rearrange("p t (h e) -> p t h e", e=2 * HD)
                        for t in range(TB):
                            b3 = bias.rearrange("p (h e) -> p h e", e=2 * HD)
                            dve.tensor_tensor(vx[:, b * TB + t, :, 0:HD], kv_t[:, t, :, HD:], b3[:, :, HD:], ALU.add)
                            last = dve.tensor_tensor(kc[:, b % KR, t * G:(t + 1) * G, :], kv_t[:, t, :, 0:HD], b3[:, :, 0:HD], ALU.add)
                        last.then_inc(s["kv_evac"], 1)
                    b = step - 1
                    if 0 <= b < NB:
                        dve.wait_ge(s["ksq_ready"], g * NB + b + 1)
                        dve.tensor_reduce(kv[:, b, :], ksq[:], AX.X, ALU.add).then_inc(s["kss_ready"], 1)
                    b = step - 3
                    if 0 <= b < NB:
                        dve.wait_ge(s["krstd_ready"], g * NB + b + 1)
                        if b >= 2:
                            dve.wait_ge(s["kt_ps"], g * NB + b - 1)
                        dve.tensor_tensor(kn[:, b % 2].rearrange("p t (h d) -> p (t h) d", d=HD), kc[:, b % KR],
                                          bc(kv[:, b, :], 2, HD), ALU.mult).then_inc(s["kn_ready"], 1)
                    b = step - DEEP
                    if b >= 0:
                        dve.wait_ge(s["kthi_ready"], g * NB + b + 1)
                        ks = slice(b * BK, (b + 1) * BK)
                        dve.tensor_tensor(ktl[:, ks], ktf[:, b % 2], two_part(kth[:, ks]), ALU.subtract).then_inc(s["ktlo_ready"], 1)

                def row_max(h):
                    for u in range(MXU):
                        kb, t = divmod(u, QT)
                        dve.wait_ge(s["ms_ready"], g * G * MXU + h * MXU + u + 1)
                        dve.reduce_max(mx[:, t, kb:kb + 1], ps_m[u % 2][:, 0:keys_in(kb)], AX.X).then_inc(s["mx_ready"], 1)
                    dve.wait_ge(s["mx_ready"], g * G * MXU + (h + 1) * MXU)
                    dve.tensor_reduce(nm[:], mx[:], AX.X, ALU.max, negate=True).then_inc(s["nm_ready"], 1)
                    dve.wait_ge(s["nm_ready"], g * G + h + 1)
                    dve.tensor_copy(mp[:, :, 0], nm[:]).then_inc(s["mp_hi"], 1)
                    dve.wait_ge(s["mp_hi"], g * G + h + 1)
                    dve.tensor_tensor(mp[:, :, 1], nm[:], two_part(mp[:, :, 0]), ALU.subtract).then_inc(s["mp_ready"], 1)

                def max_rows(h):
                    dve.wait_ge(s["mt_ps"], g * G + h + 1)
                    dve.tensor_copy(qg[3 * HD:, h, :], ps_m[0][0:2, 0:LQ]).then_inc(s["qm_ready"], 1)

                row_max(0)
                max_rows(0)
                for h in range(G):
                    if h + 1 < G:
                        row_max(h + 1)
                    dve.wait_ge(s["pv_ready"], g * PVB + (h + 1) * NB)
                    if h >= 1:
                        dve.wait_ge(s["f_ready"], g * G + h)
                    dve.tensor_copy(o[:], ps_o[:, 0:LQ]).then_inc(s["o_ready"], 1)
                    if h + 1 < G:
                        max_rows(h + 1)
                dve.wait_ge(s["f_ready"], g * G + G)
                dve.reciprocal(rden[:], ps_f[:, LQ:]).then_inc(s["rden_ready"], 1)
                dve.wait_ge(s["rden_ready"], g + 1)
                dve.tensor_tensor(keep.ctxT[:, bass.ts(g, LQ)], ps_f[:, 0:LQ], rden[:], ALU.mult).then_inc(s["cx_ready"], 1)

        @block.tensor
        def _(pe):
            pe.wait_ge(s["consts"], 5)
            with pe.Fori(0, NG) as g:
                pe.wait_ge(s["wg_in"], g * 16 + 16)
                for step in range(NB + 3):
                    b = step
                    if b < NB:
                        if b >= 2:
                            pe.wait_ge(s["kv_evac"], g * NB + b - 1)
                        for t in range(TB):
                            tok = slice((b * TB + t) * P, (b * TB + t + 1) * P)
                            passes = [(a, w, c) for a, w in ((keep.cTh, 0), (keep.cTl, 0), (keep.cTh, 1)) for c in range(KC)]
                            for i, (a, w, c) in enumerate(passes):
                                last = pe.matmul(ps_e[b % 2][:, t, :], a[:, c, tok], wg[:, w, c, :], start=i == 0, stop=i == len(passes) - 1)
                        last.then_inc(s["kv_ps"], 1)
                    b = step - 3
                    if b >= 0:
                        pe.wait_ge(s["kn_ready"], g * NB + b + 1)
                        if b >= 2:
                            pe.wait_ge(s["kthi_ready"], g * NB + b - 1)
                        for t in range(TB):
                            last = pe.transpose(ps_m[b % 2][:, t * P:(t + 1) * P], kn[:, b % 2, t, :], keep.ident[:])
                        last.then_inc(s["kt_ps"], 1)
                pe.wait_ge(s["kthi_ready"], g * NB + NB)
                pe.wait_ge(s["kv_evac"], g * NB + NB)
                pe.wait_ge(s["qg_in"], g * 16 + 16)

                def max_unit(h, u):
                    kb, t = divmod(u, QT)
                    n = keys_in(kb)
                    if t == 0:
                        pe.wait_ge(kst_in[h % 2][kb // 2], g * 96 + 48 * (h // 2 + 1))
                    if h * MXU + u >= 2:
                        pe.wait_ge(s["mx_ready"], g * G * MXU + h * MXU + u - 1)
                    pe.matmul(ps_m[u % 2][:, 0:n], qg[0:3 * HD, h, t * P:(t + 1) * P], kst[h % 2][0:3 * HD, kb * BK:kb * BK + n],
                              start=True, stop=True).then_inc(s["ms_ready"], 1)

                def turn_max(h):
                    pe.wait_ge(s["mp_ready"], g * G + h + 1)
                    for t in range(QT):
                        last = pe.transpose(ps_m[0][0:2, t * P:(t + 1) * P], two_part(mp[:, t, :]), keep.ident[:])
                    last.then_inc(s["mt_ps"], 1)

                def scores(h, b):
                    n = h * NB + b
                    if b == 0:
                        pe.wait_ge(s["qm_ready"], g * G + h + 1)
                    if n >= 2:
                        pe.wait_ge(s["p_ready"], g * PVB + n - 1)
                    for t in range(TB):
                        m = min(P, keys_in(b) - t * P)
                        at = b * BK + t * P
                        last = pe.matmul(ps_e[n % 2][0:m, t, :], kst[h % 2][:, at:at + m], qg[:, h, :], start=True, stop=True)
                    last.then_inc(s["es_ready"], 1)

                def weighted(h, b):
                    n = h * NB + b
                    pe.wait_ge(s["p_ready"], g * PVB + n + 1)
                    if b == 0 and h >= 1:
                        pe.wait_ge(s["o_ready"], g * G + h)
                    for t in range(TB):
                        m = min(P, keys_in(b) - t * P)
                        half = slice(t % 2 * 2 * HD, (t % 2 + 1) * 2 * HD)
                        last = pe.matmul(ps_o[half, 0:LQ], vx[0:m, b * TB + t, h, :], pr[0:m, n % 2, t, :],
                                         start=b == 0 and t < 2, stop=b == NB - 1 and t >= TB - 2)
                    last.then_inc(s["pv_ready"], 1)

                def fold(h):
                    pe.wait_ge(s["o_ready"], g * G + h + 1)
                    rows = slice(h * HD, (h + 1) * HD)
                    pe.matmul(ps_f[rows, 0:LQ], keep.fold_num[:], o[:], start=True, stop=True)
                    pe.matmul(ps_f[rows, LQ:], keep.fold_den[:], o[:], start=True, stop=True).then_inc(s["f_ready"], 1)

                for u in range(MXU):
                    max_unit(0, u)
                turn_max(0)
                for h in range(G):
                    done = 0
                    for b in range(NB):
                        scores(h, b)
                        while h + 1 < G and done < min(MXU, MXU * (b + 1) // (NB - 1)):
                            max_unit(h + 1, done)
                            done += 1
                        if b >= 1:
                            weighted(h, b - 1)
                        if b == 1 and h >= 1:
                            fold(h - 1)
                    weighted(h, NB - 1)
                    if h + 1 < G:
                        turn_max(h + 1)
                fold(G - 1)


def project_attention(nc, io, keep):
    with ExitStack() as ctx:
        p = Pools(nc, ctx)
        wo = p.sb("w_o", [P, MC, DM])
        bo = p.sb("b_o", [P, DM])
        x = p.sb("x_again", [P, QT, DM])
        c = p.sb("ctx_sum", [P, NG * LQ])
        ps = [p.ps(f"ps_wo{t}", [P, DM]) for t in range(QT)]
        wo_in, xb_in, xb_ready, c_ready, wo_ps = (p.sem(n) for n in ("wo_in", "xb_in", "xb_ready", "c_ready", "wo_ps"))
        block = ctx.enter_context(nc.Block())

        @block.sync
        def _(sp):
            sp.dma_start(wo[:], io["L0_xattn_Wo"].rearrange("(c p) n -> p c n", p=P)).then_inc(wo_in, 16)
            sp.dma_start(bo[:], io["L0_xattn_bo"].partition_broadcast(P)).then_inc(xb_in, 16)
            sp.dma_start(x[:], io["x"].rearrange("o (t p) d -> p (o t) d", p=P)).then_inc(xb_in, 16)

        @block.vector
        def _(dve):
            dve.tensor_tensor(c[:], keep.ctxT[:], keep.dcaT[:].rearrange("p g l -> p (g l)"), ALU.add).then_inc(c_ready, 1)
            dve.wait_ge(xb_in, 32)
            dve.tensor_tensor(x[:], x[:], bc(bo[:], 1, QT), ALU.add).then_inc(xb_ready, 1)
            dve.wait_ge(xb_ready, 1)
            for t in range(QT):
                dve.wait_ge(wo_ps, t + 1)
                dve.tensor_tensor(keep.x1[:, t, :], ps[t][:], x[:, t, :], ALU.add).then_inc(keep.x1_ready, 1)

        @block.tensor
        def _(pe):
            pe.wait_ge(wo_in, 16)
            pe.wait_ge(c_ready, 1)
            for t in range(QT):
                for g in range(NG):
                    at = g * LQ + t * P
                    last = pe.matmul(ps[t][:], c[:, at:at + P], wo[:, g, :], start=g == 0, stop=g == NG - 1)
                last.then_inc(wo_ps, 1)


DI = 1024
NS = 128
NH = 16
HP = DI // NH
CT = DI // P
XT = (DI + 2 * NS) // P
TAPS = 4
CH = 128
NCH = LQ // CH
BT, CTT = CT, CT + 1


def mixer_projections(nc, io, keep):
    with ExitStack() as ctx:
        p = Pools(nc, ctx)
        stat = p.sb("u_stat", [P, QT, 6])
        aggr = p.sb("u_aggr", [P, QT, 2])
        ur = p.sb("u_rstd", [P, QT])
        un = p.sb("u", [P, QT, DM])
        mhalf = p.sb("minus_half3", [P, QT])
        uh = p.sb("u_T_hi", [P, MC, LQ], F32R)
        ul = p.sb("u_T_lo", [P, MC, LQ], F32R)
        w = p.sb("w_in_rows", [P, 2, DM])
        wh = [p.sb(f"w_in_T_hi{i}", [P, MC, P], F32R) for i in range(2)]
        wl = [p.sb(f"w_in_T_lo{i}", [P, MC, P], F32R) for i in range(2)]
        wdt = p.sb("w_dt_rows", [NH, DM])
        wdh = p.sb("w_dt_T_hi", [P, MC, NH], F32R)
        wdl = p.sb("w_dt_T_lo", [P, MC, NH], F32R)
        cw = p.sb("conv_w", [P, XT, TAPS])
        cb = p.sb("conv_b", [P, XT])
        xp = p.sb("conv_in", [P, 2, TAPS - 1 + LQ])
        cv = p.sb("conv_sum", [P, 2, TAPS, LQ])
        ps_t = [p.ps(f"ps_wt{i}", [P, DM]) for i in range(2)]
        ps_x = [p.ps(f"ps_xz{i}", [P, DM]) for i in range(2)]
        ps_u = [p.ps(f"ps_u{i}", [P, DM]) for i in range(2)]
        ps_d = [p.ps(f"ps_dt{i}", [P, DM]) for i in range(2)]
        names = ("var_u rstd_u un_ready uT_ps uh_ready ul_ready wT_ps wh_ready wl_ready xz_ps xz_read conv_ready xc_done "
                 "wd_in wdT_ps wdh_ready wdl_ready dt_ps conv_in zero_ready pool_c")
        s = {n: p.sem("m_" + n) for n in names.split()}
        w_in = [p.sem(f"w_rows_in{i}") for i in range(2)]
        block = ctx.enter_context(nc.Block())
        wv = io["L0_attn_W_in"]
        NZ, NX = CT // 2, XT // 2

        @block.sync
        def _(sp):
            sp.dma_start(wdt[:], wv[(CT + XT) * P:, :]).then_inc(s["wd_in"], 16)
            rows = wv[0:(CT + XT) * P, :].rearrange("(i j p) d -> i j p d", j=2, p=P)
            for j in range(2):
                sp.dma_start(w[:, j, :], rows[0, j]).then_inc(w_in[j], 16)
            sp.dma_start(cw[:], io["L0_attn_conv_w"].rearrange("(c p) k -> p c k", p=P)).then_inc(s["conv_in"], 16)
            sp.dma_start(cb[:], io["L0_attn_conv_b"].rearrange("(c p) -> p c", p=P), allow_slow_non_contiguous=True).then_inc(s["conv_in"], 16)
            with sp.Fori(1, NZ + NX) as i:
                for j in range(2):
                    sp.wait_ge(s["wT_ps"], 2 * i + j - 1)
                    sp.dma_start(w[:, j, :], rows[i, j]).then_inc(w_in[j], 16)

        @block.gpsimd
        def _(pool):
            pool.memset(mhalf[:], -0.5).then_inc(s["pool_c"], 1)
            pool.memset(xp[:, :, 0:TAPS - 1], 0.0).then_inc(s["zero_ready"], 1)
            pool.wait_ge(s["pool_c"], 1)
            pool.wait_ge(s["var_u"], 1)
            pool.tensor_tensor(ur[:], ur[:], mhalf[:], ALU.pow).then_inc(s["rstd_u"], 1)

        @block.scalar
        def _(act):
            for i in range(2):
                act.wait_ge(s["uT_ps"], i + 1)
                act.activation(uh[:, 2 * i:2 * i + 2, :], ps_u[i][:].rearrange("p (c l) -> p c l", c=2), ACT.Copy).then_inc(s["uh_ready"], 1)
            act.wait_ge(s["wdT_ps"], 1)
            act.activation(wdh[:], ps_d[0][:, 0:MC * NH].rearrange("p (c h) -> p c h", c=MC), ACT.Copy).then_inc(s["wdh_ready"], 1)

            def w_high(n, j):
                act.wait_ge(s["wT_ps"], n + 1)
                act.activation(wh[j][:], ps_t[j][:].rearrange("p (c n) -> p c n", c=MC), ACT.Copy).then_inc(s["wh_ready"], 1)

            with act.Fori(0, NZ) as i:
                for j in range(2):
                    w_high(2 * i + j, j)
                for j in range(2):
                    act.wait_ge(s["xz_ps"], 2 * i + j + 1)
                    act.activation(keep.zs[:, bass.ts(2 * i + j, LQ)], ps_x[j][:, 0:LQ], ACT.Silu).then_inc(s["xz_read"], 1)
            act.wait_ge(s["zero_ready"], 1)
            with act.Fori(0, NX) as i:
                for j in range(2):
                    w_high(2 * i + j + CT, j)
                for j in range(2):
                    act.wait_ge(s["xz_ps"], 2 * i + j + 1 + CT)
                    act.activation(xp[:, j, TAPS - 1:], ps_x[j][:, 0:LQ], ACT.Copy).then_inc(s["xz_read"], 1)
                for j in range(2):
                    act.wait_ge(s["conv_ready"], (2 * i + j + 1) * TAPS)
                    act.activation(keep.xc[:, bass.ts(2 * i + j, LQ)], cv[:, j, TAPS - 1, :], ACT.Silu).then_inc(s["xc_done"], 1)

        @block.vector
        def _(dve):
            link = p.chain(dve, "m_dve_chain")
            dve.wait_ge(keep.x1_ready, QT)
            for t in range(QT):
                link(dve.bn_stats(stat[:, t, :], keep.x1[:, t, :]))
                link(dve.bn_aggr(aggr[:, t, :], stat[:, t, :]))
            dve.tensor_scalar(ur[:], aggr[:, :, 1], 1e-5, None, ALU.add).then_inc(s["var_u"], 1)
            dve.wait_ge(s["rstd_u"], 1)
            for t in range(QT):
                dve.tensor_scalar(un[:, t, :], keep.x1[:, t, :], aggr[:, t, 0:1], ur[:, t:t + 1], ALU.subtract, ALU.mult).then_inc(s["un_ready"], 1)
            for i in range(2):
                dve.wait_ge(s["uh_ready"], i + 1)
                part = slice(2 * i, 2 * i + 2)
                dve.tensor_tensor(ul[:, part, :], ps_u[i][:].rearrange("p (c l) -> p c l", c=2), two_part(uh[:, part, :]),
                                  ALU.subtract).then_inc(s["ul_ready"], 1)
            dve.wait_ge(s["wdh_ready"], 1)
            dve.tensor_tensor(wdl[:], ps_d[0][:, 0:MC * NH].rearrange("p (c h) -> p c h", c=MC), two_part(wdh[:]), ALU.subtract).then_inc(s["wdl_ready"], 1)

            def w_low(n, j):
                dve.wait_ge(s["wh_ready"], n + 1)
                dve.tensor_tensor(wl[j][:], ps_t[j][:].rearrange("p (c n) -> p c n", c=MC), two_part(wh[j][:]), ALU.subtract).then_inc(s["wl_ready"], 1)

            with dve.Fori(0, NZ) as i:
                for j in range(2):
                    w_low(2 * i + j, j)
            dve.wait_ge(s["conv_in"], 32)
            with dve.Fori(0, NX) as i:
                for j in range(2):
                    w_low(2 * i + j + CT, j)
                for j in range(2):
                    dve.wait_ge(s["xz_read"], 2 * i + j + 1 + CT)
                    done = (2 * i + j) * TAPS
                    tile = 2 * i + j
                    taps = cw[:].rearrange("p c k -> p (c k)")[:, bass.ts(tile, TAPS)]
                    dve.tensor_scalar(cv[:, j, 0, :], xp[:, j, 0:LQ], taps[:, 0:1], cb[:, bass.ts(tile, 1)], ALU.mult, ALU.add).then_inc(s["conv_ready"], 1)
                    for k in range(1, TAPS):
                        dve.wait_ge(s["conv_ready"], done + k)
                        dve.scalar_tensor_tensor(cv[:, j, k, :], xp[:, j, k:k + LQ], taps[:, k:k + 1], cv[:, j, k - 1, :],
                                                 ALU.mult, ALU.add).then_inc(s["conv_ready"], 1)
            for t in range(QT):
                dve.wait_ge(s["dt_ps"], t + 1)
                dve.tensor_copy(keep.dt[:, t, :], ps_d[t][:, 256:256 + NH]).then_inc(keep.dt_ready, 1)

        @block.tensor
        def _(pe):
            pe.wait_ge(s["wd_in"], 16)
            for c in range(MC):
                last = pe.transpose(ps_d[0][:, c * NH:(c + 1) * NH], wdt[:, c * P:(c + 1) * P], keep.ident[0:NH, 0:NH])
            last.then_inc(s["wdT_ps"], 1)
            pe.wait_ge(s["un_ready"], QT)
            for c in range(MC):
                for t in range(QT):
                    last = pe.transpose(ps_u[c // 2][:, (c % 2) * LQ + t * P:(c % 2) * LQ + (t + 1) * P],
                                        un[:, t, c * P:(c + 1) * P], keep.ident[:])
                if c % 2:
                    last.then_inc(s["uT_ps"], 1)
            passes = lambda h, l, a, b: [(x, y, c) for x, y in ((h, a), (l, a), (h, b)) for c in range(MC)]

            def pair(i, base):
                for j in range(2):
                    pe.wait_ge(w_in[j], 16 * (i + base // 2 + 1))
                    if base:
                        pe.wait_ge(s["wl_ready"], 2 * i + j + base - 1)
                    for c in range(MC):
                        last = pe.transpose(ps_t[j][:, c * P:(c + 1) * P], w[:, j, c * P:(c + 1) * P], keep.ident[:])
                    last.then_inc(s["wT_ps"], 1)
                for j in range(2):
                    pe.wait_ge(s["wl_ready"], 2 * i + j + base + 1)
                    if base:
                        pe.wait_ge(s["xz_read"], 2 * i + j + base - 1)
                    every = passes(wh[j], wl[j], uh, ul)
                    for n, (a, b, c) in enumerate(every):
                        last = pe.matmul(ps_x[j][:, 0:LQ], a[:, c, :], b[:, c, :], start=n == 0, stop=n == len(every) - 1)
                    last.then_inc(s["xz_ps"], 1)

            pe.wait_ge(s["ul_ready"], 2)
            pair(0, 0)
            with pe.Fori(0, NZ + NX - 1) as i:
                pair(i, 2)
            pe.wait_ge(s["wdl_ready"], 1)
            for t in range(QT):
                every = passes(uh, ul, wdh, wdl)
                for n, (a, b, c) in enumerate(every):
                    last = pe.matmul(ps_d[t][:, 256:256 + NH], a[:, c, t * P:(t + 1) * P], b[:, c, :], start=n == 0, stop=n == len(every) - 1)
                last.then_inc(s["dt_ps"], 1)


def mixer(nc, io, keep):
    with ExitStack() as ctx:
        p = Pools(nc, ctx)
        wo = p.sb("w_out_rows", [P, MC, DI])
        woT = p.sb("w_out_T", [P, CT, DM])
        dtb = p.sb("dt_bias", [P, NH])
        al = p.sb("a_log", [P, NH])
        dsk = p.sb("d_skip", [P, CT])
        nw = p.sb("norm_w", [P, CT])
        tri = p.sb("tri", [P, P])
        ones = p.sb("ones", [P, P])
        t1 = p.sb("dt_tmp", [P, NCH * NH])
        t2 = p.sb("dt_pos", [P, NCH * NH])
        dA = p.sb("dA", [P, NCH, NH])
        acs = p.sb("a_cumsum", [P, NCH, NH])
        dAU = p.sb("dA_tri", [P, NCH, NH, P])
        seg = p.sb("decay", [P, NCH, NH, P])
        eA = p.sb("exp_a", [P, NH, P])
        gt = p.sb("b_c", [P, NCH, P])
        xdt = p.sb("x_dt", [P, NCH, DI])
        dst = p.sb("decay_to_end", [P, NH])
        xdd = p.sb("x_dt_decay", [P, DI])
        bt = p.sb("b_tokens", [P, NS])
        st = p.sb("state_T", [P, DI])
        yg = p.sb("y_gated", [P, CT, LQ])
        ysq = p.sb("y_sq", [P, CT, LQ])
        rs = p.sb("y_rstd", [P, QT])
        mhalf = p.sb("minus_half4", [P, QT])
        ps_r = p.ps("ps_rep", [P, NH, P])
        ps_a = [p.ps(f"ps_ma{i}", [P, DM]) for i in range(4)]
        names = ("wo_in par_in tri_ready v1 e1 l1 ea dA_ready dAU_ready acs_ps acs_ready rep_ps seg_sub seg_exp eA_ready cbx gt_ps gt_ready "
                 "wts_ready xt_ps xdt_ready bt_ready dst_sub dst_ready xdd_ready st_ps st_ready cp_ready y_ps yx yz ysq_ready woT_ps woT_ready "
                 "rs_ps rs_var rs_ready yn_ready out_ps mixc")
        s = {n: p.sem("x_" + n) for n in names.split()}
        block = ctx.enter_context(nc.Block())

        @block.sync
        def _(sp):
            sp.dma_start(wo[:], io["L0_attn_W_out"].rearrange("(c p) n -> p c n", p=P)).then_inc(s["wo_in"], 16)
            sp.dma_start(dtb[:], io["L0_attn_dt_bias"].partition_broadcast(P)).then_inc(s["par_in"], 16)
            sp.dma_start(al[:], io["L0_attn_A_log"].partition_broadcast(P)).then_inc(s["par_in"], 16)
            sp.dma_start(nw[:], io["L0_attn_norm_weight"].rearrange("(c p) -> p c", p=P), allow_slow_non_contiguous=True).then_inc(s["par_in"], 16)
            for k in range(P // HP):
                src = io["L0_attn_D"].rearrange("(c k) -> k c", k=P // HP)[k].partition_broadcast(HP)
                sp.dma_start(dsk[k * HP:(k + 1) * HP, :], src, allow_slow_non_contiguous=True).then_inc(s["par_in"], 16)

        @block.gpsimd
        def _(pool):
            link = p.chain(pool, "x_pool_chain")
            link(pool.memset(ones[:], 1.0))
            link(pool.memset(tri[:], 1.0))
            link(pool.affine_select(out=tri[:], in_=tri[:], compare_op=ALU.is_ge, fill=0.0, base=0, pattern=[[1, P]], channel_multiplier=-1))
            pool.memset(mhalf[:], -0.5).then_inc(s["tri_ready"], 1)
            pool.wait_ge(s["rs_var"], 1)
            pool.tensor_tensor(rs[:], rs[:], mhalf[:], ALU.pow).then_inc(s["rs_ready"], 1)

        @block.scalar
        def _(act):
            act.wait_ge(s["v1"], 1)
            act.activation(t1[:], t1[:], ACT.Exp, scale=-1.0).then_inc(s["e1"], 1)
            act.wait_ge(s["par_in"], 80)
            act.activation(al[:], al[:], ACT.Exp).then_inc(s["ea"], 1)
            act.wait_ge(s["e1"], 1)
            act.activation(t1[:], t1[:], ACT.Ln, bias=1.0).then_inc(s["l1"], 1)
            for c in range(NCH):
                act.wait_ge(s["seg_sub"], c + 1)
                act.activation(seg[:, c], seg[:, c], ACT.Exp).then_inc(s["seg_exp"], 1)
                if c == 0:
                    act.wait_ge(s["dst_sub"], 1)
                    act.activation(dst[:], dst[:], ACT.Exp).then_inc(s["dst_ready"], 1)
                else:
                    act.activation(eA[:], ps_r[:], ACT.Exp).then_inc(s["eA_ready"], 1)
            act.wait_ge(s["st_ps"], 1)
            for i in range(2):
                act.activation(st[:, i * DM:(i + 1) * DM], ps_a[i][:], ACT.Copy).then_inc(s["st_ready"], 1)
            for k in range(CT):
                act.wait_ge(s["woT_ps"], k + 1)
                act.activation(woT[:, k, :], ps_r[:].rearrange("p h l -> p (h l)")[:, (k % 4) * DM:(k % 4 + 1) * DM], ACT.Copy).then_inc(s["woT_ready"], 1)
            for k in range(CT):
                act.wait_ge(s["yz"], k + 1)
                act.activation(ysq[:, k, :], yg[:, k, :], ACT.Square).then_inc(s["ysq_ready"], 1)

        @block.vector
        def _(dve):
            link = p.chain(dve, "x_dve_chain")
            dve.wait_ge(s["par_in"], 80)
            dve.wait_ge(keep.dt_ready, QT)
            dt2 = keep.dt[:].rearrange("p t h -> p (t h)")
            link(dve.tensor_tensor(keep.dt[:], keep.dt[:], bc(dtb[:], 1, NCH), ALU.add))
            link(dve.tensor_scalar(t2[:], dt2, 0.0, None, ALU.max))
            link(dve.tensor_scalar(t1[:], dt2, -1.0, None, ALU.mult))
            dve.tensor_tensor(t1[:], t1[:], dt2, ALU.max).then_inc(s["v1"], 1)
            dve.wait_ge(s["l1"], 1)
            link(dve.tensor_tensor(dt2, t2[:], t1[:], ALU.add))
            dve.wait_ge(s["ea"], 1)
            link(dve.tensor_scalar(al[:], al[:], -1.0, None, ALU.mult))
            dve.tensor_tensor(dA[:], keep.dt[:], bc(al[:], 1, NCH), ALU.mult).then_inc(s["dA_ready"], 1)
            dve.wait_ge(s["dA_ready"], 1)
            dve.wait_ge(s["tri_ready"], 1)
            for c in range(NCH):
                dve.tensor_tensor(dAU[:, c], bc(dA[:, c, :], 2, P), bc(tri[:], 1, NH), ALU.mult).then_inc(s["dAU_ready"], 1)
            dve.wait_ge(s["acs_ps"], 1)
            dve.tensor_copy(acs[:], ps_a[0][:, 0:NCH * NH].rearrange("p (c h) -> p c h", c=NCH)).then_inc(s["acs_ready"], 1)
            dve.wait_ge(s["acs_ready"], 1)
            for c in range(NCH):
                dve.wait_ge(s["gt_ps"], c + 1)
                dve.tensor_tensor(gt[:, c, :], ps_a[1][:, c * P:(c + 1) * P], tri[:], ALU.mult).then_inc(s["gt_ready"], 1)
            for c in range(NCH):
                dve.wait_ge(s["rep_ps"], c + 1)
                link(dve.tensor_tensor(seg[:, c], ps_r[:], bc(acs[:, c, :], 2, P), ALU.subtract))
                dve.tensor_scalar(seg[:, c], seg[:, c], 0.0, None, ALU.min).then_inc(s["seg_sub"], 1)
                if c == 0:
                    dve.tensor_tensor(dst[:], ps_r[:, :, P - 1], acs[:, 0, :], ALU.subtract).then_inc(s["dst_sub"], 1)
                for i in range(2):
                    dve.wait_ge(s["xt_ps"], 2 * c + i + 1)
                    part = slice(i * DM, (i + 1) * DM)
                    dve.tensor_tensor(xdt[:, c, part].rearrange("p (h e) -> p h e", e=HP), ps_a[2 + i][:].rearrange("p (h e) -> p h e", e=HP),
                                      bc(keep.dt[:, c, i * NH // 2:(i + 1) * NH // 2], 2, HP), ALU.mult).then_inc(s["xdt_ready"], 1)
                dve.wait_ge(s["seg_exp"], c + 1)
                dve.wait_ge(s["gt_ready"], c + 1)
                dve.tensor_tensor(seg[:, c], seg[:, c], bc(gt[:, c, :], 1, NH), ALU.mult).then_inc(s["wts_ready"], 1)
                if c == 0:
                    dve.wait_ge(s["cbx"], 1)
                    dve.tensor_copy(bt[:], ps_a[1][:, 2 * P:3 * P]).then_inc(s["bt_ready"], 1)
                    dve.wait_ge(s["dst_ready"], 1)
                    dve.wait_ge(s["xdt_ready"], 2)
                    dve.tensor_tensor(xdd[:].rearrange("p (h e) -> p h e", e=HP), xdt[:, 0, :].rearrange("p (h e) -> p h e", e=HP),
                                      bc(dst[:], 2, HP), ALU.mult).then_inc(s["xdd_ready"], 1)
            dve.wait_ge(s["eA_ready"], 1)
            dve.tensor_tensor(eA[:], eA[:], bc(keep.xc[:, CTT * LQ + CH:(CTT + 1) * LQ], 1, NH), ALU.mult).then_inc(s["cp_ready"], 1)
            for k in range(CT):
                dve.wait_ge(s["y_ps"], k + 1)
                xs = keep.xc[:, k * LQ:(k + 1) * LQ]
                dve.scalar_tensor_tensor(yg[:, k, :], xs, dsk[:, k:k + 1], ps_a[2 + k % 2][:, 0:LQ], ALU.mult, ALU.add).then_inc(s["yx"], 1)
                dve.wait_ge(s["yx"], k + 1)
                dve.tensor_tensor(yg[:, k, :], yg[:, k, :], keep.zs[:, k * LQ:(k + 1) * LQ], ALU.mult).then_inc(s["yz"], 1)
                dve.wait_ge(s["ysq_ready"], k + 1)
                dve.tensor_scalar(yg[:, k, :], yg[:, k, :], nw[:, k:k + 1], None, ALU.mult).then_inc(s["yn_ready"], 1)
            dve.wait_ge(s["rs_ps"], 1)
            dve.tensor_scalar(rs[:], ps_a[0][:, 0:QT], 1.0 / DI, 1e-5, ALU.mult, ALU.add).then_inc(s["rs_var"], 1)
            dve.wait_ge(s["rs_ready"], 1)
            for t in range(QT):
                dve.wait_ge(s["out_ps"], t + 1)
                dve.scalar_tensor_tensor(keep.x1[:, t, :], ps_a[2 + t][:], rs[:, t:t + 1], keep.x1[:, t, :], ALU.mult, ALU.add).then_inc(keep.x2_ready, 1)

        @block.tensor
        def _(pe):
            cols = lambda k, c: slice(k * LQ + c * CH, k * LQ + (c + 1) * CH)
            for c in range(NCH):
                pe.matmul(ps_a[1][:, c * P:(c + 1) * P], keep.xc[:, cols(BT, c)], keep.xc[:, cols(CTT, c)], start=True, stop=True).then_inc(s["gt_ps"], 1)
            pe.wait_ge(s["tri_ready"], 1)
            pe.wait_ge(s["dA_ready"], 1)
            for c in range(NCH):
                last = pe.matmul(ps_a[0][:, c * NH:(c + 1) * NH], tri[:], dA[:, c, :], start=True, stop=True)
            last.then_inc(s["acs_ps"], 1)

            def turn_x(c):
                if c:
                    pe.wait_ge(s["xdt_ready"], 2)
                for k in range(CT):
                    last = pe.transpose(ps_a[2 + k // 4][:, (k % 4) * P:(k % 4 + 1) * P], keep.xc[:, cols(k, c)], keep.ident[:])
                    if k % 4 == 3:
                        last.then_inc(s["xt_ps"], 1)

            for c in range(NCH):
                pe.wait_ge(s["dAU_ready"], c + 1)
                if c:
                    pe.wait_ge(s["seg_sub"], 1)
                    pe.wait_ge(s["dst_sub"], 1)
                for i in range(NH // 4):
                    last = pe.matmul(ps_r[:, 4 * i:4 * i + 4, :], ones[:], dAU[:, c, 4 * i:4 * i + 4, :], start=True, stop=True)
                last.then_inc(s["rep_ps"], 1)
                turn_x(c)
                if c == 0:
                    pe.wait_ge(s["gt_ready"], NCH)
                    pe.transpose(ps_a[1][:, 2 * P:3 * P], keep.xc[:, cols(BT, 0)], keep.ident[:]).then_inc(s["cbx"], 1)
            pe.wait_ge(s["bt_ready"], 1)
            pe.wait_ge(s["acs_ready"], 1)
            pe.wait_ge(s["xdd_ready"], 1)
            for i in range(2):
                last = pe.matmul(ps_a[i][:], bt[:], xdd[:, i * DM:(i + 1) * DM], start=True, stop=True)
            last.then_inc(s["st_ps"], 1)
            pe.wait_ge(s["wo_in"], 16)
            pe.wait_ge(s["eA_ready"], 1)
            pe.wait_ge(s["seg_sub"], NCH)
            for k in range(CT):
                if k >= 4:
                    pe.wait_ge(s["woT_ready"], k - 3)
                for m in range(MC):
                    last = pe.transpose(ps_r[:, (k % 4) * 4 + m, :], wo[:, m, k * P:(k + 1) * P], keep.ident[:])
                last.then_inc(s["woT_ps"], 1)
            pe.wait_ge(s["wts_ready"], NCH)
            pe.wait_ge(s["xdt_ready"], 4)
            pe.wait_ge(s["st_ready"], 2)
            pe.wait_ge(s["cp_ready"], 1)
            for k in range(CT):
                if k >= 2:
                    pe.wait_ge(s["yx"], k - 1)
                for c in range(NCH):
                    for hh in range(2):
                        h = 2 * k + hh
                        dst_ps = ps_a[2 + k % 2][hh * HP:(hh + 1) * HP, c * CH:(c + 1) * CH]
                        hs = slice(h * HP, (h + 1) * HP)
                        last = pe.matmul(dst_ps, xdt[:, c, hs], seg[:, c, h, :], start=True, stop=c == 0)
                        if c:
                            last = pe.matmul(dst_ps, st[:, hs], eA[:, h, :], start=False, stop=True)
                last.then_inc(s["y_ps"], 1)
            for t in range(QT):
                for k in range(CT):
                    pe.wait_ge(s["ysq_ready"], k + 1)
                    last = pe.matmul(ps_a[0][:, t:t + 1], ysq[:, k, t * P:(t + 1) * P], ones[:, 0:1], start=k == 0, stop=k == CT - 1)
            last.then_inc(s["rs_ps"], 1)
            pe.wait_ge(s["yn_ready"], CT)
            pe.wait_ge(s["woT_ready"], CT)
            for t in range(QT):
                for k in range(CT):
                    last = pe.matmul(ps_a[2 + t][:], yg[:, k, t * P:(t + 1) * P], woT[:, k, :], start=k == 0, stop=k == CT - 1)
                last.then_inc(s["out_ps"], 1)


E = 64
FG = 8
GS = E // FG
TOPK = 8
FI = 352
FT = -(-FI // P)
NEG_INF = -1e9


def route(nc, io, keep):
    with ExitStack() as ctx:
        p = Pools(nc, ctx)
        stat = p.sb("h_stat", [P, QT, 6])
        aggr = p.sb("h_aggr", [P, QT, 2])
        hr = p.sb("h_rstd", [P, QT])
        hn = p.sb("h_norm", [P, QT, DM])
        mhalf = p.sb("minus_half5", [P, QT])
        gw = p.sb("gate_rows", [E, DM])
        gwT = p.sb("gate_T", [P, MC, E])
        mu = p.sb("mask_up_rows", [P, MC, FG, GS])
        idx = p.sb("expert_index", [E, E], I32)
        idf = p.sb("expert_index_f", [E, E])
        idn = p.sb("expert_index_wrapped", [E, E])
        row = p.sb("row_number", [E, 1], I32)
        rowf = p.sb("row_number_f", [E, 1])
        pick = p.sb("pick", [E, E])
        sc = p.sb("router_scores", [P, QT, E])
        mxs = p.sb("router_max", [P, QT])
        sm = p.sb("router_sum", [P, QT])
        top = p.sb("router_top", [P, QT, TOPK])
        rest = p.sb("router_rest", [P, QT, E])
        we = p.sb("expert_weights", [P, QT, E])
        weT = p.sb("expert_weights_T", [E, LQ])
        flat = p.sb("grouped_weights", [P, QT * FG, GS])
        soft = p.sb("group_softmax", [P, QT * FG, GS])
        gm = p.sb("group_max", [P, QT * FG])
        gsum = p.sb("group_sum", [P, QT * FG])
        gmask = p.sb("group_rows", [E, FG])
        softT = p.sb("group_softmax_T", [E, LQ])
        ps_h = [p.ps(f"ps_h{i}", [P, DM]) for i in range(2)]
        ps_g = [p.ps(f"ps_gt{i}", [P, DM]) for i in range(4)]
        names = ("gw_in mu_in idx_in pool_c masks row_ready var_h rstd_h hn_ready hT_ps hT_ready gwT_ps gwT_ready lg_ps lgm_ready "
                 "exp_ready we_ready weT_ps weT_ready pick_ready flat_ps fsub_ready fexp_ready soft_ready softT_ps softT_ready muT_ps "
                 "softz_ready zero_ready")
        s = {n: p.sem("r_" + n) for n in names.split()}
        block = ctx.enter_context(nc.Block())

        @block.sync
        def _(sp):
            sp.dma_start(gw[:], io["L0_ffn_gate_w"]).then_inc(s["gw_in"], 16)
            for c in range(MC):
                sp.dma_start(mu[:, c], io["L0_ffn_mask_up_w"][:, c * P:(c + 1) * P, :].rearrange("g p i -> p g i")).then_inc(s["mu_in"], 16)
            sp.dma_start(idx[:], io["L0_ffn_inv_map"].rearrange("a b -> (a b)").partition_broadcast(E)).then_inc(s["idx_in"], 16)

        @block.gpsimd
        def _(pool):
            link = p.chain(pool, "r_pool_chain")
            pool.memset(mhalf[:], -0.5).then_inc(s["pool_c"], 1)
            pool.wait_ge(s["pool_c"], 1)
            pool.wait_ge(s["var_h"], 1)
            pool.tensor_tensor(hr[:], hr[:], mhalf[:], ALU.pow).then_inc(s["rstd_h"], 1)
            link(pool.iota(row[:], pattern=[[0, 1]], base=0, channel_multiplier=1))
            pool.tensor_copy(rowf[:], row[:]).then_inc(s["row_ready"], 1)
            pool.wait_ge(s["row_ready"], 1)
            link(pool.memset(gmask[:], 1.0))
            link(pool.affine_select(out=gmask[:], in_=gmask[:], compare_op=ALU.is_ge, fill=0.0, base=0,
                                    pattern=[[-GS, FG]], channel_multiplier=1))
            pool.affine_select(out=gmask[:], in_=gmask[:], compare_op=ALU.is_ge, fill=0.0, base=GS - 1,
                               pattern=[[GS, FG]], channel_multiplier=-1).then_inc(s["masks"], 1)
            pool.wait_ge(s["masks"], 1)
            link(pool.memset(keep.softz[E:, :], 0.0))
            pool.memset(keep.muT[E:, :], 0.0).then_inc(s["zero_ready"], 1)

        @block.scalar
        def _(act):
            act.wait_ge(s["gwT_ps"], 1)
            act.activation(gwT[:], ps_g[0][:, 0:MC * E].rearrange("p (c e) -> p c e", c=MC), ACT.Copy).then_inc(s["gwT_ready"], 1)
            for i in range(2):
                act.wait_ge(s["hT_ps"], i + 1)
                act.activation(keep.hT[:, 2 * i:2 * i + 2, :], ps_h[i][:].rearrange("p (c l) -> p c l", c=2), ACT.Copy).then_inc(s["hT_ready"], 1)
            act.wait_ge(s["muT_ps"], 1)
            act.activation(keep.muT[0:E, :], ps_g[3][0:E, :], ACT.Copy).then_inc(keep.muT_ready, 1)
            act.wait_ge(s["lgm_ready"], 1)
            act.activation(sc[:], sc[:], ACT.Exp).then_inc(s["exp_ready"], 1)
            act.wait_ge(s["weT_ps"], 1)
            act.activation(weT[:], ps_g[0][0:E, 0:LQ], ACT.Copy).then_inc(s["weT_ready"], 1)
            act.wait_ge(s["fsub_ready"], 1)
            act.activation(soft[:], soft[:], ACT.Exp).then_inc(s["fexp_ready"], 1)

        @block.vector
        def _(dve):
            link = p.chain(dve, "r_dve_chain")
            dve.wait_ge(keep.x2_ready, QT)
            for t in range(QT):
                link(dve.bn_stats(stat[:, t, :], keep.x1[:, t, :]))
                link(dve.bn_aggr(aggr[:, t, :], stat[:, t, :]))
            dve.tensor_scalar(hr[:], aggr[:, :, 1], 1e-5, None, ALU.add).then_inc(s["var_h"], 1)
            dve.wait_ge(s["rstd_h"], 1)
            for t in range(QT):
                dve.tensor_scalar(hn[:, t, :], keep.x1[:, t, :], aggr[:, t, 0:1], hr[:, t:t + 1], ALU.subtract, ALU.mult).then_inc(s["hn_ready"], 1)
            dve.wait_ge(s["idx_in"], 16)
            dve.wait_ge(s["row_ready"], 1)
            link(dve.tensor_copy(idf[:], idx[:]))
            link(dve.tensor_scalar(idn[:], idf[:], float(E), rowf[:, 0:1], ALU.add, ALU.is_equal))
            link(dve.tensor_scalar(idf[:], idf[:], rowf[:, 0:1], None, ALU.is_equal))
            dve.tensor_tensor(pick[:], idf[:], idn[:], ALU.add).then_inc(s["pick_ready"], 1)
            dve.wait_ge(s["lg_ps"], 1)
            lg = ps_g[1][:, 0:QT * E].rearrange("p (t e) -> p t e", t=QT)
            link(dve.tensor_reduce(mxs[:], lg, AX.X, ALU.max))
            dve.tensor_tensor(sc[:], lg, bc(mxs[:], 2, E), ALU.subtract).then_inc(s["lgm_ready"], 1)
            dve.wait_ge(s["exp_ready"], 1)
            link(dve.tensor_reduce(sm[:], sc[:], AX.X, ALU.add))
            link(dve.reciprocal(sm[:], sm[:]))
            link(dve.tensor_tensor(sc[:], sc[:], bc(sm[:], 2, E), ALU.mult))
            for t in range(QT):
                link(dve.max(top[:, t, :], sc[:, t, :]))
                link(dve.match_replace(rest[:, t, :], top[:, t, :], sc[:, t, :], 0.0))
            dve.tensor_tensor(we[:], sc[:], rest[:], ALU.subtract).then_inc(s["we_ready"], 1)
            dve.wait_ge(s["flat_ps"], 1)
            f3 = ps_g[2][:, 0:QT * E].rearrange("p (g i) -> p g i", i=GS)
            dve.tensor_reduce(keep.scal[:], f3, AX.X, ALU.add).then_inc(keep.scal_ready, 1)
            link(dve.tensor_copy(flat[:], f3))
            link(dve.tensor_scalar(soft[:], flat[:], 0.0, NEG_INF, ALU.is_equal, ALU.mult))
            link(dve.tensor_tensor(soft[:], soft[:], flat[:], ALU.add))
            link(dve.tensor_reduce(gm[:], soft[:], AX.X, ALU.max))
            dve.tensor_tensor(soft[:], soft[:], bc(gm[:], 2, GS), ALU.subtract).then_inc(s["fsub_ready"], 1)
            dve.wait_ge(s["fexp_ready"], 1)
            link(dve.tensor_reduce(gsum[:], soft[:], AX.X, ALU.add))
            link(dve.reciprocal(gsum[:], gsum[:]))
            dve.tensor_tensor(soft[:], soft[:], bc(gsum[:], 2, GS), ALU.mult).then_inc(s["soft_ready"], 1)
            dve.wait_ge(s["softT_ps"], 1)
            dve.wait_ge(s["masks"], 1)
            dve.tensor_copy(softT[:], ps_g[0][0:E, LQ:]).then_inc(s["softT_ready"], 1)
            dve.wait_ge(s["softT_ready"], 1)
            for g in range(FG):
                dve.tensor_scalar(keep.softz[0:E, g * LQ:(g + 1) * LQ], softT[:], gmask[:, g:g + 1], None, ALU.mult).then_inc(keep.softz_ready, 1)
            dve.wait_ge(s["zero_ready"], 1)

        @block.tensor
        def _(pe):
            pe.wait_ge(s["gw_in"], 16)
            for c in range(MC):
                last = pe.transpose(ps_g[0][:, c * E:(c + 1) * E], gw[:, c * P:(c + 1) * P], keep.ident[0:E, 0:E])
            last.then_inc(s["gwT_ps"], 1)
            pe.wait_ge(s["mu_in"], 16 * MC)
            for c in range(MC):
                last = pe.transpose(ps_g[3][0:E, c * P:(c + 1) * P], mu[:, c].rearrange("p g i -> p (g i)"), keep.ident[:])
            last.then_inc(s["muT_ps"], 1)
            pe.wait_ge(s["hn_ready"], QT)
            for c in range(MC):
                for t in range(QT):
                    last = pe.transpose(ps_h[c // 2][:, (c % 2) * LQ + t * P:(c % 2) * LQ + (t + 1) * P],
                                        hn[:, t, c * P:(c + 1) * P], keep.ident[:])
                if c % 2:
                    last.then_inc(s["hT_ps"], 1)
            pe.wait_ge(s["hT_ready"], 2)
            pe.wait_ge(s["gwT_ready"], 1)
            for t in range(QT):
                for c in range(MC):
                    last = pe.matmul(ps_g[1][:, t * E:(t + 1) * E], keep.hT[:, c, t * P:(t + 1) * P], gwT[:, c, :], start=c == 0, stop=c == MC - 1)
            last.then_inc(s["lg_ps"], 1)
            pe.wait_ge(s["we_ready"], 1)
            for t in range(QT):
                last = pe.transpose(ps_g[0][0:E, t * P:(t + 1) * P], we[:, t, :], keep.ident[:])
            last.then_inc(s["weT_ps"], 1)
            pe.wait_ge(s["weT_ready"], 1)
            pe.wait_ge(s["pick_ready"], 1)
            for t in range(QT):
                last = pe.matmul(ps_g[2][:, t * E:(t + 1) * E], weT[:, t * P:(t + 1) * P], pick[:], start=True, stop=True)
            last.then_inc(s["flat_ps"], 1)
            pe.wait_ge(s["soft_ready"], 1)
            for t in range(QT):
                src = soft[:].rearrange("p (t g) i -> p t (g i)", t=QT)[:, t, :]
                last = pe.transpose(ps_g[0][0:E, LQ + t * P:LQ + (t + 1) * P], src, keep.ident[:])
            last.then_inc(s["softT_ps"], 1)


def experts(nc, io, keep):
    with ExitStack() as ctx:
        p = Pools(nc, ctx)
        two = lambda name, shape, dt=F32: [p.sb(f"{name}{i}", shape, dt) for i in range(2)]
        wg, wu, wd = two("gate_rows_", [P, FT, DM]), two("up_rows_", [P, FT, DM]), two("down_rows_", [P, MC, FI])
        gh, gl = two("gate_T_hi", [P, MC, FI], F32R), two("gate_T_lo", [P, MC, FI], F32R)
        uh, ul = two("up_T_hi", [P, MC, FI], F32R), two("up_T_lo", [P, MC, FI], F32R)
        dh, dl = two("down_T_hi", [P, FT, DM], F32R), two("down_T_lo", [P, FT, DM], F32R)
        xg = p.sb("x_group", [P, MC, LQ])
        xh = p.sb("x_group_hi", [P, MC, LQ], F32R)
        xl = p.sb("x_group_lo", [P, MC, LQ], F32R)
        sg = p.sb("gate_silu", [P, FT, LQ])
        ac = p.sb("act", [P, FT, LQ])
        ah = p.sb("act_hi", [P, FT, LQ], F32R)
        al = p.sb("act_lo", [P, FT, LQ], F32R)
        ps_t = [p.ps(f"ps_wt_{i}", [P, DM]) for i in range(2)]
        ps_x = p.ps("ps_xg", [P, MC, LQ])
        ps_gu = [p.ps(f"ps_gu{i}", [P, 2 * LQ]) for i in range(2)]
        ps_y = [p.ps(f"ps_y{i}", [P, DM]) for i in range(2)]
        names = "wt_ps wt_hi wt_lo xg_ps xg_ready xh_ready xl_ready gu_ps sg_ready ac_ready ah_ready al_ready y_ps y_read"
        s = {n: p.sem("f_" + n) for n in names.split()}
        w_in = {(n, j): p.sem(f"{n}_in{j}") for n in "gud" for j in range(2)}
        block = ctx.enter_context(nc.Block())
        rows = [min(P, FI - i * P) for i in range(FT)]
        NT = 2 * MC + FT

        def banks(j):
            for hi, lo in ((gh[j], gl[j]), (uh[j], ul[j])):
                for c in range(MC):
                    yield P, FI, hi[:, c, :], lo[:, c, :]
            for i in range(FT):
                yield rows[i], DM, dh[j][0:rows[i], i, :], dl[j][0:rows[i], i, :]

        @block.sync
        def _(sp):
            def load(g, j):
                full = (FT - 1) * P
                for n, w, t in (("g", io["L0_ffn_gate_proj_w"], wg[j]), ("u", io["L0_ffn_up_proj_w"], wu[j])):
                    sp.dma_start(t[:, 0:FT - 1, :], w[bass.ds(g, 1), 0:full, :].rearrange("o (i p) d -> p (o i) d", p=P)).then_inc(w_in[n, j], 16)
                    sp.dma_start(t[0:rows[-1], FT - 1, :], w[bass.ds(g, 1), full:, :].rearrange("o p d -> p (o d)")).then_inc(w_in[n, j], 16)
                sp.dma_start(wd[j][:], io["L0_ffn_down_proj_w"][bass.ds(g, 1), :, :].rearrange("o (c p) i -> p (o c) i", p=P)).then_inc(w_in["d", j], 16)

            load(0, 0)
            load(1, 1)
            with sp.Fori(0, FG // 2 - 1) as i:
                for j in range(2):
                    sp.wait_ge(s["wt_ps"], (2 * i + j + 1) * NT)
                    load(2 * i + j + 2, j)

        @block.scalar
        def _(act):
            def high(g, j):
                for n, (r, w, hi, lo) in enumerate(banks(j)):
                    act.wait_ge(s["wt_ps"], g * NT + n + 1)
                    act.activation(hi, ps_t[(j * NT + n) % 2][0:r, 0:w], ACT.Copy).then_inc(s["wt_hi"], 1)
                    yield

            def silu(g, j):
                for i in range(FT):
                    act.wait_ge(s["gu_ps"], g * FT + i + 1)
                    act.activation(sg[0:rows[i], i, :], ps_gu[(j * FT + i) % 2][0:rows[i], 0:LQ], ACT.Silu).then_inc(s["sg_ready"], 1)

            def turn(g, j, more):
                ahead = high(g + 1, 1 - j) if more else iter(())
                for n in range(MC):
                    next(ahead, None)
                for i in range(FT):
                    act.wait_ge(s["gu_ps"], g * FT + i + 1)
                    act.activation(sg[0:rows[i], i, :], ps_gu[(j * FT + i) % 2][0:rows[i], 0:LQ], ACT.Silu).then_inc(s["sg_ready"], 1)
                    for n in range(2):
                        next(ahead, None)
                for _ in ahead:
                    pass

            for _ in high(0, 0):
                pass
            with act.Fori(0, FG // 2 - 1) as i:
                for j in range(2):
                    turn(2 * i + j, j, True)
            turn(FG - 2, 0, True)
            turn(FG - 1, 1, False)

        @block.vector
        def _(dve):
            def low(g, j):
                for n, (r, w, hi, lo) in enumerate(banks(j)):
                    dve.wait_ge(s["wt_hi"], g * NT + n + 1)
                    dve.tensor_tensor(lo, ps_t[(j * NT + n) % 2][0:r, 0:w], two_part(hi), ALU.subtract).then_inc(s["wt_lo"], 1)
                    yield

            def inputs(g):
                dve.wait_ge(s["xg_ps"], g + 1)
                dve.tensor_tensor(xg[:], ps_x[:], keep.hT[:], ALU.add).then_inc(s["xg_ready"], 1)
                dve.wait_ge(s["xg_ready"], g + 1)
                dve.tensor_copy(xh[:], xg[:]).then_inc(s["xh_ready"], 1)
                dve.wait_ge(s["xh_ready"], g + 1)
                dve.tensor_tensor(xl[:], xg[:], two_part(xh[:]), ALU.subtract).then_inc(s["xl_ready"], 1)

            def turn(g, j, more):
                inputs(g)
                ahead = low(g + 1, 1 - j) if more else iter(())
                for n in range(MC):
                    next(ahead, None)
                for i in range(FT):
                    r = rows[i]
                    dve.wait_ge(s["sg_ready"], g * FT + i + 1)
                    dve.tensor_tensor(ac[0:r, i, :], sg[0:r, i, :], ps_gu[(j * FT + i) % 2][0:r, LQ:], ALU.mult).then_inc(s["ac_ready"], 1)
                    dve.wait_ge(s["ac_ready"], g * FT + i + 1)
                    dve.tensor_copy(ah[0:r, i, :], ac[0:r, i, :]).then_inc(s["ah_ready"], 1)
                    dve.wait_ge(s["ah_ready"], g * FT + i + 1)
                    dve.tensor_tensor(al[0:r, i, :], ac[0:r, i, :], two_part(ah[0:r, i, :]), ALU.subtract).then_inc(s["al_ready"], 1)
                    for n in range(2):
                        next(ahead, None)
                for _ in ahead:
                    pass
                for t in range(QT):
                    dve.wait_ge(s["y_ps"], g * QT + t + 1)
                    weight = keep.scal[:, bass.ds(g + t * FG, 1)]
                    dve.scalar_tensor_tensor(keep.x1[:, t, :], ps_y[t][:], weight, keep.x1[:, t, :], ALU.mult, ALU.add).then_inc(s["y_read"], 1)

            dve.wait_ge(keep.scal_ready, 1)
            for _ in low(0, 0):
                pass
            with dve.Fori(0, FG // 2 - 1) as i:
                for j in range(2):
                    turn(2 * i + j, j, True)
            turn(FG - 2, 0, True)
            turn(FG - 1, 1, False)

        @block.tensor
        def _(pe):
            def turned(g, j):
                n = 0

                def bank(width, parts, height):
                    nonlocal n
                    k = j * NT + n
                    if not (isinstance(g, int) and g * NT + n < 2):
                        pe.wait_ge(s["wt_lo"], g * NT + n - 1)
                    for at, src, size in parts:
                        last = pe.transpose(ps_t[k % 2][0:height, at:at + size], src, keep.ident[0:size, 0:size])
                    last.then_inc(s["wt_ps"], 1)
                    n += 1

                for name, w in (("g", wg[j]), ("u", wu[j])):
                    pe.wait_ge(w_in[name, j], 32 * turn_of(g, j) + 32)
                    for c in range(MC):
                        bank(FI, [(i * P, w[0:rows[i], i, c * P:(c + 1) * P], rows[i]) for i in range(FT)], P)
                        yield
                pe.wait_ge(w_in["d", j], 16 * turn_of(g, j) + 16)
                for i in range(FT):
                    bank(DM, [(c * P, wd[j][:, c, i * P:i * P + rows[i]], P) for c in range(MC)], rows[i])
                    yield

            def turn_of(g, j):
                return turn_index[0]

            turn_index = [0]

            def inputs(g):
                pe.wait_ge(keep.softz_ready, FG)
                if not (isinstance(g, int) and g == 0):
                    pe.wait_ge(s["xg_ready"], g)
                for c in range(MC):
                    last = pe.matmul(ps_x[:, c, :], keep.muT[:, c * P:(c + 1) * P], keep.softz[:, bass.ts(g, LQ)], start=True, stop=True)
                last.then_inc(s["xg_ps"], 1)

            def turn(g, j, i2, more):
                turn_index[0] = i2 + j
                ahead = turned(g + 1, 1 - j) if more else iter(())
                for n in range(2):
                    next(ahead, None)
                pe.wait_ge(s["xl_ready"], g + 1)
                pe.wait_ge(s["wt_lo"], g * NT + NT)
                for i in range(FT):
                    if not (isinstance(g, int) and g * FT + i < 2):
                        pe.wait_ge(s["ac_ready"], g * FT + i - 1)
                    at = slice(i * P, i * P + rows[i])
                    for half, (hi, lo) in enumerate(((gh[j], gl[j]), (uh[j], ul[j]))):
                        every = [(a, b, c) for a, b in ((hi, xh), (lo, xh), (hi, xl)) for c in range(MC)]
                        for n, (a, b, c) in enumerate(every):
                            last = pe.matmul(ps_gu[(j * FT + i) % 2][0:rows[i], half * LQ:(half + 1) * LQ], a[:, c, at], b[:, c, :],
                                             start=n == 0, stop=n == len(every) - 1)
                    last.then_inc(s["gu_ps"], 1)
                    for n in range(2):
                        next(ahead, None)
                if more:
                    inputs(g + 1)
                for _ in ahead:
                    pass
                pe.wait_ge(s["al_ready"], g * FT + FT)
                for t in range(QT):
                    if not (isinstance(g, int) and g == 0):
                        pe.wait_ge(s["y_read"], (g - 1) * QT + t + 1)
                    every = [(a, b, i) for a, b in ((ah, dh[j]), (al, dh[j]), (ah, dl[j])) for i in range(FT)]
                    for n, (a, b, i) in enumerate(every):
                        last = pe.matmul(ps_y[t][:], a[0:rows[i], i, t * P:(t + 1) * P], b[0:rows[i], i, :], start=n == 0, stop=n == len(every) - 1)
                    last.then_inc(s["y_ps"], 1)

            pe.wait_ge(keep.muT_ready, 1)
            inputs(0)
            for _ in turned(0, 0):
                pass
            turn(0, 0, 0, True)
            turn(1, 1, 0, True)
            with pe.Fori(1, FG // 2 - 1) as i:
                for j in range(2):
                    turn(2 * i + j, j, i, True)
            turn(FG - 2, 0, FG // 2 - 1, True)
            turn(FG - 1, 1, FG // 2 - 1, False)
            pe.wait_ge(s["y_read"], FG * QT)


class Keep:
    pass


def declare_experts(f, keep):
    keep.hT = f.sb("h_T", [P, MC, LQ])
    keep.muT = f.sb("mask_up_T", [P, DM])
    keep.softz = f.sb("group_softmax_rows", [P, FG * LQ])
    keep.scal = f.sb("group_weight", [P, QT * FG])
    keep.muT_ready, keep.scal_ready, keep.softz_ready = f.sem("muT_ready"), f.sem("scal_ready"), f.sem("softz_ready")


def build_program(nc, io, out):
    with ExitStack() as ctx:
        p = Pools(nc, ctx)
        keep = Keep()
        keep.ident = p.sb("ident", [P, P])
        keep.x1 = p.sb("x1", [P, QT, DM])
        keep.x1_ready, keep.kn_in, keep.dca_done = p.sem("x1_ready"), p.sem("kn_in"), p.sem("dca_done")
        keep.dt_ready, keep.x2_ready = p.sem("dt_ready"), p.sem("x2_ready")
        q_scr = nc.dram_tensor("q_scratch", [3 * HD, H, LQ], F32).ap()
        w_scr = nc.dram_tensor("w_scratch", [P, 2, KC, 2 * DM], F32).ap()
        with ExitStack() as actx:
            a = Pools(nc, actx)
            keep.eps = a.sb("eps", [P, 1])
            keep.fold_num = a.sb("fold_num", [P, HD])
            keep.fold_den = a.sb("fold_den", [P, HD])
            keep.bkv = a.sb("b_kv", [P, 2 * DM])
            keep.knw = a.sb("kn_w", [P, 1])
            keep.knb = a.sb("kn_b", [P, 1])
            keep.ctxT = a.sb("attn_T", [P, NG * LQ])
            keep.dcaT = a.sb("dca_T", [P, NG, LQ])
            with ExitStack() as cctx:
                c = Pools(nc, cctx)
                keep.cTh = c.sb("ctx_T_hi", [P, KC, LK], F32R)
                keep.cTl = c.sb("ctx_T_lo", [P, KC, LK], F32R)
                prepare_attention(nc, io, keep, q_scr, w_scr)
                attend(nc, io, keep, q_scr, w_scr)
            project_attention(nc, io, keep)
        with ExitStack() as mctx:
            m = Pools(nc, mctx)
            keep.zs = m.sb("z_gate", [P, CT * LQ])
            keep.xc = m.sb("x_conv", [P, XT * LQ])
            keep.dt = m.sb("dt", [P, QT, NH])
            mixer_projections(nc, io, keep)
            mixer(nc, io, keep)
        with ExitStack() as fctx:
            f = Pools(nc, fctx)
            declare_experts(f, keep)
            route(nc, io, keep)
            experts(nc, io, keep)
        with ExitStack() as ectx:
            done = Pools(nc, ectx).sem("done")
            block = ectx.enter_context(nc.Block())

            @block.sync
            def _(sp):
                sp.dma_start(out.rearrange("o (t p) d -> p (o t) d", p=P), keep.x1[:]).then_inc(done, 16)
                sp.wait_ge(done, 16)


_INS = ["x", "ctx_1024"] + ["L0_xattn_" + n for n in (
    "Wq bq Wk bk Wv bv Wkv_dca bkv_dca qn_w qn_b kn_w kn_b kn_dca_w kn_dca_b Wo bo").split()] + ["L0_attn_" + n for n in (
    "W_in conv_w conv_b dt_bias A_log D norm_weight W_out").split()] + ["L0_ffn_" + n for n in (
    "gate_w mask_up_w gate_proj_w up_proj_w down_proj_w inv_map").split()]


def kernel(**inputs):
    import numpy as np
    from concourse import bacc
    from concourse.bass_utils import run_bass_kernel_spmd

    nc = bacc.Bacc("TRN2", target_bir_lowering=False, num_devices=1)
    arrays = {n: np.ascontiguousarray(inputs[n]) for n in _INS}
    io = {n: nc.dram_tensor(n, a.shape, mybir.dt.from_np(a.dtype), kind="ExternalInput").ap() for n, a in arrays.items()}
    out = nc.dram_tensor("out", (1, LQ, DM), F32, kind="ExternalOutput").ap()
    build_program(nc, io, out)
    r = run_bass_kernel_spmd(nc, [arrays], core_ids=[0])
    return r.results[0]["out"]
```

```python
import concourse.bass as bass
from concourse import mybir
from contextlib import ExitStack
from itertools import islice

F32 = mybir.dt.float32
F32R = mybir.dt.float32r
I32 = mybir.dt.int32
ALU = mybir.AluOpType
ACT = mybir.ActivationFunctionType
AX = mybir.AxisListType

P = 128
LQ = 256
QT = LQ // P
DM = 512
MC = DM // P
LK = 4096
NDCA = 16
KDIM = 256
KC = KDIM // P
H = 16
HD = 32
G = 4
NG = H // G
NB = 8
TB = LK // P // NB
BK = TB * P
KEYS = LK - NDCA
LAST = KEYS - (LK - P)
SCALE = float(HD) ** -0.5


def two_part(t):
    return t.bitcast(F32)


class Pools:

    def __init__(self, nc, ctx):
        self.nc, self.ctx, self.sems = nc, ctx, []
        ctx.callback(self.clear)

    def clear(self):
        if self.sems:
            self.nc.clear_and_free_semaphores(self.sems)
            self.nc.all_engine_barrier()

    def sb(self, name, shape, dt=F32):
        return self.ctx.enter_context(self.nc.sbuf_tensor(name, shape, dt))

    def ps(self, name, shape):
        return self.ctx.enter_context(self.nc.psum_tensor(name, shape, F32))

    def sem(self, name):
        self.sems.append(self.nc.alloc_semaphore(name))
        return self.sems[-1]

    def chain(self, eng, name):
        sem, count = self.sem(name), [0]

        def link(ins):
            count[0] += 1
            ins.then_inc(sem, 1)
            eng.wait_ge(sem, count[0])
        return link


def bc(ap, axis, n):
    ap = ap.unsqueeze(axis)
    shape = list(ap.shape)
    shape[axis] = n
    return ap.to_broadcast(shape)


def load_group_weights(sp, keep, w_scr, b_scr, g):
    sp.dma_start(two_part(keep.wg[:]), w_scr[:, :, :, bass.ts(g, 2 * P)]).then_inc(keep.wg_in, 16)
    sp.dma_start(keep.bg[:], b_scr[:, bass.ts(g, 2 * P)]).then_inc(keep.wg_in, 16)


def load_head_queries(sp, keep, q_scr, g, h):
    sp.dma_start(two_part(keep.qg[0:3 * HD, h, :]), q_scr[:, bass.ds(g * G + h, 1), :].rearrange("p h l -> p (h l)")).then_inc(keep.q_in[h], 16)


RSQRT_STEPS = 10


def rsqrt_step(dve, i, x, y, tmp):
    if i == 0:
        return dve.tensor_scalar(y.bitcast(I32), x.bitcast(I32), -0.5, float(0x5F3759DF), ALU.mult, ALU.add)
    if i % 3 == 1:
        return dve.scalar_tensor_tensor(tmp, y, -0.5, y, ALU.mult, ALU.mult)
    if i % 3 == 2:
        return dve.tensor_tensor(tmp, tmp, x, ALU.mult)
    return dve.scalar_tensor_tensor(y, tmp, 1.5, y, ALU.add, ALU.mult)


def prepare_attention(nc, io, keep, q_scr, w_scr, b_scr, d_scr):
    with ExitStack() as ctx:
        p = Pools(nc, ctx)
        x = keep.x1
        dcaT = keep.ctxT[:].rearrange("p (g l) -> p g l", g=NG)
        xn = p.sb("x_norm", [P, QT, DM])
        xT = p.sb("x_norm_T", [P, MC, LQ])
        stat = p.sb("x_stat", [P, QT, 6])
        aggr = p.sb("x_aggr", [P, QT, 2])
        xr = p.sb("x_rstd", [P, QT])
        mhalf = p.sb("minus_half", [P, 32])
        cin = p.sb("ctx_in", [P, NB, TB, KDIM])
        wkv = p.sb("w_kv", [P, KC, 2 * DM])
        wsp = p.sb("w_kv_parts", [P, 2, KC, 2 * DM], F32R)
        wq = p.sb("w_q", [P, MC, DM])
        bq = p.sb("b_q", [P, DM])
        bkv = p.sb("b_kv", [P, 2 * DM])
        wd = p.sb("w_dca", [P, KC, 2 * DM])
        bd = p.sb("b_dca", [NDCA, 2 * DM])
        qw = p.sb("qn_w", [P, HD])
        qb = p.sb("qn_b", [P, HD])
        dw = p.sb("kn_dca_w", [NDCA, HD])
        db = p.sb("kn_dca_b", [NDCA, HD])
        mean = p.sb("w_mean", [P, MC * H])
        room = keep.vnew[:].rearrange("p t n -> p (t n)")
        q = room[:, QT * H * 3 * HD:].rearrange("p (n d) -> p n d", d=HD)
        qsq = p.sb("q_sq", [P, QT * H, HD])
        qv = p.sb("q_var", [P, QT * H])
        qrs = p.sb("q_rstd", [P, QT * H])
        qtmp = p.sb("q_rstd_tmp", [P, QT * H])
        qs = room[:, 0:QT * H * 3 * HD].rearrange("p (t h e) -> p t h e", t=QT, h=H).bitcast(F32R)
        spare = cin[:].rearrange("p b t c -> p (b t c)")
        qall = spare[0:3 * HD, 0:H * LQ].rearrange("p (h l) -> p h l", h=H).bitcast(F32R)
        pdT = spare[0:G * NDCA, H * LQ:(H + 4) * LQ].rearrange("p (g l) -> p g l", g=NG)
        qT = spare[:, (H + 4) * LQ:(H + 8) * LQ].rearrange("p (g l) -> p g l", g=NG)
        vdb = spare[0:G * NDCA, (H + 8) * LQ:(H + 10) * LQ].rearrange("p (g n) -> p g n", g=NG)
        yd = p.sb("y_dca", [NDCA, KDIM])
        ydT = p.sb("y_dca_T", [P, KC, NDCA])
        kd = p.sb("kv_dca", [NDCA, 2 * DM])
        kdsq = p.sb("k_dca_sq", [NDCA, H, HD])
        kdv = p.sb("k_dca_var", [NDCA, H])
        kdb = p.sb("k_dca_blocks", [P, NG, G * NDCA])
        sd = p.sb("s_dca", [P, QT * H, NDCA])
        sm = p.sb("s_dca_max", [P, QT * H])
        ssum = p.sb("s_dca_sum", [P, QT * H])
        mkd = p.sb("mask_k_dca", [P, G, NDCA])
        mvd = p.sb("mask_v_dca", [G * NDCA, G, HD])
        rep = p.sb("repeat_dca", [NDCA, G, NDCA])
        psc = [p.ps(f"ps_ctx{i}", [P, KC, BK]) for i in range(2)]
        psa = [p.ps(f"ps_a{i}", [P, DM]) for i in range(2)]
        psb = [p.ps(f"ps_b{i}", [P, DM]) for i in range(2)]

        x_in, yd_in, mask_done = p.sem("x_in_"), p.sem("yd_in"), p.sem("masks_done")
        ctx_in = [p.sem(f"ctx_in{b}") for b in range(NB)]
        wkv_in, wq_in, wd_in, par_in = p.sem("wkv_in"), p.sem("wq_in"), p.sem("wd_in"), p.sem("par_in")
        cT_ready, chi_ready, clo_ready = p.sem("cT_ready"), p.sem("chi_ready"), p.sem("clo_ready")
        var_ready, rstd_ready = p.sem("var_ready"), p.sem("rstd_ready")
        xn_ready, qh_ready, xT_ps, xT_ready = p.sem("xn_ready"), p.sem("qh_ready"), p.sem("xT_ps"), p.sem("xT_ready")
        wkc_ready, wsh_ready, ydT_ps, q_ps, qc_ready, qsq_ready = p.sem("wkc_ready"), p.sem("wsh_ready"), p.sem("ydT_ps"), p.sem("q_ps"), p.sem("qc_ready"), p.sem("qsq_ready")
        qn_ready, q_ready, qst_ps, qst_ready, qT_ps, qT_ready = (p.sem(n) for n in ("qn_ready", "q_ready", "qst_ps", "qst_ready", "qT_ps", "qT_ready"))
        wsp_ready, scr_out, q_out = p.sem("wsp_ready"), p.sem("scr_out"), p.sem("q_out")
        yd_ready, kd_ps, kdc_ready, kdsq_ready, kd_ready = (p.sem(n) for n in ("yd_ready", "kd_ps", "kdc_ready", "kdsq_ready", "kd_ready"))
        kdT_ps, vrep_ps, blocks_ready, sd_ps, sdm_ready, sde_ready = (p.sem(n) for n in ("kdT_ps", "vrep_ps", "blocks_ready", "sd_ps", "sdm_ready", "sde_ready"))
        pd_ready, pdT_ps, pdT_ready, cd_ps = (p.sem(n) for n in ("pd_ready", "pdT_ps", "pdT_ready", "cd_ps"))
        block = ctx.enter_context(nc.Block())

        @block.sync
        def _(sp):
            sp.dma_start(x[:], io["x"].rearrange("o (t p) d -> p (o t) d", p=P)).then_inc(x_in, 16)
            sp.dma_start(wq[:], io["L0_xattn_Wq"].rearrange("(c p) n -> p c n", p=P)).then_inc(wq_in, 16)
            sp.dma_start(bq[:], io["L0_xattn_bq"].partition_broadcast(P)).then_inc(wq_in, 16)
            for b in range(NB):
                src = io["ctx_1024"][0, b * BK:(b + 1) * BK, :].rearrange("(t p) c -> p t c", p=P)
                sp.dma_start(cin[:, b], src).then_inc(ctx_in[b], 16)
            sp.wait_ge(wsp_ready, 1)
            sp.dma_start(w_scr, two_part(wsp[:])).then_inc(scr_out, 16)
            sp.dma_start(b_scr, bkv[:]).then_inc(scr_out, 16)
            sp.wait_ge(scr_out, 32)
            load_group_weights(sp, keep, w_scr, b_scr, 0)
            sp.wait_ge(qst_ready, NB)
            sp.dma_start(q_scr, two_part(qall)).then_inc(q_out, 16)
            sp.wait_ge(q_out, 16)
            for h in range(G):
                load_head_queries(sp, keep, q_scr, 0, h)
            sp.wait_ge(keep.dca_done, 2)
            sp.dma_start(d_scr, keep.ctxT[:]).then_inc(keep.d_out, 16)

        @block.scalar
        def _(act):
            w3 = lambda a: a.rearrange("(c p) n -> p c n", p=P)
            act.dma_start(yd[:], io["ctx_1024"][0, LK - NDCA:, :]).then_inc(yd_in, 16)
            act.dma_start(wkv[:, :, 0:DM], w3(io["L0_xattn_Wk"])).then_inc(wkv_in, 16)
            act.dma_start(wkv[:, :, DM:], w3(io["L0_xattn_Wv"])).then_inc(wkv_in, 16)
            act.dma_start(bkv[:, 0:DM], io["L0_xattn_bk"].partition_broadcast(P)).then_inc(wkv_in, 16)
            act.dma_start(bkv[:, DM:], io["L0_xattn_bv"].partition_broadcast(P)).then_inc(wkv_in, 16)
            act.dma_start(wd[:], w3(io["L0_xattn_Wkv_dca"])).then_inc(wd_in, 16)
            act.dma_start(bd[:], io["L0_xattn_bkv_dca"].partition_broadcast(NDCA)).then_inc(wd_in, 16)
            act.dma_start(qw[:], io["L0_xattn_qn_w"].partition_broadcast(P)).then_inc(par_in, 16)
            act.dma_start(qb[:], io["L0_xattn_qn_b"].partition_broadcast(P)).then_inc(par_in, 16)
            act.dma_start(dw[:], io["L0_xattn_kn_dca_w"].partition_broadcast(NDCA)).then_inc(par_in, 16)
            act.dma_start(db[:], io["L0_xattn_kn_dca_b"].partition_broadcast(NDCA)).then_inc(par_in, 16)
            for h in range(G):
                rows = slice(h * HD, (h + 1) * HD)
                act.dma_start(keep.knw[rows, :], io["L0_xattn_kn_w"].unsqueeze(1)).then_inc(keep.kn_in, 16)
                act.dma_start(keep.knb[rows, :], io["L0_xattn_kn_b"].unsqueeze(1)).then_inc(keep.kn_in, 16)
            def high(b):
                act.wait_ge(cT_ready, b + 1)
                act.activation(keep.cTh[:, :, b * BK:(b + 1) * BK], psc[b % 2][:], ACT.Copy).then_inc(chi_ready, 1)

            act.wait_ge(ydT_ps, 1)
            act.activation(ydT[:], psb[0][:, 0:KC * NDCA].rearrange("p (c k) -> p c k", c=KC), ACT.Copy).then_inc(yd_ready, 1)
            for i in range(2):
                act.wait_ge(xT_ps, i + 1)
                act.activation(xT[:, 2 * i:2 * i + 2, :], psa[i][:].rearrange("p (c l) -> p c l", c=2), ACT.Copy).then_inc(xT_ready, 1)
            high(0)
            act.wait_ge(wkc_ready, 1)
            act.activation(wsp[:, 0], wkv[:], ACT.Copy).then_inc(wsh_ready, 1)
            high(1)
            high(2)
            high(3)
            act.wait_ge(qc_ready, 1)
            act.activation(qsq[:], q, ACT.Square).then_inc(qsq_ready, 1)
            high(4)
            high(5)
            act.wait_ge(qn_ready, 1)
            for i in range(2):
                act.activation(qs.rearrange("p t h e -> p (t h) e")[:, :, i * HD:(i + 1) * HD], q, ACT.Copy).then_inc(qh_ready, 1)
            act.wait_ge(kdc_ready, 1)
            act.activation(kdsq[:], kd[:, 0:DM].rearrange("p (h d) -> p h d", d=HD), ACT.Square).then_inc(kdsq_ready, 1)
            high(6)
            high(7)
            for b in range(NB):
                act.wait_ge(qst_ps, b + 1)
                act.activation(qall[:, 2 * b:2 * b + 2, :], psa[b % 2][0:3 * HD, :].rearrange("p (h l) -> p h l", h=2),
                               ACT.Copy).then_inc(qst_ready, 1)
            for i in range(2):
                act.wait_ge(qT_ps, i + 1)
                act.activation(qT[:, 2 * i:2 * i + 2, :], psb[i][:].rearrange("p (c l) -> p c l", c=2), ACT.Copy).then_inc(qT_ready, 1)
            act.wait_ge(sdm_ready, 1)
            act.activation(sd[:], sd[:], ACT.Exp).then_inc(sde_ready, 1)

        @block.gpsimd
        def _(pool):
            link = p.chain(pool, "pool_chain")
            link(pool.memset(keep.ident[:], 0.0))
            link(pool.affine_select(out=keep.ident[:], in_=keep.ident[:], compare_op=ALU.not_equal, fill=1.0, base=0,
                                    pattern=[[-1, P]], channel_multiplier=1))
            pool.memset(mhalf[:], -0.5).then_inc(mask_done, 1)
            pool.wait_ge(mask_done, 1)
            pool.wait_ge(var_ready, 1)
            pool.tensor_tensor(xr[:], xr[:], mhalf[:, 0:QT], ALU.pow).then_inc(rstd_ready, 1)
            link(pool.memset(mkd[:], 1.0))
            link(pool.affine_select(out=mkd[:], in_=mkd[:], compare_op=ALU.is_ge, fill=0.0, base=0,
                                    pattern=[[-HD, G], [0, NDCA]], channel_multiplier=1))
            link(pool.affine_select(out=mkd[:], in_=mkd[:], compare_op=ALU.is_ge, fill=0.0, base=HD - 1,
                                    pattern=[[HD, G], [0, NDCA]], channel_multiplier=-1))
            link(pool.memset(mvd[:], 1.0))
            link(pool.affine_select(out=mvd[:], in_=mvd[:], compare_op=ALU.is_ge, fill=0.0, base=0,
                                    pattern=[[-NDCA, G], [0, HD]], channel_multiplier=1))
            link(pool.affine_select(out=mvd[:], in_=mvd[:], compare_op=ALU.is_ge, fill=0.0, base=NDCA - 1,
                                    pattern=[[NDCA, G], [0, HD]], channel_multiplier=-1))
            link(pool.memset(rep[:], 0.0))
            link(pool.affine_select(out=rep[:], in_=rep[:], compare_op=ALU.not_equal, fill=1.0, base=0,
                                    pattern=[[0, G], [-1, NDCA]], channel_multiplier=1))
            link(pool.memset(keep.fold[:], 0.0))
            for quarter in range(G):
                link(pool.affine_select(out=keep.fold[:], in_=keep.fold[:], compare_op=ALU.not_equal, fill=1.0, base=-quarter * HD,
                                        pattern=[[-1, HD]], channel_multiplier=1))
            pool.memset(keep.eps[:], 0.0).then_inc(mask_done, 1)
            pool.wait_ge(var_ready, 2)
            pool.tensor_tensor(kdv[:], kdv[:], mhalf[0:NDCA, 0:H], ALU.pow).then_inc(rstd_ready, 1)

        @block.vector
        def _(dve):
            link = p.chain(dve, "dve_chain")

            def centre(w, groups, done=None):
                n = w.shape[0]
                link(dve.tensor_reduce(mean[0:n, 0:groups], w, AX.X, ALU.add))
                link(dve.tensor_scalar(mean[0:n, 0:groups], mean[0:n, 0:groups], 1.0 / HD, None, ALU.mult))
                ins = dve.tensor_tensor(w, w, bc(mean[0:n, 0:groups], 2, HD), ALU.subtract)
                if done is None:
                    link(ins)
                else:
                    ins.then_inc(done, 1)
                    dve.wait_ge(done, 1)

            dve.wait_ge(x_in, 16)
            for t in range(QT):
                link(dve.bn_stats(stat[:, t, :], x[:, t, :]))
                link(dve.bn_aggr(aggr[:, t, :], stat[:, t, :]))
            dve.tensor_scalar(xr[:], aggr[:, :, 1], 1e-5, None, ALU.add).then_inc(var_ready, 1)

            def low(b):
                dve.wait_ge(chi_ready, b + 1)
                part = slice(b * BK, (b + 1) * BK)
                dve.tensor_tensor(keep.cTl[:, :, part], psc[b % 2][:], two_part(keep.cTh[:, :, part]), ALU.subtract).then_inc(clo_ready, 1)

            heads = lambda w: w.rearrange("p (h d) -> p h d", d=HD)
            dve.wait_ge(rstd_ready, 1)
            for t in range(QT):
                dve.tensor_scalar(xn[:, t, :], x[:, t, :], aggr[:, t, 0:1], xr[:, t:t + 1], ALU.subtract, ALU.mult).then_inc(xn_ready, 1)
            dve.wait_ge(wkv_in, 64)
            centre(wkv[:].rearrange("p c (h e) -> p (c h) e", e=2 * HD)[:, :, 0:HD], KC * H)
            centre(bkv[:].rearrange("p (h e) -> p h e", e=2 * HD)[:, :, 0:HD], H, wkc_ready)
            low(0)
            low(1)
            low(2)
            dve.wait_ge(wsh_ready, 1)
            dve.tensor_tensor(wsp[:, 1], wkv[:], two_part(wsp[:, 0]), ALU.subtract).then_inc(wsp_ready, 1)
            for t in range(QT):
                dve.wait_ge(q_ps, t + 1)
                link(dve.tensor_tensor(q[:, t * H:(t + 1) * H, :].rearrange("p h d -> p (h d)"), psa[t][:], bq[:], ALU.add))
            centre(q, QT * H, qc_ready)
            low(3)
            dve.wait_ge(qsq_ready, 1)
            link(dve.tensor_reduce(qv[:], qsq[:], AX.X, ALU.add))
            link(dve.tensor_scalar(qv[:], qv[:], 1.0 / HD, 1e-6, ALU.mult, ALU.add))
            for i in range(RSQRT_STEPS):
                link(rsqrt_step(dve, i, qv[:], qrs[:], qtmp[:]))
            low(4)
            dve.wait_ge(par_in, 64)
            link(dve.tensor_scalar(qw[:], qw[:], SCALE, None, ALU.mult))
            link(dve.tensor_scalar(qb[:], qb[:], SCALE, None, ALU.mult))
            link(dve.tensor_tensor(q, q, bc(qrs[:], 2, HD), ALU.mult))
            link(dve.tensor_tensor(q, q, bc(qw[:], 1, QT * H), ALU.mult))
            dve.tensor_tensor(q, q, bc(qb[:], 1, QT * H), ALU.add).then_inc(qn_ready, 1)
            dve.wait_ge(wd_in, 32)
            vb = heads(bd[:, DM:])
            link(dve.tensor_tensor(vb, vb, bkv[0:NDCA, :].rearrange("p (h e) -> p h e", e=2 * HD)[:, :, HD:], ALU.add))
            low(5)
            qs3 = qs.rearrange("p t h e -> p (t h) e")
            dve.wait_ge(qh_ready, 1)
            dve.tensor_tensor(qs3[:, :, 2 * HD:], q, two_part(qs3[:, :, 0:HD]), ALU.subtract).then_inc(q_ready, 1)
            for i in range(2):
                dve.wait_ge(kd_ps, i + 1)
                link(dve.tensor_tensor(kd[:, i * DM:(i + 1) * DM], psb[i][0:NDCA, :], bd[:, i * DM:(i + 1) * DM], ALU.add))
            centre(heads(kd[:, 0:DM]), H, kdc_ready)
            dve.wait_ge(kdsq_ready, 1)
            link(dve.tensor_reduce(kdv[:], kdsq[:], AX.X, ALU.add))
            dve.tensor_scalar(kdv[:], kdv[:], 1.0 / HD, 1e-6, ALU.mult, ALU.add).then_inc(var_ready, 1)
            low(6)
            low(7)
            dve.wait_ge(rstd_ready, 2)
            k3 = heads(kd[:, 0:DM])
            link(dve.tensor_tensor(k3, k3, bc(kdv[:], 2, HD), ALU.mult))
            link(dve.tensor_tensor(k3, k3, bc(dw[:], 1, H), ALU.mult))
            dve.tensor_tensor(k3, k3, bc(db[:], 1, H), ALU.add).then_inc(kd_ready, 1)
            dve.wait_ge(mask_done, 2)
            dve.wait_ge(kdT_ps, 1)
            for g in range(NG):
                dve.tensor_tensor(kdb[:, g, :].rearrange("p (h k) -> p h k", h=G),
                                  bc(psa[0][:, g * NDCA:(g + 1) * NDCA], 1, G), mkd[:], ALU.mult).then_inc(blocks_ready, 1)
            dve.wait_ge(vrep_ps, 1)
            for g in range(NG):
                dve.tensor_tensor(vdb[:, g, :], psa[1][0:G * NDCA, g * P:(g + 1) * P],
                                  mvd[:].rearrange("p h d -> p (h d)"), ALU.mult).then_inc(blocks_ready, 1)
            dve.wait_ge(sd_ps, 1)
            s3 = psa[0][:].rearrange("p (h k) -> p h k", k=NDCA)
            link(dve.tensor_reduce(sm[:], s3, AX.X, ALU.max))
            dve.tensor_tensor(sd[:], s3, bc(sm[:], 2, NDCA), ALU.subtract).then_inc(sdm_ready, 1)
            dve.wait_ge(sde_ready, 1)
            link(dve.tensor_reduce(ssum[:], sd[:], AX.X, ALU.add))
            link(dve.reciprocal(ssum[:], ssum[:]))
            dve.tensor_tensor(sd[:], sd[:], bc(ssum[:], 2, NDCA), ALU.mult).then_inc(pd_ready, 1)
            for i in range(2):
                dve.wait_ge(pdT_ps, i + 1)
                dve.tensor_copy(pdT[:, 2 * i:2 * i + 2, :], psb[i][0:G * NDCA, :].rearrange("p (c l) -> p c l", c=2)).then_inc(pdT_ready, 1)
            for i in range(2):
                dve.wait_ge(cd_ps, i + 1)
                dve.tensor_copy(dcaT[:, 2 * i:2 * i + 2, :], psa[i][:].rearrange("p (c l) -> p c l", c=2)).then_inc(keep.dca_done, 1)

        @block.tensor
        def _(pe):
            pe.wait_ge(mask_done, 1)

            def turn_context(b):
                pe.wait_ge(ctx_in[b], 16)
                if b >= 2:
                    pe.wait_ge(clo_ready, b - 1)
                for t in range(TB):
                    for c in range(KC):
                        last = pe.transpose(psc[b % 2][:, c, t * P:(t + 1) * P], cin[:, b, t, c * P:(c + 1) * P], keep.ident[:])
                last.then_inc(cT_ready, 1)

            pe.wait_ge(yd_in, 16)
            for c in range(KC):
                last = pe.transpose(psb[0][:, c * NDCA:(c + 1) * NDCA], yd[:, c * P:(c + 1) * P], keep.ident[0:NDCA, 0:NDCA])
            last.then_inc(ydT_ps, 1)
            pe.wait_ge(xn_ready, QT)
            for c in range(MC):
                for t in range(QT):
                    last = pe.transpose(psa[c // 2][:, (c % 2) * LQ + t * P:(c % 2) * LQ + (t + 1) * P],
                                        xn[:, t, c * P:(c + 1) * P], keep.ident[:])
                if c % 2:
                    last.then_inc(xT_ps, 1)
            for b in range(3):
                turn_context(b)
            pe.wait_ge(xT_ready, 2)
            pe.wait_ge(wq_in, 32)
            for t in range(QT):
                for c in range(MC):
                    last = pe.matmul(psa[t][:], xT[:, c, t * P:(t + 1) * P], wq[:, c, :], start=c == 0, stop=c == MC - 1)
                last.then_inc(q_ps, 1)
            turn_context(3)
            pe.wait_ge(yd_ready, 1)
            pe.wait_ge(wd_in, 32)
            for i in range(2):
                for c in range(KC):
                    last = pe.matmul(psb[i][0:NDCA, :], ydT[:, c, :], wd[:, c, i * DM:(i + 1) * DM], start=c == 0, stop=c == KC - 1)
                last.then_inc(kd_ps, 1)
            for b in range(4, NB):
                turn_context(b)
            pe.wait_ge(qh_ready, 2)
            pe.wait_ge(q_ready, 1)
            for b in range(NB):
                if b >= 2:
                    pe.wait_ge(qst_ready, b - 1)
                for hh in range(2):
                    for t in range(QT):
                        last = pe.transpose(psa[b % 2][0:3 * HD, hh * LQ + t * P:hh * LQ + (t + 1) * P],
                                            two_part(qs[:, t, 2 * b + hh, :]), keep.ident[:])
                last.then_inc(qst_ps, 1)
            pe.wait_ge(kdc_ready, 1)
            for g in range(NG):
                for t in range(QT):
                    src = q[:, t * H + g * G:t * H + (g + 1) * G, :].rearrange("p h d -> p (h d)")
                    last = pe.transpose(psb[g // 2][:, (g % 2) * LQ + t * P:(g % 2) * LQ + (t + 1) * P], src, keep.ident[:])
                if g % 2:
                    last.then_inc(qT_ps, 1)
            pe.wait_ge(kd_ready, 1)
            pe.wait_ge(mask_done, 2)
            pe.wait_ge(qst_ready, NB)
            for g in range(NG):
                last = pe.transpose(psa[0][:, g * NDCA:(g + 1) * NDCA], kd[:, g * P:(g + 1) * P], keep.ident[0:NDCA, 0:NDCA])
            last.then_inc(kdT_ps, 1)
            pe.matmul(psa[1][0:G * NDCA, :], rep[:].rearrange("p h k -> p (h k)"), kd[:, DM:], start=True, stop=True).then_inc(vrep_ps, 1)
            pe.wait_ge(blocks_ready, 2 * NG)
            pe.wait_ge(qT_ready, 2)
            for t in range(QT):
                for g in range(NG):
                    at = (t * NG + g) * G * NDCA
                    last = pe.matmul(psa[0][:, at:at + G * NDCA], qT[:, g, t * P:(t + 1) * P], kdb[:, g, :], start=True, stop=True)
            last.then_inc(sd_ps, 1)
            pe.wait_ge(pd_ready, 1)
            for g in range(NG):
                for t in range(QT):
                    src = sd[:, t * H + g * G:t * H + (g + 1) * G, :].rearrange("p h k -> p (h k)")
                    last = pe.transpose(psb[g // 2][0:G * NDCA, (g % 2) * LQ + t * P:(g % 2) * LQ + (t + 1) * P], src, keep.ident[:])
                if g % 2:
                    last.then_inc(pdT_ps, 1)
            pe.wait_ge(pdT_ready, 2)
            for g in range(NG):
                last = pe.matmul(psa[g // 2][:, (g % 2) * LQ:(g % 2 + 1) * LQ], vdb[:, g, :], pdT[:, g, :], start=True, stop=True)
                if g % 2:
                    last.then_inc(cd_ps, 1)


def after_attention(keep):
    room = keep.vnew[:].rearrange("p t n -> p (t n)")
    wo = room[:, 0:MC * DM].rearrange("p (c n) -> p c n", c=MC)
    x = room[:, MC * DM + NG * LQ:].rearrange("p (t n) -> p t n", t=QT)
    return wo, room[:, MC * DM:MC * DM + NG * LQ], x


def attend(nc, io, keep, q_scr, w_scr, b_scr, d_scr):
    with ExitStack() as ctx:
        p = Pools(nc, ctx)
        wg, bg, qg, q_in = keep.wg, keep.bg, keep.qg, keep.q_in
        kth = p.sb("k_T_hi", [P, LK], F32R)
        ktl = p.sb("k_T_lo", [P, LK], F32R)
        vnew = keep.vnew
        v = p.sb("v", [P, LK // P, P])
        kst = [p.sb(f"k_stack{i}", [3 * HD + 2, LK], F32R) for i in range(2)]
        KR = 4
        kc = p.sb("k_centred", [P, KR, TB * G, HD])
        ksq = p.sb("k_sq", [P, TB * G, HD])
        kv = p.sb("k_var", [P, NB, TB * G])
        kn = keep.x1[:, 0, :].rearrange("p (t n) -> p t n", t=TB)
        ktf = keep.x1[:, 1, :]
        PR = 4
        pr = p.sb("probs", [P, PR, 2, LQ])
        prs = p.sb("probs_pair_sum", [P, 2, 2 * LQ])
        mx = p.sb("row_max", [P, QT, NB])
        nm = p.sb("minus_max", [P, QT])
        mp = p.sb("minus_max_parts", [P, QT, 2], F32R)
        o = p.sb("out_parts", [P, 2 * LQ])
        og = p.sb("group_out", [P, 2, LQ])
        mhalf = p.sb("minus_half2", [P, TB * G])
        epst = p.sb("k_eps", [P, TB * G])
        krs = p.sb("k_rstd", [P, 2, TB * G])
        ktmp = p.sb("k_rstd_tmp", [P, 2, TB * G])
        ones = p.sb("ones_hd", [P, HD])
        ps_e = [p.ps(f"ps_e{i}", [P, 2 * LQ]) for i in range(2)]
        ps_m = [p.ps(f"ps_m{i}", [P, BK]) for i in range(2)]
        ps_o = [p.ps(f"ps_o{i}", [P, 2 * LQ]) for i in range(2)]
        ps_kv = p.ps("ps_kv", [P, BK])
        ps_kt = p.ps("ps_kt", [P, BK])
        KVB = {True: [ps_kv, ps_o[0]], False: [ps_kv]}
        KTB = {True: [ps_kt, ps_o[1]], False: [ps_kt]}

        names = ("rows kv_ps kv_evac v_evac ksq_ready kss_ready krstd_step kvar_pool kpow_ready kn_ready kt_ps kthi_ready "
                 "ktf_ready ktlo_ready ms_ready mx_ready nm_ready mp_hi mp_ready mt_ps qm_ready es_ready p_ready pv_ready "
                 "pair_ready sum_ready o_ready f_ready og_ready rden_ready cx_ready")
        s = {n: p.sem(n) for n in names.split()}
        s["wg_in"] = keep.wg_in
        kst_in = [[p.sem(f"kst_in{i}_{c}") for c in range(NB // 2)] for i in range(2)]
        v_in = [p.sem(f"v_in{c}") for c in range(NB // 2)]
        block = ctx.enter_context(nc.Block())
        UN = LK // P // 2
        MXU = QT * NB
        HV = 2 * NB
        NC4 = NB // 2

        def wait(eng, name, value):
            if not (isinstance(value, int) and value <= 0):
                eng.wait_ge(s[name], value)

        def by_pool(gp, b):
            return isinstance(gp, int) and gp == 0 and b % 2 == 0

        def keys_in(b):
            return min(BK, KEYS - b * BK)

        def tile_keys(t):
            return min(P, KEYS - t * P)

        def max_units(u, half):
            at = 2 * u + half
            return range(min(MXU, MXU * at // 24), min(MXU, MXU * (at + 1) // 24))

        at = lambda k, lag: (k - lag) // 2 if k is not None and k >= lag and (k - lag) % 2 == 0 and (k - lag) // 2 < NB else None
        SQ, RED, RSTD, NORM, TURN, HIGH, LOW = 2, 3, 4, 7, 8, 9, 10
        RSTD_STEPS = RSQRT_STEPS + 1
        TURNS = 2 * NB + LOW
        FIRST_MAX = 4 + LOW

        def turn_in(h, u):
            m = h * UN + u - 20
            k = m * 3 // 4
            return k if 0 <= k < TURNS and k != (m - 1) * 3 // 4 else None

        def stack_high(sp, h, c):
            ks = slice(c * 2 * BK, (c + 1) * 2 * BK)
            hr = slice(h * HD, (h + 1) * HD)
            for row in (0, 2 * HD):
                sp.dma_start(two_part(kst[h % 2][row:row + HD, ks]), two_part(kth[hr, ks])).then_inc(kst_in[h % 2][c], 16)

        def stack_low(sp, h, c):
            ks = slice(c * 2 * BK, (c + 1) * 2 * BK)
            hr = slice(h * HD, (h + 1) * HD)
            sp.dma_start(two_part(kst[h % 2][HD:2 * HD, ks]), two_part(ktl[hr, ks])).then_inc(kst_in[h % 2][c], 16)

        def stack(sp, h, c):
            stack_high(sp, h, c)
            stack_low(sp, h, c)

        @block.sync
        def _(sp):
            tiles = LK // P // NC4

            def copy_v(c):
                part = slice(c * tiles, (c + 1) * tiles)
                sp.dma_start(v[:, part, :], vnew[:, part, :]).then_inc(v_in[c], 16)

            def group(g, more):
                es = g * G * UN
                if more:
                    sp.wait_ge(s["kv_ps"], (g + 1) * HV)
                    load_group_weights(sp, keep, w_scr, b_scr, g + 1)
                for h in (2, 3):
                    for c in range(NC4):
                        sp.wait_ge(s["es_ready"], es + (h - 2) * UN + 4 * (c + 1))
                        stack(sp, h, c)
                    if more:
                        load_head_queries(sp, keep, q_scr, g + 1, h - 2)
                if more:
                    for c in range(NC4):
                        sp.wait_ge(s["kthi_ready"], (g + 1) * NB + 2 * (c + 1))
                        stack_high(sp, 0, c)
                        sp.wait_ge(s["ktlo_ready"], (g + 1) * NB + 2 * (c + 1))
                        stack_low(sp, 0, c)
                    sp.wait_ge(s["es_ready"], es + 3 * UN)
                    load_head_queries(sp, keep, q_scr, g + 1, 2)
                    for c in range(NC4):
                        sp.wait_ge(s["pv_ready"], es + 3 * UN + 4 * (c + 1))
                        copy_v(c)
                        stack(sp, 1, c)
                    sp.wait_ge(s["es_ready"], es + 4 * UN)
                    load_head_queries(sp, keep, q_scr, g + 1, 3)

            for c in range(NC4):
                sp.wait_ge(s["kthi_ready"], 2 * (c + 1))
                stack_high(sp, 0, c)
                sp.wait_ge(s["ktlo_ready"], 2 * (c + 1))
                stack_low(sp, 0, c)
            for c in range(NC4):
                stack(sp, 1, c)
            group(0, True)
            with sp.Fori(1, NG - 1) as g:
                group(g, True)
            for c in range(NC4):
                sp.wait_ge(v_in[c], (NG - 1) * 16)
            wo, dca, x = after_attention(keep)
            sp.wait_ge(keep.d_out, 16)
            sp.dma_start(dca, d_scr).then_inc(keep.dca_in, 16)
            sp.dma_start(wo, io["L0_xattn_Wo"].rearrange("(c p) n -> p c n", p=P)).then_inc(keep.wo_in, 16)
            sp.dma_start(x, io["x"].rearrange("o (t p) d -> p (o t) d", p=P)).then_inc(keep.xb_in, 16)
            group(NG - 1, False)

        @block.gpsimd
        def _(pool):
            for n, (t, value) in enumerate(((epst[:], 1e-6), (mhalf[:], -0.5))):
                pool.memset(t, value).then_inc(s["kvar_pool"], 1)
                pool.wait_ge(s["kvar_pool"], n + 1)
            for b in range(0, NB, 2):
                pool.wait_ge(s["kss_ready"], b + 1)
                pool.tensor_tensor(kv[:, b, :], kv[:, b, :], epst[:], ALU.add).then_inc(s["kvar_pool"], 1)
                pool.wait_ge(s["kvar_pool"], b // 2 + 3)
                if b >= 2:
                    pool.wait_ge(s["kn_ready"], b - 1)
                pool.tensor_tensor(krs[:, 0, :], kv[:, b, :], mhalf[:], ALU.pow).then_inc(s["kpow_ready"], 1)
            pool.wait_ge(s["kpow_ready"], NB // 2)
            pool.memset(ones[:], 1.0).then_inc(s["rows"], 1)
            for i in range(2):
                pool.wait_ge(s["rows"], i + 1)
                pool.memset(two_part(kst[i][3 * HD:, :]), 1.0).then_inc(s["rows"], 1)

            def group(g, more):
                for h in range(G):
                    n = g * G + h
                    for u in range(UN):
                        if u % 2 and u < UN - 1:
                            pair = u // 2
                            pool.wait_ge(s["p_ready"], n * UN + u + 1)
                            wait(pool, "sum_ready", n * 4 + pair // 2)
                            pool.tensor_tensor(prs[:, pair % 2, :], pr[:, (u - 1) % PR].rearrange("p t l -> p (t l)"),
                                               pr[:, u % PR].rearrange("p t l -> p (t l)"), ALU.add).then_inc(s["pair_ready"], 1)

            group(0, True)
            with pool.Fori(1, NG - 1) as g:
                group(g, True)
            group(NG - 1, False)

        @block.scalar
        def _(act):
            def values(gp, hv, first):
                act.wait_ge(s["kv_evac"], gp * HV + hv + 1)
                if hv % 4 == 0 and not (isinstance(gp, int) and gp < 2):
                    act.wait_ge(v_in[hv // 4], (gp - 1) * 16)
                src = KVB[first][hv % len(KVB[first])][:].rearrange("p (t h e) -> p t h e", t=2, e=2 * HD)
                act.activation((v if first else vnew)[:, 2 * hv:2 * hv + 2, :].rearrange("p t (h d) -> p t h d", d=HD), src[:, :, :, HD:], ACT.Copy).then_inc(s["v_evac"], 1)

            def square(gp, b):
                act.wait_ge(s["kv_evac"], gp * HV + 2 * b + 2)
                wait(act, "kss_ready", gp * NB + b)
                act.activation(ksq[:], kc[:, b % KR], ACT.Square, scale=HD ** -0.5).then_inc(s["ksq_ready"], 1)

            def high(gp, b, first):
                bank = KTB[first][b % len(KTB[first])]
                act.wait_ge(s["kt_ps"], gp * NB + b + 1)
                wait(act, "ktlo_ready", gp * NB + b)
                if not first and b % 2 == 0:
                    act.wait_ge(kst_in[1][b // 2], gp * 96)
                act.activation(ktf, bank[:], ACT.Identity, bias=keep.knb[:], scale=keep.knw[:]).then_inc(s["ktf_ready"], 1)
                act.activation(kth[:, b * BK:(b + 1) * BK], bank[:], ACT.Identity, bias=keep.knb[:], scale=keep.knw[:]).then_inc(s["kthi_ready"], 1)

            def out_parts(n, h):
                act.wait_ge(s["pv_ready"], (n + 1) * UN)
                act.wait_ge(s["sum_ready"], (n + 1) * 4)
                wait(act, "f_ready", n)
                act.activation(o[:], ps_o[h % 2][:], ACT.Copy).then_inc(s["o_ready"], 1)

            def head_out(g, n, h):
                act.wait_ge(s["f_ready"], n + 1)
                if h == 0:
                    wait(act, "cx_ready", g)
                rows = slice(h * HD, (h + 1) * HD)
                act.activation(og[rows].rearrange("p t l -> p (t l)"), ps_o[h % 2][rows, :], ACT.Copy).then_inc(s["og_ready"], 1)

            def group(g, more):
                for h in range(G):
                    n = g * G + h
                    before = isinstance(n, int) and n == 0
                    for u in range(UN):
                        act.wait_ge(s["es_ready"], n * UN + u + 1)
                        wait(act, "pv_ready", n * UN + u - PR + 1)
                        if u % 2 == 0:
                            wait(act, "pair_ready", n * 7 + ((u - PR) // 2 + 1 if u >= PR else 0))
                        if u < UN - 1:
                            act.activation(pr[:, u % PR].rearrange("p t l -> p (t l)"), ps_e[u % 2][:], ACT.Exp).then_inc(s["p_ready"], 1)
                        else:
                            last = tile_keys(2 * u + 1)
                            act.activation(pr[:, u % PR, 0], ps_e[u % 2][:, 0:LQ], ACT.Exp)
                            act.activation(pr[0:last, u % PR, 1], ps_e[u % 2][0:last, LQ:], ACT.Exp).then_inc(s["p_ready"], 1)
                        if not before and u == 1:
                            out_parts(n - 1, (h - 1) % G)
                        if not before and u == 5:
                            head_out(g if h else g - 1, n - 1, (h - 1) % G)
                        k = turn_in(h, u)
                        if more and k is not None and k < HV:
                            values(g + 1, k, False)
                        if more and at(k, SQ) is not None:
                            square(g + 1, at(k, SQ))
                        if more and at(k, HIGH) is not None:
                            high(g + 1, at(k, HIGH), False)

            act.wait_ge(keep.kn_in, 16 * 2 * G)
            for k in range(TURNS):
                if k < HV:
                    values(0, k, True)
                if at(k, SQ) is not None:
                    square(0, at(k, SQ))
                if at(k, HIGH) is not None:
                    high(0, at(k, HIGH), True)
            group(0, True)
            with act.Fori(1, NG - 1) as g:
                group(g, True)
            group(NG - 1, False)
            out_parts(NG * G - 1, G - 1)
            head_out(NG - 1, NG * G - 1, G - 1)

        @block.vector
        def _(dve):
            def evacuate(gp, hv, first):
                dve.wait_ge(s["kv_ps"], gp * HV + hv + 1)
                src = KVB[first][hv % len(KVB[first])][:].rearrange("p (t h e) -> p t h e", t=2, e=2 * HD)
                bias = bc(bg[:].rearrange("p (h e) -> p h e", e=2 * HD), 1, 2)
                if hv % 2 == 0 and not (first and hv // 2 < KR):
                    dve.wait_ge(s["kn_ready"], gp * NB + hv // 2 - KR + 1)
                half = slice(hv % 2 * 2 * G, (hv % 2 + 1) * 2 * G)
                dve.tensor_tensor(kc[:, hv // 2 % KR, half, :].rearrange("p (t h) d -> p t h d", t=2), src[:, :, :, 0:HD],
                                  bias[:, :, :, 0:HD], ALU.add).then_inc(s["kv_evac"], 1)

            def reduce(gp, b):
                dve.wait_ge(s["ksq_ready"], gp * NB + b + 1)
                dve.tensor_reduce(kv[:, b, :], ksq[:], AX.X, ALU.add).then_inc(s["kss_ready"], 1)

            def steps_before(gp, b):
                return b // 2 * RSTD_STEPS if isinstance(gp, int) and gp == 0 else (gp * NB - NB // 2 + b) * RSTD_STEPS

            def rstd(gp, b, i):
                if i == 0:
                    dve.wait_ge(s["kss_ready"], gp * NB + b + 1)
                    ins = dve.tensor_scalar(kv[:, b, :], kv[:, b, :], 1e-6, None, ALU.add)
                else:
                    dve.wait_ge(s["krstd_step"], steps_before(gp, b) + i)
                    ins = rsqrt_step(dve, i - 1, kv[:, b, :], krs[:, b % 2, :], ktmp[:, b % 2, :])
                ins.then_inc(s["krstd_step"], 1)

            def norm(gp, b):
                if by_pool(gp, b):
                    dve.wait_ge(s["kpow_ready"], b // 2 + 1)
                else:
                    dve.wait_ge(s["krstd_step"], steps_before(gp, b) + RSTD_STEPS)
                wait(dve, "kt_ps", gp * NB + b)
                dve.tensor_tensor(kn.rearrange("p t (h d) -> p (t h) d", d=HD), kc[:, b % KR], bc(krs[:, b % 2, :], 2, HD), ALU.mult).then_inc(s["kn_ready"], 1)

            def low(gp, b, first):
                dve.wait_ge(s["kthi_ready"], gp * NB + b + 1)
                if not first and b % 2 == 0:
                    dve.wait_ge(kst_in[1][b // 2], gp * 96)
                ks = slice(b * BK, (b + 1) * BK)
                dve.tensor_tensor(ktl[:, ks], ktf, two_part(kth[:, ks]), ALU.subtract).then_inc(s["ktlo_ready"], 1)

            def project(gp, k, first):
                steps = iter([(b, i) for lag in (2, 1, 0) for b in [at(k, RSTD + lag)] if b is not None and not by_pool(gp, b)
                              for i in range(RSTD_STEPS) if i // 4 == lag])

                def rstd_steps(n):
                    for step in islice(steps, n):
                        rstd(gp, *step)

                rest = [(at(k, NORM), norm)]
                rest.append((k if k is not None and k < HV else None, lambda gp, hv: evacuate(gp, hv, first)))
                rest.append((at(k, RED), reduce))
                rest.append((at(k, LOW), lambda gp, b: low(gp, b, first)))
                for what, work in rest:
                    if what is not None:
                        work(gp, what)
                        rstd_steps(2)
                rstd_steps(2 * RSTD_STEPS)

            def row_max(n, u):
                kb, t = divmod(u, QT)
                dve.wait_ge(s["ms_ready"], n * MXU + u + 1)
                dve.reduce_max(mx[:, t, kb:kb + 1], ps_m[u % 2][:, 0:keys_in(kb)], AX.X).then_inc(s["mx_ready"], 1)

            def minus_max(n):
                dve.wait_ge(s["mx_ready"], n * MXU + MXU)
                dve.tensor_reduce(nm[:], mx[:], AX.X, ALU.max, negate=True).then_inc(s["nm_ready"], 1)
                dve.wait_ge(s["nm_ready"], n + 1)
                dve.tensor_copy(mp[:, :, 0], nm[:]).then_inc(s["mp_hi"], 1)
                dve.wait_ge(s["mp_hi"], n + 1)
                dve.tensor_tensor(mp[:, :, 1], nm[:], two_part(mp[:, :, 0]), ALU.subtract).then_inc(s["mp_ready"], 1)

            def max_rows(n, h):
                dve.wait_ge(s["mt_ps"], n + 1)
                dve.tensor_copy(qg[3 * HD:, h, :], ps_m[0][0:2, 0:LQ]).then_inc(s["qm_ready"], 1)

            def normalise(g):
                dve.wait_ge(s["og_ready"], (g + 1) * G)
                part = LQ // 4
                for i in range(4):
                    cols = slice(i * part, (i + 1) * part)
                    dve.reciprocal(og[:, 1, cols], og[:, 1, cols]).then_inc(s["rden_ready"], 1)
                    yield
                dve.wait_ge(s["rden_ready"], 4 * g + 4)
                dve.wait_ge(keep.d_out, 16)
                dve.tensor_tensor(keep.ctxT[:, bass.ts(g, LQ)], og[:, 0, :], og[:, 1, :], ALU.mult).then_inc(s["cx_ready"], 1)
                yield

            def group(g, more):
                for h in range(G):
                    n = g * G + h
                    for u in range(UN):
                        ahead = more or h + 1 < G
                        if ahead:
                            if u == 15:
                                max_rows(n + 1, (h + 1) % G)
                            if u == 12:
                                minus_max(n + 1)
                            for m in max_units(u, 0):
                                row_max(n + 1, m)
                        if more:
                            project(g + 1, turn_in(h, u), False)
                        if ahead:
                            for m in max_units(u, 1):
                                row_max(n + 1, m)
                        if h == 0 and u == 7:
                            steps = iter(()) if isinstance(g, int) and g == 0 else normalise(g - 1)
                        if h == 0 and u >= 7:
                            next(steps, None)

            dve.wait_ge(s["wg_in"], 32)
            for k in range(FIRST_MAX + MXU):
                project(0, k, True)
                if 0 <= k - FIRST_MAX < MXU:
                    row_max(0, k - FIRST_MAX)
            minus_max(0)
            max_rows(0, 0)
            group(0, True)
            with dve.Fori(1, NG - 1) as g:
                group(g, True)
            group(NG - 1, False)
            for _ in normalise(NG - 1):
                pass

        @block.tensor
        def _(pe):
            def project(gp, hv, first):
                if hv == 0:
                    pe.wait_ge(s["wg_in"], gp * 32 + 32)
                bank = KVB[first][hv % len(KVB[first])]
                wait(pe, "v_evac", gp * HV + hv + 1 - len(KVB[first]))
                for t in range(2):
                    tok = slice((2 * hv + t) * P, (2 * hv + t + 1) * P)
                    passes = [(a, w, c) for a, w in ((keep.cTh, 0), (keep.cTl, 0), (keep.cTh, 1)) for c in range(KC)]
                    for i, (a, w, c) in enumerate(passes):
                        last = pe.matmul(bank[:, t * 2 * P:(t + 1) * 2 * P], a[:, c, tok], wg[:, w, c, :], start=i == 0, stop=i == len(passes) - 1)
                last.then_inc(s["kv_ps"], 1)

            def turn(gp, b, first):
                bank = KTB[first][b % len(KTB[first])]
                pe.wait_ge(s["kn_ready"], gp * NB + b + 1)
                wait(pe, "kthi_ready", gp * NB + b + 1 - len(KTB[first]))
                for t in range(TB):
                    last = pe.transpose(bank[:, t * P:(t + 1) * P], kn[:, t, :], keep.ident[:])
                last.then_inc(s["kt_ps"], 1)

            def max_unit(g, h, n, u):
                kb, t = divmod(u, QT)
                m = keys_in(kb)
                if u == 0:
                    pe.wait_ge(q_in[h], g * 16 + 16)
                if kb % 2 == 0 and t == 0:
                    pe.wait_ge(kst_in[h % 2][kb // 2], g * 96 + 48 * (h // 2 + 1))
                if not (isinstance(n, int) and n == 0 and u < 2):
                    pe.wait_ge(s["mx_ready"], n * MXU + u - 1)
                pe.matmul(ps_m[u % 2][:, 0:m], qg[0:3 * HD, h, t * P:(t + 1) * P], kst[h % 2][0:3 * HD, kb * BK:kb * BK + m],
                          start=True, stop=True).then_inc(s["ms_ready"], 1)

            def turn_max(n):
                pe.wait_ge(s["mp_ready"], n + 1)
                for t in range(QT):
                    last = pe.transpose(ps_m[0][0:2, t * P:(t + 1) * P], two_part(mp[:, t, :]), keep.ident[:])
                last.then_inc(s["mt_ps"], 1)

            def scores(n, h, u):
                if u == 0:
                    pe.wait_ge(s["qm_ready"], n + 1)
                wait(pe, "p_ready", n * UN + u - 1)
                for t in range(2):
                    m = tile_keys(2 * u + t)
                    ks = (2 * u + t) * P
                    last = pe.matmul(ps_e[u % 2][0:m, t * LQ:(t + 1) * LQ], kst[h % 2][:, ks:ks + m], qg[:, h, :], start=True, stop=True)
                last.then_inc(s["es_ready"], 1)

            def weighted(g, n, h, u):
                pe.wait_ge(s["p_ready"], n * UN + u + 1)
                if h == 0 and u % 4 == 0:
                    if isinstance(g, int) and g == 0:
                        pe.wait_ge(s["v_evac"], HV)
                    else:
                        pe.wait_ge(v_in[u // 4], g * 16)
                for t in range(2):
                    m = tile_keys(2 * u + t)
                    row = (2 * u + t) % 4 * HD
                    last = pe.matmul(ps_o[h % 2][row:row + HD, 0:LQ], v[0:m, 2 * u + t, h * HD:(h + 1) * HD], pr[0:m, u % PR, t, :],
                                     start=u < 2, stop=u >= UN - 2, skip_group_check=True)
                last.then_inc(s["pv_ready"], 1)

            def sums(n, h, j):
                pe.wait_ge(s["pair_ready"], n * 7 + min(2 * j + 2, 7))
                what = [prs[:, k, t * LQ:(t + 1) * LQ] for k in range(2 if j < 3 else 1) for t in range(2)]
                if j == 3:
                    what += [pr[0:tile_keys(2 * u + t), u % PR, t, :] for u in (UN - 2, UN - 1) for t in range(2)]
                for i, w in enumerate(what):
                    row = i % 4 * HD
                    last = pe.matmul(ps_o[h % 2][row:row + HD, LQ:], ones[0:w.shape[0], :], w, start=False, stop=j == 3, skip_group_check=True)
                last.then_inc(s["sum_ready"], 1)

            def fold(n, h):
                pe.wait_ge(s["o_ready"], n + 1)
                rows = slice(h * HD, (h + 1) * HD)
                pe.matmul(ps_o[h % 2][rows, :], keep.fold[:], o[:], start=True, stop=True).then_inc(s["f_ready"], 1)

            def group(g, more):
                for h in range(G):
                    n = g * G + h
                    before = isinstance(n, int) and n == 0
                    for u in range(UN):
                        k = turn_in(h, u)
                        scores(n, h, u)
                        unit_of = lambda m: max_unit(g, h + 1, n + 1, m) if h + 1 < G else max_unit(g + 1, 0, n + 1, m)
                        ahead = more or h + 1 < G
                        for m in max_units(u, 0) if ahead else ():
                            unit_of(m)
                        if more and k is not None and k < HV:
                            project(g + 1, k, False)
                        if more and at(k, TURN) is not None:
                            turn(g + 1, at(k, TURN), False)
                        if u == 14 and ahead:
                            turn_max(n + 1)
                        if u and u % 2 == 0:
                            if u == 2:
                                wait(pe, "og_ready", n - 1)
                            weighted(g, n, h, u - 2)
                            weighted(g, n, h, u - 1)
                        elif u == 0 and not before:
                            finish(g if h else g - 1, n - 1, (h - 1) % G)
                        if u in (6, 10, 14):
                            sums(n, h, (u - 6) // 4)
                        if u == 4 and not before:
                            fold(n - 1, (h - 1) % G)
                        for m in max_units(u, 1) if ahead else ():
                            unit_of(m)

            def finish(g, n, h):
                weighted(g, n, h, UN - 2)
                weighted(g, n, h, UN - 1)
                sums(n, h, 3)

            for k in range(FIRST_MAX + MXU):
                if k < HV:
                    project(0, k, True)
                if at(k, TURN) is not None:
                    turn(0, at(k, TURN), True)
                if 0 <= k - FIRST_MAX < MXU:
                    max_unit(0, 0, 0, k - FIRST_MAX)
            turn_max(0)
            pe.wait_ge(s["kthi_ready"], NB)
            pe.wait_ge(s["rows"], 3)
            group(0, True)
            with pe.Fori(1, NG - 1) as g:
                group(g, True)
            group(NG - 1, False)
            finish(NG - 1, NG * G - 1, G - 1)
            fold(NG * G - 1, G - 1)


def project_attention(nc, io, keep):
    with ExitStack() as ctx:
        p = Pools(nc, ctx)
        wo, dca, x = after_attention(keep)
        bo = p.sb("b_o", [P, DM])
        c = p.sb("ctx_sum", [P, NG * LQ])
        ps = [p.ps(f"ps_wo{t}", [P, DM]) for t in range(QT)]
        bo_in, xb_ready, c_ready, wo_ps = (p.sem(n) for n in ("bo_in", "xb_ready", "c_ready", "wo_ps"))
        block = ctx.enter_context(nc.Block())

        @block.sync
        def _(sp):
            sp.dma_start(bo[:], io["L0_xattn_bo"].partition_broadcast(P)).then_inc(bo_in, 16)

        @block.vector
        def _(dve):
            dve.wait_ge(keep.dca_in, 16)
            for g in range(NG):
                part = slice(g * LQ, (g + 1) * LQ)
                dve.tensor_tensor(c[:, part], keep.ctxT[:, part], dca[:, part], ALU.add).then_inc(c_ready, 1)
            dve.wait_ge(keep.xb_in, 16)
            dve.wait_ge(bo_in, 16)
            dve.tensor_tensor(x, x, bc(bo[:], 1, QT), ALU.add).then_inc(xb_ready, 1)
            dve.wait_ge(xb_ready, 1)
            for t in range(QT):
                dve.wait_ge(wo_ps, t + 1)
                dve.tensor_tensor(keep.x1[:, t, :], ps[t][:], x[:, t, :], ALU.add).then_inc(keep.x1_ready, 1)

        @block.tensor
        def _(pe):
            pe.wait_ge(keep.wo_in, 16)
            for t in range(QT):
                for g in range(NG):
                    pe.wait_ge(c_ready, g + 1)
                    at = g * LQ + t * P
                    last = pe.matmul(ps[t][:], c[:, at:at + P], wo[:, g, :], start=g == 0, stop=g == NG - 1)
                last.then_inc(wo_ps, 1)


DI = 1024
NS = 128
NH = 16
HP = DI // NH
CT = DI // P
XT = (DI + 2 * NS) // P
TAPS = 4
CH = 128
NCH = LQ // CH
BT, CTT = CT, CT + 1

E = 64
FG = 8
GS = E // FG
TOPK = 8
FI = 352
FT = -(-FI // P)
NEG_INF = -1e9


def load_expert(sp, io, keep, g, j):
    full = (FT - 1) * P
    for n, w, t in (("g", io["L0_ffn_gate_proj_w"], keep.wg[j]), ("u", io["L0_ffn_up_proj_w"], keep.wu[j])):
        sp.dma_start(t[:, 0:FT - 1, :], w[bass.ds(g, 1), 0:full, :].rearrange("o (i p) d -> p (o i) d", p=P)).then_inc(keep.w_in[n, j], 16)
        sp.dma_start(t[0:FI - full, FT - 1, :], w[bass.ds(g, 1), full:, :].rearrange("o p d -> p (o d)")).then_inc(keep.w_in[n, j], 16)
    sp.dma_start(keep.wd[j][:], io["L0_ffn_down_proj_w"][bass.ds(g, 1), :, :].rearrange("o (c p) i -> p (o c) i", p=P)).then_inc(keep.w_in["d", j], 16)


def mixer_projections(nc, io, keep):
    with ExitStack() as ctx:
        p = Pools(nc, ctx)
        stat = p.sb("u_stat", [P, QT, 6])
        aggr = p.sb("u_aggr", [P, QT, 2])
        ur = p.sb("u_rstd", [P, QT])
        un = p.sb("u", [P, QT, DM])
        mhalf = p.sb("minus_half3", [P, QT])
        uh = p.sb("u_T_hi", [P, MC, LQ], F32R)
        ul = p.sb("u_T_lo", [P, MC, LQ], F32R)
        w = p.sb("w_in_rows", [P, 2, DM])
        wh = [p.sb(f"w_in_T_hi{i}", [P, MC, P], F32R) for i in range(2)]
        wl = [p.sb(f"w_in_T_lo{i}", [P, MC, P], F32R) for i in range(2)]
        wdt = p.sb("w_dt_rows", [NH, DM])
        wdh = p.sb("w_dt_T_hi", [P, MC, NH], F32R)
        wdl = p.sb("w_dt_T_lo", [P, MC, NH], F32R)
        cw = p.sb("conv_w", [P, XT, TAPS])
        cb = p.sb("conv_b", [P, XT])
        XW = TAPS - 1 + LQ
        xp = p.sb("conv_in", [P, XT * XW])
        cv = p.sb("conv_sum", [P, 2, TAPS, LQ])
        dtb = p.sb("dt_bias", [P, NH])
        al = p.sb("a_log", [P, NH])
        t1 = p.sb("dt_tmp", [P, NCH * NH])
        t2 = p.sb("dt_pos", [P, NCH * NH])
        ps_t = [p.ps(f"ps_wt{i}", [P, DM]) for i in range(2)]
        ps_x = [p.ps(f"ps_xz{i}", [P, DM]) for i in range(2)]
        ps_u = [p.ps(f"ps_u{i}", [P, DM]) for i in range(2)]
        ps_d = [p.ps(f"ps_dt{i}", [P, DM]) for i in range(2)]
        names = ("var_u rstd_u un_ready uT_ps uh_ready ul_ready wT_ps wh_ready wl_ready xz_ps xz_read conv_ready xc_done "
                 "wd_in wdT_ps wdh_ready wdl_ready dt_ps conv_in zero_ready pool_c v1 e1 l1 ea dA_set")
        s = {n: p.sem("m_" + n) for n in names.split()}
        w_in = [p.sem(f"w_rows_in{i}") for i in range(2)]
        block = ctx.enter_context(nc.Block())
        wv = io["L0_attn_W_in"]
        NZ, NX = CT // 2, XT // 2

        @block.sync
        def _(sp):
            sp.dma_start(wdt[:], wv[(CT + XT) * P:, :]).then_inc(s["wd_in"], 16)
            rows = wv[0:(CT + XT) * P, :].rearrange("(i j p) d -> i j p d", j=2, p=P)
            for j in range(2):
                sp.dma_start(w[:, j, :], rows[NZ, j]).then_inc(w_in[j], 16)
            sp.dma_start(cw[:], io["L0_attn_conv_w"].rearrange("(c p) k -> p c k", p=P)).then_inc(s["conv_in"], 16)
            sp.dma_start(cb[:], io["L0_attn_conv_b"].rearrange("(c p) -> p c", p=P), allow_slow_non_contiguous=True).then_inc(s["conv_in"], 16)
            sp.dma_start(dtb[:], io["L0_attn_dt_bias"].partition_broadcast(P)).then_inc(keep.mix_par_in, 16)
            sp.dma_start(al[:], io["L0_attn_A_log"].partition_broadcast(P)).then_inc(keep.mix_par_in, 16)
            sp.dma_start(keep.nw[:], io["L0_attn_norm_weight"].rearrange("(c p) -> p c", p=P), allow_slow_non_contiguous=True).then_inc(keep.mix_par_in, 16)
            for k in range(P // HP):
                src = io["L0_attn_D"].rearrange("(c k) -> k c", k=P // HP)[k].partition_broadcast(HP)
                sp.dma_start(keep.dsk[k * HP:(k + 1) * HP, :], src, allow_slow_non_contiguous=True).then_inc(keep.mix_par_in, 16)

            def load_w(i, row):
                for j in range(2):
                    sp.wait_ge(s["wT_ps"], 2 * i + j - 1)
                    sp.dma_start(w[:, j, :], rows[row, j]).then_inc(w_in[j], 16)

            with sp.Fori(1, NX) as i:
                load_w(i, i + NZ)
            with sp.Fori(NX, NX + NZ) as i:
                load_w(i, i - NX)
            sp.dma_start(keep.wo[:], io["L0_attn_W_out"].rearrange("(c p) n -> p c n", p=P)).then_inc(keep.w_out_in, 16)

        @block.gpsimd
        def _(pool):
            pool.memset(mhalf[:], -0.5).then_inc(s["pool_c"], 1)
            pool.memset(xp[:].rearrange("p (m l) -> p m l", m=XT)[:, :, 0:TAPS - 1], 0.0).then_inc(s["zero_ready"], 1)
            pool.wait_ge(s["pool_c"], 1)
            pool.wait_ge(s["var_u"], 1)
            pool.tensor_tensor(ur[:], ur[:], mhalf[:], ALU.pow).then_inc(s["rstd_u"], 1)
            link = p.chain(pool, "x_pool_chain")
            link(pool.memset(keep.ones[:], 1.0))
            link(pool.memset(keep.tri[:], 1.0))
            link(pool.affine_select(out=keep.tri[:], in_=keep.tri[:], compare_op=ALU.is_ge, fill=0.0, base=0, pattern=[[1, P]], channel_multiplier=-1))
            pool.wait_ge(s["dA_set"], 1)
            for c in range(NCH):
                pool.tensor_tensor(keep.dAU[:, c], bc(keep.dA[:, c, :], 2, P), bc(keep.tri[:], 1, NH), ALU.mult).then_inc(keep.dAU_ready, 1)

        @block.scalar
        def _(act):
            act.wait_ge(s["wdT_ps"], 1)
            act.activation(wdh[:], ps_d[0][:, 0:MC * NH].rearrange("p (c h) -> p c h", c=MC), ACT.Copy).then_inc(s["wdh_ready"], 1)

            def w_high(n, j):
                act.wait_ge(s["wT_ps"], n + 1)
                act.activation(wh[j][:], ps_t[j][:].rearrange("p (c n) -> p c n", c=MC), ACT.Copy).then_inc(s["wh_ready"], 1)

            w_high(0, 0)
            w_high(1, 1)
            for i in range(2):
                act.wait_ge(s["uT_ps"], i + 1)
                act.activation(uh[:, 2 * i:2 * i + 2, :], ps_u[i][:].rearrange("p (c l) -> p c l", c=2), ACT.Copy).then_inc(s["uh_ready"], 1)
            def gates(i):
                for j in range(2):
                    act.wait_ge(s["conv_ready"], 2 * TAPS * i + 2 * TAPS - 1 + j)
                    act.activation(keep.xc[:, (2 * i + j) * LQ:(2 * i + j + 1) * LQ], cv[:, j, TAPS - 1, :], ACT.Silu).then_inc(s["xc_done"], 1)

            act.wait_ge(s["zero_ready"], 1)
            for i in range(NX):
                for m in (2 * i, 2 * i + 1):
                    act.wait_ge(s["xz_ps"], m + 1)
                    act.activation(xp[:, m * XW + TAPS - 1:(m + 1) * XW], ps_x[m % 2][:, 0:LQ], ACT.Copy).then_inc(s["xz_read"], 1)
                    w_high(m + 2, m % 2)
                    if i > 1 and m == 2 * i:
                        gates(i - 2)
                if i == 1:
                    act.wait_ge(s["v1"], 1)
                    act.activation(t1[:], t1[:], ACT.Exp, scale=-1.0).then_inc(s["e1"], 1)
                    act.wait_ge(keep.mix_par_in, 80)
                    act.activation(al[:], al[:], ACT.Exp).then_inc(s["ea"], 1)
                    act.wait_ge(s["e1"], 1)
                    act.activation(t1[:], t1[:], ACT.Ln, bias=1.0).then_inc(s["l1"], 1)
            for n in range(CT):
                act.wait_ge(s["xz_ps"], n + XT + 1)
                act.activation(keep.zs[:, n * LQ:(n + 1) * LQ], ps_x[n % 2][:, 0:LQ], ACT.Silu).then_inc(s["xz_read"], 1)
                if n < CT - 2:
                    w_high(n + XT + 2, n % 2)
                if n in (0, 2):
                    gates(NX - 2 + n // 2)

        @block.vector
        def _(dve):
            link = p.chain(dve, "m_dve_chain")
            dve.wait_ge(keep.x1_ready, QT)
            for t in range(QT):
                link(dve.bn_stats(stat[:, t, :], keep.x1[:, t, :]))
                link(dve.bn_aggr(aggr[:, t, :], stat[:, t, :]))
            dve.tensor_scalar(ur[:], aggr[:, :, 1], 1e-5, None, ALU.add).then_inc(s["var_u"], 1)
            dve.wait_ge(s["rstd_u"], 1)
            for t in range(QT):
                dve.tensor_scalar(un[:, t, :], keep.x1[:, t, :], aggr[:, t, 0:1], ur[:, t:t + 1], ALU.subtract, ALU.mult).then_inc(s["un_ready"], 1)
            def w_low(n, j):
                dve.wait_ge(s["wh_ready"], n + 1)
                dve.tensor_tensor(wl[j][:], ps_t[j][:].rearrange("p (c n) -> p c n", c=MC), two_part(wh[j][:]), ALU.subtract).then_inc(s["wl_ready"], 1)

            def conv(i):
                for k in range(TAPS):
                    for j in range(2):
                        m = 2 * i + j
                        taps = cw[:].rearrange("p c k -> p (c k)")[:, bass.ts(m, TAPS)]
                        src = xp[:, bass.ds(m * XW + k, LQ)]
                        if k == 0:
                            dve.wait_ge(s["xz_read"], m + 1)
                            if not (isinstance(i, int) and i == 0):
                                dve.wait_ge(s["xc_done"], m - 1)
                            ins = dve.tensor_scalar(cv[:, j, 0, :], src, taps[:, 0:1], cb[:, bass.ts(m, 1)], ALU.mult, ALU.add)
                        else:
                            dve.wait_ge(s["conv_ready"], (i * TAPS + k - 1) * 2 + j + 1)
                            ins = dve.scalar_tensor_tensor(cv[:, j, k, :], src, taps[:, k:k + 1], cv[:, j, k - 1, :], ALU.mult, ALU.add)
                        ins.then_inc(s["conv_ready"], 1)
                    yield

            def pair(i):
                steps = iter(()) if isinstance(i, int) and i == 0 else conv(i - 1)
                for j in range(2):
                    w_low(2 * i + 2 + j, j)
                    for _ in range(TAPS // 2):
                        next(steps, None)

            w_low(0, 0)
            w_low(1, 1)
            for i in range(2):
                dve.wait_ge(s["uh_ready"], i + 1)
                part = slice(2 * i, 2 * i + 2)
                dve.tensor_tensor(ul[:, part, :], ps_u[i][:].rearrange("p (c l) -> p c l", c=2), two_part(uh[:, part, :]),
                                  ALU.subtract).then_inc(s["ul_ready"], 1)
            dve.wait_ge(s["wdh_ready"], 1)
            dve.tensor_tensor(wdl[:], ps_d[0][:, 0:MC * NH].rearrange("p (c h) -> p c h", c=MC), two_part(wdh[:]), ALU.subtract).then_inc(s["wdl_ready"], 1)
            dve.wait_ge(s["conv_in"], 32)
            pair(0)
            for t in range(QT):
                dve.wait_ge(s["dt_ps"], t + 1)
                link(dve.tensor_copy(keep.dt[:, t, :], ps_d[t][:, 256:256 + NH]))
            dve.wait_ge(keep.mix_par_in, 80)
            dt2 = keep.dt[:].rearrange("p t h -> p (t h)")
            link(dve.tensor_tensor(keep.dt[:], keep.dt[:], bc(dtb[:], 1, NCH), ALU.add))
            link(dve.tensor_scalar(t2[:], dt2, 0.0, None, ALU.max))
            link(dve.tensor_scalar(t1[:], dt2, -1.0, None, ALU.mult))
            dve.tensor_tensor(t1[:], t1[:], dt2, ALU.max).then_inc(s["v1"], 1)
            pair(1)
            dve.wait_ge(s["l1"], 1)
            link(dve.tensor_tensor(dt2, t2[:], t1[:], ALU.add))
            dve.wait_ge(s["ea"], 1)
            link(dve.tensor_scalar(al[:], al[:], -1.0, None, ALU.mult))
            dve.tensor_tensor(keep.dA[:], keep.dt[:], bc(al[:], 1, NCH), ALU.mult).then_inc(s["dA_set"], 1)
            with dve.Fori(2, NX + 1) as i:
                pair(i)
            with dve.Fori(NX + 1, NX + NZ - 1) as i:
                for j in range(2):
                    w_low(2 * i + 2 + j, j)

        @block.tensor
        def _(pe):
            pe.wait_ge(s["wd_in"], 16)
            for c in range(MC):
                last = pe.transpose(ps_d[0][:, c * NH:(c + 1) * NH], wdt[:, c * P:(c + 1) * P], keep.ident[0:NH, 0:NH])
            last.then_inc(s["wdT_ps"], 1)

            def turn_w(n, j, load):
                pe.wait_ge(w_in[j], 16 * load)
                if not (isinstance(n, int) and n < 2):
                    pe.wait_ge(s["wl_ready"], n - 1)
                for c in range(MC):
                    last = pe.transpose(ps_t[j][:, c * P:(c + 1) * P], w[:, j, c * P:(c + 1) * P], keep.ident[:])
                last.then_inc(s["wT_ps"], 1)

            turn_w(0, 0, 1)
            turn_w(1, 1, 1)
            pe.wait_ge(s["un_ready"], QT)
            for c in range(MC):
                for t in range(QT):
                    last = pe.transpose(ps_u[c // 2][:, (c % 2) * LQ + t * P:(c % 2) * LQ + (t + 1) * P],
                                        un[:, t, c * P:(c + 1) * P], keep.ident[:])
                if c % 2:
                    last.then_inc(s["uT_ps"], 1)
            passes = lambda h, l, a, b: [(x, y, c) for x, y in ((h, a), (l, a), (h, b)) for c in range(MC)]

            def pair(i, more):
                for j in range(2):
                    n = 2 * i + j
                    if (j == 0 or more) and not (isinstance(n, int) and n == 0):
                        turn_w(n + 1, 1 - j, i + 1 + j)
                    pe.wait_ge(s["wl_ready"], n + 1)
                    if not (isinstance(n, int) and n < 2):
                        pe.wait_ge(s["xz_read"], n - 1)
                    every = passes(wh[j], wl[j], uh, ul)
                    for k, (a, b, c) in enumerate(every):
                        last = pe.matmul(ps_x[j][:, 0:LQ], a[:, c, :], b[:, c, :], start=k == 0, stop=k == len(every) - 1)
                    last.then_inc(s["xz_ps"], 1)

            pe.wait_ge(s["ul_ready"], 2)
            pair(0, True)
            pe.wait_ge(s["wdl_ready"], 1)
            for t in range(QT):
                every = passes(uh, ul, wdh, wdl)
                for n, (a, b, c) in enumerate(every):
                    last = pe.matmul(ps_d[t][:, 256:256 + NH], a[:, c, t * P:(t + 1) * P], b[:, c, :], start=n == 0, stop=n == len(every) - 1)
                last.then_inc(s["dt_ps"], 1)
            with pe.Fori(1, NZ + NX - 1) as i:
                pair(i, True)
            pair(NZ + NX - 1, False)


def mixer(nc, io, keep):
    with ExitStack() as ctx:
        p = Pools(nc, ctx)
        woT = p.sb("w_out_T", [P, CT, DM])
        acs = p.sb("a_cumsum", [P, NCH, NH])
        seg = p.sb("decay", [P, NCH, NH, P])
        eA = p.sb("exp_a", [P, NH, P])
        gt = p.sb("b_c", [P, NCH, P])
        xdt = p.sb("x_dt", [P, NCH, DI])
        dst = p.sb("decay_to_end", [P, NH])
        xdd = p.sb("x_dt_decay", [P, DI])
        bt = p.sb("b_tokens", [P, NS])
        st = p.sb("state_T", [P, DI])
        yg = p.sb("y_gated", [P, CT, LQ])
        ysq = p.sb("y_sq", [P, CT, LQ])
        rs = p.sb("y_rstd", [P, QT])
        mhalf = p.sb("minus_half4", [P, QT])
        zero = p.sb("zero", [P, 1])
        ps_r = p.ps("ps_rep", [P, NH, P])
        ps_a = [p.ps(f"ps_ma{i}", [P, DM]) for i in range(4)]
        names = ("acs_ps acs_ready rep_ps seg_sub seg_exp eA_ready cbx gt_ps gt_ready "
                 "wts_ready xt_ps xdt_ready bt_ready dst_sub dst_ready xdd_ready st_ps st_ready cp_early cp_late y_ps yx yz ysq_ready woT_ps woT_ready "
                 "rs_ps rs_var rs_ready out_ps mixc zero_in")
        s = {n: p.sem("x_" + n) for n in names.split()}
        block = ctx.enter_context(nc.Block())

        @block.sync
        def _(sp):
            for j in range(2):
                load_expert(sp, io, keep, j, j)

        @block.gpsimd
        def _(pool):
            pool.memset(zero[:], 0.0).then_inc(s["zero_in"], 1)
            pool.memset(mhalf[:], -0.5).then_inc(s["mixc"], 1)
            pool.wait_ge(s["eA_ready"], 1)
            pool.tensor_tensor(eA[:, NH // 2:], eA[:, NH // 2:], bc(keep.xc[:, CTT * LQ + CH:(CTT + 1) * LQ], 1, NH // 2), ALU.mult).then_inc(s["cp_late"], 1)
            pool.wait_ge(s["mixc"], 1)
            pool.wait_ge(s["rs_var"], 1)
            pool.tensor_tensor(rs[:], rs[:], mhalf[:], ALU.pow).then_inc(s["rs_ready"], 1)

        @block.scalar
        def _(act):
            for c in range(NCH):
                act.wait_ge(s["seg_sub"], c + 1)
                act.activation(seg[:, c], seg[:, c], ACT.Exp).then_inc(s["seg_exp"], 1)
                if c == 0:
                    act.wait_ge(s["dst_sub"], 1)
                    act.activation(dst[:], dst[:], ACT.Exp).then_inc(s["dst_ready"], 1)
                else:
                    act.activation(eA[:], ps_r[:], ACT.Exp).then_inc(s["eA_ready"], 1)
            act.wait_ge(s["st_ps"], 1)
            for i in range(2):
                act.activation(st[:, i * DM:(i + 1) * DM], ps_a[i][:], ACT.Copy).then_inc(s["st_ready"], 1)
            act.wait_ge(s["zero_in"], 1)
            act.wait_ge(keep.mix_par_in, 80)
            for k in range(CT):
                act.wait_ge(s["woT_ps"], k + 1)
                act.activation(woT[:, k, :], ps_r[:].rearrange("p h l -> p (h l)")[:, (k % 4) * DM:(k % 4 + 1) * DM], ACT.Identity,
                               bias=zero[:], scale=keep.nw[:, k:k + 1]).then_inc(s["woT_ready"], 1)
            for k in range(CT):
                act.wait_ge(s["yz"], k + 1)
                act.activation(ysq[:, k, :], yg[:, k, :], ACT.Square).then_inc(s["ysq_ready"], 1)

        @block.vector
        def _(dve):
            link = p.chain(dve, "x_dve_chain")
            dve.wait_ge(keep.mix_par_in, 80)
            dve.wait_ge(s["acs_ps"], 1)
            dve.tensor_copy(acs[:], ps_a[0][:, 0:NCH * NH].rearrange("p (c h) -> p c h", c=NCH)).then_inc(s["acs_ready"], 1)
            dve.wait_ge(s["acs_ready"], 1)
            for c in range(NCH):
                dve.wait_ge(s["gt_ps"], c + 1)
                dve.tensor_tensor(gt[:, c, :], ps_a[1][:, c * P:(c + 1) * P], keep.tri[:], ALU.mult).then_inc(s["gt_ready"], 1)
            for c in range(NCH):
                dve.wait_ge(s["rep_ps"], c + 1)
                link(dve.tensor_tensor(seg[:, c], ps_r[:], bc(acs[:, c, :], 2, P), ALU.subtract))
                dve.tensor_scalar(seg[:, c], seg[:, c], 0.0, None, ALU.min).then_inc(s["seg_sub"], 1)
                if c == 0:
                    dve.tensor_tensor(dst[:], ps_r[:, :, P - 1], acs[:, 0, :], ALU.subtract).then_inc(s["dst_sub"], 1)
                for i in range(2):
                    dve.wait_ge(s["xt_ps"], 2 * c + i + 1)
                    part = slice(i * DM, (i + 1) * DM)
                    dve.tensor_tensor(xdt[:, c, part].rearrange("p (h e) -> p h e", e=HP), ps_a[2 + i][:].rearrange("p (h e) -> p h e", e=HP),
                                      bc(keep.dt[:, c, i * NH // 2:(i + 1) * NH // 2], 2, HP), ALU.mult).then_inc(s["xdt_ready"], 1)
                dve.wait_ge(s["seg_exp"], c + 1)
                dve.wait_ge(s["gt_ready"], c + 1)
                dve.tensor_tensor(seg[:, c], seg[:, c], bc(gt[:, c, :], 1, NH), ALU.mult).then_inc(s["wts_ready"], 1)
                if c == 0:
                    dve.wait_ge(s["cbx"], 1)
                    dve.tensor_copy(bt[:], ps_a[1][:, 2 * P:3 * P]).then_inc(s["bt_ready"], 1)
                    dve.wait_ge(s["dst_ready"], 1)
                    dve.wait_ge(s["xdt_ready"], 2)
                    dve.tensor_tensor(xdd[:].rearrange("p (h e) -> p h e", e=HP), xdt[:, 0, :].rearrange("p (h e) -> p h e", e=HP),
                                      bc(dst[:], 2, HP), ALU.mult).then_inc(s["xdd_ready"], 1)
            dve.wait_ge(s["eA_ready"], 1)
            dve.tensor_tensor(eA[:, 0:NH // 2], eA[:, 0:NH // 2], bc(keep.xc[:, CTT * LQ + CH:(CTT + 1) * LQ], 1, NH // 2), ALU.mult).then_inc(s["cp_early"], 1)

            def skip(k):
                dve.wait_ge(s["y_ps"], k + 1)
                xs = keep.xc[:, k * LQ:(k + 1) * LQ]
                dve.scalar_tensor_tensor(yg[:, k, :], xs, keep.dsk[:, k:k + 1], ps_a[k % 2][:, 0:LQ], ALU.mult, ALU.add).then_inc(s["yx"], 1)

            for k in range(CT):
                skip(k)
                dve.wait_ge(s["yx"], k + 1)
                dve.tensor_tensor(yg[:, k, :], yg[:, k, :], keep.zs[:, k * LQ:(k + 1) * LQ], ALU.mult).then_inc(s["yz"], 1)
            dve.wait_ge(s["rs_ps"], 1)
            dve.tensor_scalar(rs[:], ps_a[0][:, 0:QT], 1.0 / DI, 1e-5, ALU.mult, ALU.add).then_inc(s["rs_var"], 1)
            dve.wait_ge(s["rs_ready"], 1)
            for t in range(QT):
                dve.wait_ge(s["out_ps"], t + 1)
                dve.scalar_tensor_tensor(keep.x1[:, t, :], ps_a[2 + t][:], rs[:, t:t + 1], keep.x1[:, t, :], ALU.mult, ALU.add).then_inc(keep.x2_ready, 1)

        @block.tensor
        def _(pe):
            cols = lambda k, c: slice(k * LQ + c * CH, k * LQ + (c + 1) * CH)
            for c in range(NCH):
                pe.matmul(ps_a[1][:, c * P:(c + 1) * P], keep.xc[:, cols(BT, c)], keep.xc[:, cols(CTT, c)], start=True, stop=True).then_inc(s["gt_ps"], 1)
            for c in range(NCH):
                last = pe.matmul(ps_a[0][:, c * NH:(c + 1) * NH], keep.tri[:], keep.dA[:, c, :], start=True, stop=True)
            last.then_inc(s["acs_ps"], 1)

            def turn_x(c):
                if c:
                    pe.wait_ge(s["xdt_ready"], 2)
                for k in range(CT):
                    last = pe.transpose(ps_a[2 + k // 4][:, (k % 4) * P:(k % 4 + 1) * P], keep.xc[:, cols(k, c)], keep.ident[:])
                    if k % 4 == 3:
                        last.then_inc(s["xt_ps"], 1)

            for c in range(NCH):
                pe.wait_ge(keep.dAU_ready, c + 1)
                if c:
                    pe.wait_ge(s["seg_sub"], 1)
                    pe.wait_ge(s["dst_sub"], 1)
                for i in range(NH // 4):
                    last = pe.matmul(ps_r[:, 4 * i:4 * i + 4, :], keep.ones[:], keep.dAU[:, c, 4 * i:4 * i + 4, :], start=True, stop=True)
                last.then_inc(s["rep_ps"], 1)
                turn_x(c)
                if c == 0:
                    pe.wait_ge(s["gt_ready"], NCH)
                    pe.transpose(ps_a[1][:, 2 * P:3 * P], keep.xc[:, cols(BT, 0)], keep.ident[:]).then_inc(s["cbx"], 1)
            pe.wait_ge(s["bt_ready"], 1)
            pe.wait_ge(s["acs_ready"], 1)
            pe.wait_ge(s["xdd_ready"], 1)
            for i in range(2):
                last = pe.matmul(ps_a[i][:], bt[:], xdd[:, i * DM:(i + 1) * DM], start=True, stop=True)
            last.then_inc(s["st_ps"], 1)
            pe.wait_ge(keep.w_out_in, 16)
            pe.wait_ge(s["eA_ready"], 1)
            pe.wait_ge(s["seg_sub"], NCH)
            for k in range(CT):
                if k >= 4:
                    pe.wait_ge(s["woT_ready"], k - 3)
                for m in range(MC):
                    last = pe.transpose(ps_r[:, (k % 4) * 4 + m, :], keep.wo[:, m, k * P:(k + 1) * P], keep.ident[:])
                last.then_inc(s["woT_ps"], 1)
            pe.wait_ge(s["wts_ready"], NCH)
            pe.wait_ge(s["xdt_ready"], 4)
            pe.wait_ge(s["st_ready"], 2)

            def y(k):
                pe.wait_ge(s["cp_early" if k < CT // 2 else "cp_late"], 1)
                if k >= 2:
                    pe.wait_ge(s["yx"], k - 1)
                for c in range(NCH):
                    for hh in range(2):
                        h = 2 * k + hh
                        dst_ps = ps_a[k % 2][hh * HP:(hh + 1) * HP, c * CH:(c + 1) * CH]
                        hs = slice(h * HP, (h + 1) * HP)
                        last = pe.matmul(dst_ps, xdt[:, c, hs], seg[:, c, h, :], start=True, stop=c == 0)
                        if c:
                            last = pe.matmul(dst_ps, st[:, hs], eA[:, h, :], start=False, stop=True)
                last.then_inc(s["y_ps"], 1)

            pe.wait_ge(s["woT_ready"], CT)
            y(0)
            for k in range(CT):
                if k + 1 < CT:
                    y(k + 1)
                else:
                    pe.wait_ge(s["ysq_ready"], CT)
                    for t in range(QT):
                        for i in range(CT):
                            last = pe.matmul(ps_a[0][:, t:t + 1], ysq[:, i, t * P:(t + 1) * P], keep.ones[:, 0:1], start=i == 0, stop=i == CT - 1)
                    last.then_inc(s["rs_ps"], 1)
                pe.wait_ge(s["yz"], k + 1)
                for t in range(QT):
                    last = pe.matmul(ps_a[2 + t][:], yg[:, k, t * P:(t + 1) * P], woT[:, k, :], start=k == 0, stop=k == CT - 1)
                    if k == CT - 1:
                        last.then_inc(s["out_ps"], 1)


def route(nc, io, keep):
    with ExitStack() as ctx:
        p = Pools(nc, ctx)
        stat = p.sb("h_stat", [P, QT, 6])
        aggr = p.sb("h_aggr", [P, QT, 2])
        hr = p.sb("h_rstd", [P, QT])
        hn = p.sb("h_norm", [P, QT, DM])
        mhalf = p.sb("minus_half5", [P, QT])
        gw = p.sb("gate_rows", [E, DM])
        gwT = p.sb("gate_T", [P, MC, E])
        mu = p.sb("mask_up_rows", [P, MC, FG, GS])
        idx = p.sb("expert_index", [E, E], I32)
        idf = p.sb("expert_index_f", [E, E])
        idn = p.sb("expert_index_wrapped", [E, E])
        row = p.sb("row_number", [E, 1], I32)
        rowf = p.sb("row_number_f", [E, 1])
        pick = p.sb("pick", [E, E])
        sc = p.sb("router_scores", [P, QT, E])
        mxs = p.sb("router_max", [P, QT])
        sm = p.sb("router_sum", [P, QT])
        top = p.sb("router_top", [P, QT, TOPK])
        rest = p.sb("router_rest", [P, QT, E])
        we = p.sb("expert_weights", [P, QT, E])
        weT = p.sb("expert_weights_T", [E, LQ])
        flat = p.sb("grouped_weights", [P, QT * FG, GS])
        soft = p.sb("group_softmax", [P, QT * FG, GS])
        gm = p.sb("group_max", [P, QT * FG])
        gsum = p.sb("group_sum", [P, QT * FG])
        gmask = p.sb("group_rows", [E, FG])
        softT = p.sb("group_softmax_T", [E, LQ])
        ps_h = [p.ps(f"ps_h{i}", [P, DM]) for i in range(2)]
        ps_g = [p.ps(f"ps_gt{i}", [P, DM]) for i in range(4)]
        names = ("gw_in mu_in idx_in pool_c masks row_ready var_h rstd_h hn_ready hT_ps hT_ready gwT_ps gwT_ready lg_ps lgm_ready "
                 "exp_ready we_ready weT_ps weT_ready pick_ready flat_ps fsub_ready fexp_ready soft_ready softT_ps softT_ready muT_ps "
                 "softz_ready zero_ready")
        s = {n: p.sem("r_" + n) for n in names.split()}
        block = ctx.enter_context(nc.Block())

        @block.sync
        def _(sp):
            sp.dma_start(gw[:], io["L0_ffn_gate_w"]).then_inc(s["gw_in"], 16)
            for c in range(MC):
                sp.dma_start(mu[:, c], io["L0_ffn_mask_up_w"][:, c * P:(c + 1) * P, :].rearrange("g p i -> p g i")).then_inc(s["mu_in"], 16)
            sp.dma_start(idx[:], io["L0_ffn_inv_map"].rearrange("a b -> (a b)").partition_broadcast(E)).then_inc(s["idx_in"], 16)

        @block.gpsimd
        def _(pool):
            link = p.chain(pool, "r_pool_chain")
            pool.memset(mhalf[:], -0.5).then_inc(s["pool_c"], 1)
            pool.wait_ge(s["pool_c"], 1)
            pool.wait_ge(s["var_h"], 1)
            pool.tensor_tensor(hr[:], hr[:], mhalf[:], ALU.pow).then_inc(s["rstd_h"], 1)
            link(pool.iota(row[:], pattern=[[0, 1]], base=0, channel_multiplier=1))
            pool.tensor_copy(rowf[:], row[:]).then_inc(s["row_ready"], 1)
            pool.wait_ge(s["row_ready"], 1)
            link(pool.memset(gmask[:], 1.0))
            link(pool.affine_select(out=gmask[:], in_=gmask[:], compare_op=ALU.is_ge, fill=0.0, base=0,
                                    pattern=[[-GS, FG]], channel_multiplier=1))
            pool.affine_select(out=gmask[:], in_=gmask[:], compare_op=ALU.is_ge, fill=0.0, base=GS - 1,
                               pattern=[[GS, FG]], channel_multiplier=-1).then_inc(s["masks"], 1)
            pool.wait_ge(s["masks"], 1)
            link(pool.memset(keep.softz[E:, :], 0.0))
            pool.memset(keep.muT[E:, :], 0.0).then_inc(s["zero_ready"], 1)

        @block.scalar
        def _(act):
            first = high_parts(act, keep, 0, 0)
            act.wait_ge(s["gwT_ps"], 1)
            act.activation(gwT[:], ps_g[0][:, 0:MC * E].rearrange("p (c e) -> p c e", c=MC), ACT.Copy).then_inc(s["gwT_ready"], 1)
            act.wait_ge(s["muT_ps"], 1)
            act.activation(keep.muT[0:E, :], ps_g[3][0:E, :], ACT.Copy).then_inc(keep.muT_ready, 1)
            steps(first, 2)
            for i in range(2):
                act.wait_ge(s["hT_ps"], i + 1)
                act.activation(keep.hT[:, 2 * i:2 * i + 2, :], ps_h[i][:].rearrange("p (c l) -> p c l", c=2), ACT.Copy).then_inc(s["hT_ready"], 1)
            steps(first, 2)
            act.wait_ge(s["lgm_ready"], 1)
            act.activation(sc[:], sc[:], ACT.Exp).then_inc(s["exp_ready"], 1)
            steps(first, 2)
            act.wait_ge(s["weT_ps"], 1)
            act.activation(weT[:], ps_g[0][0:E, 0:LQ], ACT.Copy).then_inc(s["weT_ready"], 1)
            steps(first, 2)
            act.wait_ge(s["fsub_ready"], 1)
            act.activation(soft[:], soft[:], ACT.Exp).then_inc(s["fexp_ready"], 1)
            steps(first, NT)

        @block.vector
        def _(dve):
            link = p.chain(dve, "r_dve_chain")
            first = low_parts(dve, keep, 0, 0)
            dve.wait_ge(keep.x2_ready, QT)
            for t in range(QT):
                link(dve.bn_stats(stat[:, t, :], keep.x1[:, t, :]))
                link(dve.bn_aggr(aggr[:, t, :], stat[:, t, :]))
            dve.tensor_scalar(hr[:], aggr[:, :, 1], 1e-5, None, ALU.add).then_inc(s["var_h"], 1)
            dve.wait_ge(s["rstd_h"], 1)
            for t in range(QT):
                dve.tensor_scalar(hn[:, t, :], keep.x1[:, t, :], aggr[:, t, 0:1], hr[:, t:t + 1], ALU.subtract, ALU.mult).then_inc(s["hn_ready"], 1)
            steps(first, 2)
            dve.wait_ge(s["idx_in"], 16)
            dve.wait_ge(s["row_ready"], 1)
            link(dve.tensor_copy(idf[:], idx[:]))
            link(dve.tensor_scalar(idn[:], idf[:], float(E), rowf[:, 0:1], ALU.add, ALU.is_equal))
            link(dve.tensor_scalar(idf[:], idf[:], rowf[:, 0:1], None, ALU.is_equal))
            dve.tensor_tensor(pick[:], idf[:], idn[:], ALU.add).then_inc(s["pick_ready"], 1)
            steps(first, 2)
            dve.wait_ge(s["lg_ps"], 1)
            lg = ps_g[1][:, 0:QT * E].rearrange("p (t e) -> p t e", t=QT)
            link(dve.tensor_reduce(mxs[:], lg, AX.X, ALU.max))
            dve.tensor_tensor(sc[:], lg, bc(mxs[:], 2, E), ALU.subtract).then_inc(s["lgm_ready"], 1)
            dve.wait_ge(s["exp_ready"], 1)
            link(dve.tensor_reduce(sm[:], sc[:], AX.X, ALU.add))
            link(dve.reciprocal(sm[:], sm[:]))
            link(dve.tensor_tensor(sc[:], sc[:], bc(sm[:], 2, E), ALU.mult))
            for t in range(QT):
                link(dve.max(top[:, t, :], sc[:, t, :]))
                link(dve.match_replace(rest[:, t, :], top[:, t, :], sc[:, t, :], 0.0))
            dve.tensor_tensor(we[:], sc[:], rest[:], ALU.subtract).then_inc(s["we_ready"], 1)
            steps(first, 2)
            dve.wait_ge(s["flat_ps"], 1)
            f3 = ps_g[2][:, 0:QT * E].rearrange("p (g i) -> p g i", i=GS)
            dve.tensor_reduce(keep.scal[:], f3, AX.X, ALU.add).then_inc(keep.scal_ready, 1)
            link(dve.tensor_copy(flat[:], f3))
            link(dve.tensor_scalar(soft[:], flat[:], 0.0, NEG_INF, ALU.is_equal, ALU.mult))
            link(dve.tensor_tensor(soft[:], soft[:], flat[:], ALU.add))
            link(dve.tensor_reduce(gm[:], soft[:], AX.X, ALU.max))
            dve.tensor_tensor(soft[:], soft[:], bc(gm[:], 2, GS), ALU.subtract).then_inc(s["fsub_ready"], 1)
            steps(first, 2)
            dve.wait_ge(s["fexp_ready"], 1)
            link(dve.tensor_reduce(gsum[:], soft[:], AX.X, ALU.add))
            link(dve.reciprocal(gsum[:], gsum[:]))
            dve.tensor_tensor(soft[:], soft[:], bc(gsum[:], 2, GS), ALU.mult).then_inc(s["soft_ready"], 1)
            dve.wait_ge(s["softT_ps"], 1)
            dve.wait_ge(s["masks"], 1)
            dve.tensor_copy(softT[:], ps_g[0][0:E, LQ:]).then_inc(s["softT_ready"], 1)
            dve.wait_ge(s["softT_ready"], 1)
            for g in range(FG):
                dve.tensor_scalar(keep.softz[0:E, g * LQ:(g + 1) * LQ], softT[:], gmask[:, g:g + 1], None, ALU.mult).then_inc(keep.softz_ready, 1)
            steps(first, NT)
            dve.wait_ge(s["zero_ready"], 1)

        @block.tensor
        def _(pe):
            pe.wait_ge(s["gw_in"], 16)
            for c in range(MC):
                last = pe.transpose(ps_g[0][:, c * E:(c + 1) * E], gw[:, c * P:(c + 1) * P], keep.ident[0:E, 0:E])
            last.then_inc(s["gwT_ps"], 1)
            pe.wait_ge(s["mu_in"], 16 * MC)
            for c in range(MC):
                last = pe.transpose(ps_g[3][0:E, c * P:(c + 1) * P], mu[:, c].rearrange("p g i -> p (g i)"), keep.ident[:])
            last.then_inc(s["muT_ps"], 1)
            first = turn_weights(pe, keep, 0, 0, 0)
            steps(first, 2)
            pe.wait_ge(s["hn_ready"], QT)
            for c in range(MC):
                for t in range(QT):
                    last = pe.transpose(ps_h[c // 2][:, (c % 2) * LQ + t * P:(c % 2) * LQ + (t + 1) * P],
                                        hn[:, t, c * P:(c + 1) * P], keep.ident[:])
                if c % 2:
                    last.then_inc(s["hT_ps"], 1)
            steps(first, 2)
            pe.wait_ge(s["hT_ready"], 2)
            pe.wait_ge(s["gwT_ready"], 1)
            for t in range(QT):
                for c in range(MC):
                    last = pe.matmul(ps_g[1][:, t * E:(t + 1) * E], keep.hT[:, c, t * P:(t + 1) * P], gwT[:, c, :], start=c == 0, stop=c == MC - 1)
            last.then_inc(s["lg_ps"], 1)
            steps(first, 2)
            pe.wait_ge(s["we_ready"], 1)
            for t in range(QT):
                last = pe.transpose(ps_g[0][0:E, t * P:(t + 1) * P], we[:, t, :], keep.ident[:])
            last.then_inc(s["weT_ps"], 1)
            pe.wait_ge(s["weT_ready"], 1)
            pe.wait_ge(s["pick_ready"], 1)
            for t in range(QT):
                last = pe.matmul(ps_g[2][:, t * E:(t + 1) * E], weT[:, t * P:(t + 1) * P], pick[:], start=True, stop=True)
            last.then_inc(s["flat_ps"], 1)
            steps(first, 2)
            pe.wait_ge(s["soft_ready"], 1)
            for t in range(QT):
                src = soft[:].rearrange("p (t g) i -> p t (g i)", t=QT)[:, t, :]
                last = pe.transpose(ps_g[0][0:E, LQ + t * P:LQ + (t + 1) * P], src, keep.ident[:])
            last.then_inc(s["softT_ps"], 1)
            steps(first, NT)


INNER = [min(P, FI - i * P) for i in range(FT)]
NT = 2 * MC + FT


def banks(keep, j):
    for hi, lo in ((keep.gh[j], keep.gl[j]), (keep.uh[j], keep.ul[j])):
        for c in range(MC):
            yield P, FI, hi[:, c, :], lo[:, c, :]
    for i in range(FT):
        yield INNER[i], DM, keep.dh[j][0:INNER[i], i, :], keep.dl[j][0:INNER[i], i, :]


def turn_weights(pe, keep, g, j, loads):
    n = 0

    def bank(parts, height):
        nonlocal n
        if not (isinstance(g, int) and g * NT + n < 2):
            pe.wait_ge(keep.wt_lo, g * NT + n - 1)
        for at, src, size in parts:
            last = pe.transpose(keep.ps_t[(j * NT + n) % 2][0:height, at:at + size], src, keep.ident[0:size, 0:size])
        last.then_inc(keep.wt_ps, 1)
        n += 1

    for name, w in (("g", keep.wg[j]), ("u", keep.wu[j])):
        pe.wait_ge(keep.w_in[name, j], 32 * loads + 32)
        for c in range(MC):
            bank([(i * P, w[0:INNER[i], i, c * P:(c + 1) * P], INNER[i]) for i in range(FT)], P)
            yield
    pe.wait_ge(keep.w_in["d", j], 16 * loads + 16)
    for i in range(FT):
        bank([(c * P, keep.wd[j][:, c, i * P:i * P + INNER[i]], P) for c in range(MC)], INNER[i])
        yield


def high_parts(act, keep, g, j):
    for n, (r, w, hi, lo) in enumerate(banks(keep, j)):
        act.wait_ge(keep.wt_ps, g * NT + n + 1)
        act.activation(hi, keep.ps_t[(j * NT + n) % 2][0:r, 0:w], ACT.Copy).then_inc(keep.wt_hi, 1)
        yield


def low_parts(dve, keep, g, j):
    for n, (r, w, hi, lo) in enumerate(banks(keep, j)):
        dve.wait_ge(keep.wt_hi, g * NT + n + 1)
        dve.tensor_tensor(lo, keep.ps_t[(j * NT + n) % 2][0:r, 0:w], two_part(hi), ALU.subtract).then_inc(keep.wt_lo, 1)
        yield


def steps(generator, n):
    for _ in range(n):
        next(generator, None)


def experts(nc, io, keep, out):
    with ExitStack() as ctx:
        p = Pools(nc, ctx)
        gh, gl, uh, ul, dh, dl = keep.gh, keep.gl, keep.uh, keep.ul, keep.dh, keep.dl
        xg = p.sb("x_group", [P, MC, LQ])
        xh = p.sb("x_group_hi", [P, MC, LQ], F32R)
        xl = p.sb("x_group_lo", [P, MC, LQ], F32R)
        sg = p.sb("gate_silu", [P, FT, LQ])
        ac = p.sb("act", [P, FT, LQ])
        ah = p.sb("act_hi", [P, FT, LQ], F32R)
        al = p.sb("act_lo", [P, FT, LQ], F32R)
        ps_x = p.ps("ps_xg", [P, MC, LQ])
        ps_gu = [p.ps(f"ps_gu{i}", [P, 2 * LQ]) for i in range(2)]
        ps_y = [p.ps(f"ps_y{i}", [P, DM]) for i in range(2)]
        names = "xg_ps xg_ready xh_ready xl_ready gu_ps sg_ready ac_ready ah_ready al_ready y_ps y_read done"
        s = {n: p.sem("f_" + n) for n in names.split()}
        s["wt_ps"], s["wt_lo"] = keep.wt_ps, keep.wt_lo
        block = ctx.enter_context(nc.Block())
        rows = INNER

        @block.sync
        def _(sp):
            with sp.Fori(0, FG // 2 - 1) as i:
                for j in range(2):
                    sp.wait_ge(s["wt_ps"], (2 * i + j + 1) * NT)
                    load_expert(sp, io, keep, 2 * i + j + 2, j)
            rows = out.rearrange("o (t p) d -> p (o t) d", p=P)
            for t in range(QT):
                sp.wait_ge(s["y_read"], (FG - 1) * QT + t + 1)
                sp.dma_start(rows[:, t, :], keep.x1[:, t, :]).then_inc(s["done"], 16)
            sp.wait_ge(s["done"], 16 * QT)

        @block.scalar
        def _(act):
            def turn(g, j, more):
                ahead = high_parts(act, keep, g + 1, 1 - j) if more else iter(())
                for n in range(MC):
                    next(ahead, None)
                for i in range(FT):
                    act.wait_ge(s["gu_ps"], g * FT + i + 1)
                    act.activation(sg[0:rows[i], i, :], ps_gu[(j * FT + i) % 2][0:rows[i], 0:LQ], ACT.Silu).then_inc(s["sg_ready"], 1)
                    for n in range(2):
                        next(ahead, None)
                for _ in ahead:
                    pass

            with act.Fori(0, FG // 2 - 1) as i:
                for j in range(2):
                    turn(2 * i + j, j, True)
            turn(FG - 2, 0, True)
            turn(FG - 1, 1, False)

        @block.vector
        def _(dve):
            def inputs(g):
                dve.wait_ge(s["xg_ps"], g + 1)
                dve.tensor_tensor(xg[:], ps_x[:], keep.hT[:], ALU.add).then_inc(s["xg_ready"], 1)
                dve.wait_ge(s["xg_ready"], g + 1)
                dve.tensor_copy(xh[:], xg[:]).then_inc(s["xh_ready"], 1)
                dve.wait_ge(s["xh_ready"], g + 1)
                dve.tensor_tensor(xl[:], xg[:], two_part(xh[:]), ALU.subtract).then_inc(s["xl_ready"], 1)

            def turn(g, j, more):
                ahead = low_parts(dve, keep, g + 1, 1 - j) if more else iter(())
                for n in range(MC):
                    next(ahead, None)
                for i in range(FT):
                    r = rows[i]
                    dve.wait_ge(s["sg_ready"], g * FT + i + 1)
                    dve.tensor_tensor(ac[0:r, i, :], sg[0:r, i, :], ps_gu[(j * FT + i) % 2][0:r, LQ:], ALU.mult).then_inc(s["ac_ready"], 1)
                    dve.wait_ge(s["ac_ready"], g * FT + i + 1)
                    dve.tensor_copy(ah[0:r, i, :], ac[0:r, i, :]).then_inc(s["ah_ready"], 1)
                    dve.wait_ge(s["ah_ready"], g * FT + i + 1)
                    dve.tensor_tensor(al[0:r, i, :], ac[0:r, i, :], two_part(ah[0:r, i, :]), ALU.subtract).then_inc(s["al_ready"], 1)
                    for n in range(2):
                        next(ahead, None)
                for _ in ahead:
                    pass
                if more:
                    inputs(g + 1)
                for t in range(QT):
                    dve.wait_ge(s["y_ps"], g * QT + t + 1)
                    weight = keep.scal[:, bass.ds(g + t * FG, 1)]
                    dve.scalar_tensor_tensor(keep.x1[:, t, :], ps_y[t][:], weight, keep.x1[:, t, :], ALU.mult, ALU.add).then_inc(s["y_read"], 1)

            dve.wait_ge(keep.scal_ready, 1)
            inputs(0)
            with dve.Fori(0, FG // 2 - 1) as i:
                for j in range(2):
                    turn(2 * i + j, j, True)
            turn(FG - 2, 0, True)
            turn(FG - 1, 1, False)

        @block.tensor
        def _(pe):
            def inputs(g):
                pe.wait_ge(keep.softz_ready, FG)
                if not (isinstance(g, int) and g == 0):
                    pe.wait_ge(s["xg_ready"], g)
                for c in range(MC):
                    last = pe.matmul(ps_x[:, c, :], keep.muT[:, c * P:(c + 1) * P], keep.softz[:, bass.ts(g, LQ)], start=True, stop=True)
                last.then_inc(s["xg_ps"], 1)

            def turn(g, j, i2, more):
                ahead = turn_weights(pe, keep, g + 1, 1 - j, i2 + j) if more else iter(())
                for n in range(2):
                    next(ahead, None)
                pe.wait_ge(s["xl_ready"], g + 1)
                pe.wait_ge(s["wt_lo"], g * NT + NT)
                for i in range(FT):
                    if not (isinstance(g, int) and g * FT + i < 2):
                        pe.wait_ge(s["ac_ready"], g * FT + i - 1)
                    at = slice(i * P, i * P + rows[i])
                    for half, (hi, lo) in enumerate(((gh[j], gl[j]), (uh[j], ul[j]))):
                        every = [(a, b, c) for a, b in ((hi, xh), (lo, xh), (hi, xl)) for c in range(MC)]
                        for n, (a, b, c) in enumerate(every):
                            last = pe.matmul(ps_gu[(j * FT + i) % 2][0:rows[i], half * LQ:(half + 1) * LQ], a[:, c, at], b[:, c, :],
                                             start=n == 0, stop=n == len(every) - 1)
                    last.then_inc(s["gu_ps"], 1)
                    for n in range(2):
                        next(ahead, None)
                if more:
                    inputs(g + 1)
                for _ in ahead:
                    pass
                for t in range(QT):
                    if not (isinstance(g, int) and g == 0):
                        pe.wait_ge(s["y_read"], (g - 1) * QT + t + 1)
                    every = [(a, b, i) for i in range(FT) for a, b in ((ah, dh[j]), (al, dh[j]), (ah, dl[j]))]
                    for n, (a, b, i) in enumerate(every):
                        if t == 0 and n % 3 == 0:
                            pe.wait_ge(s["al_ready"], g * FT + i + 1)
                        last = pe.matmul(ps_y[t][:], a[0:rows[i], i, t * P:(t + 1) * P], b[0:rows[i], i, :], start=n == 0, stop=n == len(every) - 1)
                    last.then_inc(s["y_ps"], 1)

            pe.wait_ge(keep.muT_ready, 1)
            inputs(0)
            turn(0, 0, 0, True)
            turn(1, 1, 0, True)
            with pe.Fori(1, FG // 2 - 1) as i:
                for j in range(2):
                    turn(2 * i + j, j, i, True)
            turn(FG - 2, 0, FG // 2 - 1, True)
            turn(FG - 1, 1, FG // 2 - 1, False)
            pe.wait_ge(s["y_read"], FG * QT)


class Keep:
    pass


def declare_experts(f, keep):
    two = lambda name, shape: [f.sb(f"{name}{i}", shape, F32R) for i in range(2)]
    keep.gh, keep.gl = two("gate_T_hi", [P, MC, FI]), two("gate_T_lo", [P, MC, FI])
    keep.uh, keep.ul = two("up_T_hi", [P, MC, FI]), two("up_T_lo", [P, MC, FI])
    keep.dh, keep.dl = two("down_T_hi", [P, FT, DM]), two("down_T_lo", [P, FT, DM])
    keep.ps_t = [f.ps(f"ps_wt_{i}", [P, DM]) for i in range(2)]
    keep.wt_ps, keep.wt_hi, keep.wt_lo = f.sem("f_wt_ps"), f.sem("f_wt_hi"), f.sem("f_wt_lo")
    keep.hT = f.sb("h_T", [P, MC, LQ])
    keep.muT = f.sb("mask_up_T", [P, DM])
    keep.softz = f.sb("group_softmax_rows", [P, FG * LQ])
    keep.scal = f.sb("group_weight", [P, QT * FG])
    keep.muT_ready, keep.scal_ready, keep.softz_ready = f.sem("muT_ready"), f.sem("scal_ready"), f.sem("softz_ready")


def build_program(nc, io, out):
    with ExitStack() as ctx:
        p = Pools(nc, ctx)
        keep = Keep()
        keep.ident = p.sb("ident", [P, P])
        keep.x1 = p.sb("x1", [P, QT, DM])
        keep.x1_ready, keep.kn_in, keep.dca_done = p.sem("x1_ready"), p.sem("kn_in"), p.sem("dca_done")
        keep.x2_ready = p.sem("x2_ready")
        q_scr = nc.dram_tensor("q_scratch", [3 * HD, H, LQ], F32).ap()
        w_scr = nc.dram_tensor("w_scratch", [P, 2, KC, 2 * DM], F32).ap()
        b_scr = nc.dram_tensor("b_scratch", [P, 2 * DM], F32).ap()
        d_scr = nc.dram_tensor("dca_scratch", [P, NG * LQ], F32).ap()
        with ExitStack() as actx:
            a = Pools(nc, actx)
            keep.eps = a.sb("eps", [P, 1])
            keep.d_out, keep.dca_in, keep.wo_in, keep.xb_in = (a.sem(n) for n in ("d_out", "dca_in", "wo_in", "xb_in"))
            keep.fold = a.sb("fold", [P, HD])
            keep.knw = a.sb("kn_w", [P, 1])
            keep.knb = a.sb("kn_b", [P, 1])
            keep.ctxT = a.sb("attn_T", [P, NG * LQ])
            with ExitStack() as cctx:
                c = Pools(nc, cctx)
                keep.cTh = c.sb("ctx_T_hi", [P, KC, LK], F32R)
                keep.cTl = c.sb("ctx_T_lo", [P, KC, LK], F32R)
                keep.vnew = c.sb("v_new", [P, LK // P, P])
                keep.wg = c.sb("w_group", [P, 2, KC, G * 2 * HD], F32R)
                keep.bg = c.sb("b_group", [P, G * 2 * HD])
                keep.qg = c.sb("q_group", [3 * HD + 2, G, LQ], F32R)
                keep.wg_in, keep.q_in = c.sem("wg_in"), [c.sem(f"q_in{h}") for h in range(G)]
                prepare_attention(nc, io, keep, q_scr, w_scr, b_scr, d_scr)
                attend(nc, io, keep, q_scr, w_scr, b_scr, d_scr)

                project_attention(nc, io, keep)
        with ExitStack() as fctx:
            f = Pools(nc, fctx)
            two = lambda name, shape: [f.sb(f"{name}{i}", shape) for i in range(2)]
            keep.wg, keep.wu, keep.wd = two("gate_rows_", [P, FT, DM]), two("up_rows_", [P, FT, DM]), two("down_rows_", [P, MC, FI])
            keep.w_in = {(n, j): f.sem(f"{n}_in{j}") for n in "gud" for j in range(2)}
            with ExitStack() as mctx:
                m = Pools(nc, mctx)
                keep.zs = m.sb("z_gate", [P, CT * LQ])
                keep.xc = m.sb("x_conv", [P, XT * LQ])
                keep.dt = m.sb("dt", [P, QT, NH])
                keep.wo = m.sb("w_out_rows", [P, MC, DI])
                keep.dsk = m.sb("d_skip", [P, CT])
                keep.nw = m.sb("norm_w", [P, CT])
                keep.ones = m.sb("ones", [P, P])
                keep.tri = m.sb("tri", [P, P])
                keep.dA = m.sb("dA", [P, NCH, NH])
                keep.dAU = m.sb("dA_tri", [P, NCH, NH, P])
                keep.mix_par_in, keep.w_out_in, keep.dAU_ready = m.sem("mix_par_in"), m.sem("w_out_in"), m.sem("dAU_ready")
                mixer_projections(nc, io, keep)
                mixer(nc, io, keep)
            declare_experts(f, keep)
            route(nc, io, keep)
            experts(nc, io, keep, out)


_INS = ["x", "ctx_1024"] + ["L0_xattn_" + n for n in (
    "Wq bq Wk bk Wv bv Wkv_dca bkv_dca qn_w qn_b kn_w kn_b kn_dca_w kn_dca_b Wo bo").split()] + ["L0_attn_" + n for n in (
    "W_in conv_w conv_b dt_bias A_log D norm_weight W_out").split()] + ["L0_ffn_" + n for n in (
    "gate_w mask_up_w gate_proj_w up_proj_w down_proj_w inv_map").split()]


def kernel(**inputs):
    import numpy as np
    from concourse import bacc
    from concourse.bass_utils import run_bass_kernel_spmd

    nc = bacc.Bacc("TRN2", target_bir_lowering=False, num_devices=1)
    arrays = {n: np.ascontiguousarray(inputs[n]) for n in _INS}
    io = {n: nc.dram_tensor(n, a.shape, mybir.dt.from_np(a.dtype), kind="ExternalInput").ap() for n, a in arrays.items()}
    out = nc.dram_tensor("out", (1, LQ, DM), F32, kind="ExternalOutput").ap()
    build_program(nc, io, out)
    r = run_bass_kernel_spmd(nc, [arrays], core_ids=[0])
    return r.results[0]["out"]
```
